# Optimizing a Trainium2 kernel written in Bass

```python
import numpy as np
import jax
import jax.numpy as jnp

def _softmax(x, axis=-1):
    return jax.nn.softmax(x, axis=axis)

def _gelu(x):
    return jax.nn.gelu(x, approximate=True)

def _silu(x):
    return jax.nn.silu(x)

def _sigmoid(x):
    return jax.nn.sigmoid(x)

def _layernorm(x, axis=-1, eps=1e-05):
    m = jnp.mean(x, axis=axis, keepdims=True)
    v = jnp.var(x, axis=axis, keepdims=True)
    return (x - m) / jnp.sqrt(v + eps)

def _scatter_add(tgt, idx, src, axis=0):
    return tgt.at[idx].add(src)

def _segment_sum(src, seg, n):
    return jax.ops.segment_sum(src, seg, n)
kernel_name = 'mk_xattn_ffn_d4_seqx_r8_53340a'

def setup_inputs(seed: int=0):
    np.random.seed(seed)
    _w = jnp.asarray

    def _rec_inputs():
        import jax
        import jax.numpy as jnp
        _rk = jax.random.key(seed)
        x = -9.806e-05 + 1 * jax.random.normal(jax.random.fold_in(_rk, 1), (16, 64, 128), jnp.float32)
        _lenS = 64 - jax.random.randint(jax.random.fold_in(_rk, 7), (16,), 0, max(1, 64 // 4) + 1, jnp.int32)
        _lenS2 = 64 - jax.random.randint(jax.random.fold_in(_rk, 8), (16,), 0, max(1, 64 // 4) + 1, jnp.int32)
        _ctx_1024P = jax.random.normal(jax.random.fold_in(_rk, 11), (16, 16, 128), jnp.float32)
        _ctx_1024c = jax.random.dirichlet(jax.random.fold_in(_rk, 511), 0.3 * jnp.ones((16,), jnp.float32), (16, 64))
        _ctx_1024t = jnp.einsum('bsk,bkd->bsd', _ctx_1024c, _ctx_1024P)
        _ctx_1024t = _ctx_1024t * jax.lax.rsqrt(jnp.mean(jnp.square(_ctx_1024t)) + 1e-12) * 0.953939
        ctx_1024 = -1.52775e-05 + 0.999936 * (_ctx_1024t + 0.3 * jax.random.normal(jax.random.fold_in(_rk, 611), (16, 64, 128), jnp.float32))
        _validS = jnp.arange(64)[None, :] < _lenS[:, None]
        _validS2 = jnp.arange(64)[None, :] < _lenS2[:, None]
        _causal = jnp.tril(jnp.ones((64, 64), dtype=bool))
        mask_BxSxS2_ik0 = jnp.where(jnp.broadcast_to(_validS2[:, None, :], (16, 64, 64)), 0, 1).astype(jnp.int32)
        return (x, ctx_1024, _lenS2, mask_BxSxS2_ik0)
    x, ctx_1024, _lenS2, mask_BxSxS2_ik0 = _rec_inputs()

    def _L0_xattn_setup():
        import jax, jax.numpy as jnp
        import numpy as np
        D_MODEL = 128
        N_HEADS = 16
        HEAD_DIM = D_MODEL // N_HEADS
        key = jax.random.key(seed)
        ks = jax.random.split(key, 10)
        B, NQ, S = (8, 64, 512)
        inv = 1.0 / np.sqrt(D_MODEL)
        inp = {'queries': jax.random.normal(ks[0], (B, NQ, D_MODEL), dtype=jnp.float32), 'context': jax.random.normal(ks[1], (B, S, D_MODEL), dtype=jnp.float32), 'wq': jax.random.normal(ks[2], (D_MODEL, D_MODEL), dtype=jnp.float32) * inv, 'bq': jnp.zeros((D_MODEL,), dtype=jnp.float32), 'wk': jax.random.normal(ks[3], (D_MODEL, D_MODEL), dtype=jnp.float32) * inv, 'bk': jnp.zeros((D_MODEL,), dtype=jnp.float32), 'wv': jax.random.normal(ks[4], (D_MODEL, D_MODEL), dtype=jnp.float32) * inv, 'bv': jnp.zeros((D_MODEL,), dtype=jnp.float32), 'wo': jax.random.normal(ks[5], (D_MODEL, D_MODEL), dtype=jnp.float32) * inv, 'bo': jnp.zeros((D_MODEL,), dtype=jnp.float32)}
        return inp
    _L0_xattn_all = _L0_xattn_setup()
    _L0_xattn_in = {k: v for k, v in _L0_xattn_all.items() if k in ('wq', 'bq', 'wk', 'bk', 'wv', 'bv', 'wo', 'bo')}
    del _L0_xattn_all

    def _L0_ffn_setup():
        import jax, jax.numpy as jnp
        import numpy as np
        L, E, H, F, K = (4, 4, 128, 512, 2)
        B, S = (4, 256)
        EPS = 1e-05

        def _moe_layer(x, rw, rb, g, b, w1, b1, w2, b2):
            logits = jnp.einsum('bsh,he->bse', x, rw) + rb
            probs = jax.nn.softmax(logits, axis=-1)
            vals, idx = jax.lax.top_k(probs, K)
            vals = vals / vals.sum(axis=-1, keepdims=True)
            mu = x.mean(axis=-1, keepdims=True)
            xc = x - mu
            xhat = xc * jax.lax.rsqrt((xc * xc).mean(axis=-1, keepdims=True) + EPS)
            xe = xhat[None] * g[:, None, None, :] + b[:, None, None, :]
            h = jax.nn.gelu(jnp.einsum('ebsh,ehf->ebsf', xe, w1) + b1[:, None, None, :], approximate=False)
            y = jnp.einsum('ebsf,efh->ebsh', h, w2) + b2[:, None, None, :]
            expert_out = x[None] + y
            comb = jnp.einsum('bsk,bske->bse', vals, jax.nn.one_hot(idx, E, dtype=x.dtype))
            return jnp.einsum('bse,ebsh->bsh', comb, expert_out)
        key = jax.random.key(seed)
        ks = jax.random.split(key, 4)
        return {'hidden_states': jax.random.normal(ks[0], (B, S, H), jnp.float32), 'router_w': 0.02 * jax.random.normal(ks[1], (L, H, E), jnp.float32), 'router_b': jnp.zeros((L, E), jnp.float32), 'ln_g': jnp.ones((L, E, H), jnp.float32), 'ln_b': jnp.zeros((L, E, H), jnp.float32), 'w1': 0.02 * jax.random.normal(ks[2], (L, E, H, F), jnp.float32), 'b1': jnp.zeros((L, E, F), jnp.float32), 'w2': 0.02 * jax.random.normal(ks[3], (L, E, F, H), jnp.float32), 'b2': jnp.zeros((L, E, H), jnp.float32)}
    _L0_ffn_all = _L0_ffn_setup()
    _L0_ffn_in = {k: v for k, v in _L0_ffn_all.items() if k in ('router_w', 'router_b', 'ln_g', 'ln_b', 'w1', 'b1', 'w2', 'b2')}
    del _L0_ffn_all

    def _L1_xattn_setup():
        import jax, jax.numpy as jnp
        import numpy as np
        import math
        B, S, D, H = (2, 256, 128, 16)
        DK = D // H

        def _split_heads(x):
            b, s, _ = x.shape
            return x.reshape(b, s, H, DK).transpose(0, 2, 1, 3)
        key = jax.random.key(seed)
        ks = jax.random.split(key, 12)
        s = 1.0 / math.sqrt(D)
        inp = {'query': jax.random.normal(ks[0], (B, S, D), jnp.float32), 'key': jax.random.normal(ks[1], (B, S, D), jnp.float32), 'value': jax.random.normal(ks[2], (B, S, D), jnp.float32), 'mask': jnp.tril(jnp.ones((S, S), jnp.int32))[None].repeat(B, axis=0), 'Wq': jax.random.normal(ks[3], (D, D), jnp.float32) * s, 'bq': jnp.zeros((D,), jnp.float32), 'Wk': jax.random.normal(ks[4], (D, D), jnp.float32) * s, 'bk': jnp.zeros((D,), jnp.float32), 'Wv': jax.random.normal(ks[5], (D, D), jnp.float32) * s, 'bv': jnp.zeros((D,), jnp.float32), 'Wo': jax.random.normal(ks[6], (D, D), jnp.float32) * s, 'bo': jnp.zeros((D,), jnp.float32)}
        return inp
    _L1_xattn_all = _L1_xattn_setup()
    _L1_xattn_in = {k: v for k, v in _L1_xattn_all.items() if k in ('Wq', 'bq', 'Wk', 'bk', 'Wv', 'bv', 'Wo', 'bo')}
    del _L1_xattn_all

    def _L1_ffn_setup():
        import jax, jax.numpy as jnp
        import numpy as np
        D_MODEL = 128
        FF = 512
        E = 8
        TOP_K = 2
        CAP_FACTOR = 1.25
        B, T = (4, 256)

        def _moe_forward(x, gate_w, gate_b, w1, b1, w2, b2):
            Bb, Tt, d = x.shape
            S = Bb * Tt
            C = int(CAP_FACTOR * S / E)
            xf = x.reshape(S, d)
            logits = xf @ gate_w + gate_b
            probs = jax.nn.softmax(logits, axis=1)
            topk_p, topk_i = jax.lax.top_k(probs, TOP_K)
            topk_pn = topk_p / jnp.sum(topk_p, axis=1, keepdims=True)
            rows = jnp.arange(S)
            w_te = jnp.zeros((S, E), xf.dtype).at[rows[:, None], topk_i].set(topk_pn)
            mask = jnp.zeros((S, E), bool).at[rows[:, None], topk_i].set(True)
            rank = jnp.cumsum(mask.astype(jnp.int32), axis=0)
            slot = jnp.where(mask & (rank <= C), rank - 1, C)
            e_grid = jnp.broadcast_to(jnp.arange(E), (S, E))
            t_grid = jnp.broadcast_to(rows[:, None], (S, E))
            buf = jnp.full((E, C + 1), S, jnp.int32).at[e_grid, slot].set(t_grid)
            idx = buf[:, :C]
            valid = idx < S
            x_pad = jnp.concatenate([xf, jnp.zeros((1, d), xf.dtype)], axis=0)
            xin = x_pad[idx]
            h = jax.nn.relu(jnp.einsum('ecd,edh->ech', xin, w1) + b1[:, None, :])
            out = jnp.einsum('ech,ehd->ecd', h, w2) + b2[:, None, :]
            w_pad = jnp.concatenate([w_te, jnp.zeros((1, E), xf.dtype)], axis=0)
            tok_w = w_pad[idx, jnp.arange(E)[:, None]]
            out = out * jnp.where(valid, tok_w, 0.0)[:, :, None]
            final = jnp.zeros((S + 1, d), xf.dtype).at[idx.reshape(-1)].add(out.reshape(-1, d))[:S]
            return final.reshape(Bb, Tt, d)
        key = jax.random.key(seed)
        ks = jax.random.split(key, 7)
        s = 0.02
        return {'x': jax.random.normal(ks[0], (B, T, D_MODEL), jnp.float32), 'gate_w': jax.random.normal(ks[1], (D_MODEL, E), jnp.float32) * s, 'gate_b': jnp.zeros((E,), jnp.float32), 'w1': jax.random.normal(ks[2], (E, D_MODEL, FF), jnp.float32) * s, 'b1': jnp.zeros((E, FF), jnp.float32), 'w2': jax.random.normal(ks[3], (E, FF, D_MODEL), jnp.float32) * s, 'b2': jnp.zeros((E, D_MODEL), jnp.float32)}
    _L1_ffn_all = _L1_ffn_setup()
    _L1_ffn_in = {k: v for k, v in _L1_ffn_all.items() if k in ('gate_w', 'gate_b', 'w1', 'b1', 'w2', 'b2')}
    del _L1_ffn_all

    def _L2_xattn_setup():
        import jax, jax.numpy as jnp
        import numpy as np
        B, SQ, SKV, E, H = (4, 256, 256, 128, 16)
        D = E // H
        key = jax.random.key(seed)
        ks = jax.random.split(key, 8)
        s = 1.0 / np.sqrt(D)
        return {'query': jax.random.normal(ks[0], (B, SQ, E), jnp.float32), 'key_value': jax.random.normal(ks[1], (B, SKV, E), jnp.float32), 'wq': jax.random.normal(ks[2], (H, D, D), jnp.float32) * s, 'bq': jnp.zeros((H, D), jnp.float32), 'wk': jax.random.normal(ks[3], (H, D, D), jnp.float32) * s, 'bk': jnp.zeros((H, D), jnp.float32), 'wv': jax.random.normal(ks[4], (H, D, D), jnp.float32) * s, 'bv': jnp.zeros((H, D), jnp.float32), 'wo': jax.random.normal(ks[5], (E, E), jnp.float32) * (1.0 / np.sqrt(E)), 'bo': jnp.zeros((E,), jnp.float32)}
    _L2_xattn_all = _L2_xattn_setup()
    _L2_xattn_in = {k: v for k, v in _L2_xattn_all.items() if k in ('wq', 'bq', 'wk', 'bk', 'wv', 'bv', 'wo', 'bo')}
    del _L2_xattn_all

    def _L2_ffn_setup():
        import jax, jax.numpy as jnp
        import numpy as np
        TOP_K = 2

        def _moe(x, Wr, br, W1, b1, W2, b2):
            B, S, D = x.shape
            E = Wr.shape[1]
            xt = x.reshape(-1, D)
            logits = xt @ Wr + br
            top_vals, top_idx = jax.lax.top_k(logits, TOP_K)
            mask = jnp.zeros_like(logits, dtype=bool).at[jnp.arange(xt.shape[0])[:, None], top_idx].set(True)
            sparse_logits = jnp.where(mask, logits, -jnp.inf)
            gate = jax.nn.softmax(sparse_logits, axis=-1)
            h = jax.nn.relu(jnp.einsum('td,edh->teh', xt, W1) + b1)
            y = jnp.einsum('teh,ehd->ted', h, W2) + b2
            out = jnp.einsum('ted,te->td', y, gate)
            return out.reshape(B, S, D)
        key = jax.random.key(seed)
        ks = jax.random.split(key, 5)
        B, S, D, E, H = (2, 256, 128, 8, 512)
        scale = 1.0 / np.sqrt(D)
        return {'x': jax.random.normal(ks[0], (B, S, D), dtype=jnp.float32), 'Wr': jax.random.normal(ks[1], (D, E), dtype=jnp.float32) * scale, 'br': jnp.zeros((E,), dtype=jnp.float32), 'W1': jax.random.normal(ks[2], (E, D, H), dtype=jnp.float32) * scale, 'b1': jnp.zeros((E, H), dtype=jnp.float32), 'W2': jax.random.normal(ks[3], (E, H, D), dtype=jnp.float32) * (1.0 / np.sqrt(H)), 'b2': jnp.zeros((E, D), dtype=jnp.float32)}
    _L2_ffn_all = _L2_ffn_setup()
    _L2_ffn_in = {k: v for k, v in _L2_ffn_all.items() if k in ('Wr', 'br', 'W1', 'b1', 'W2', 'b2')}
    del _L2_ffn_all

    def _L3_xattn_setup():
        import jax, jax.numpy as jnp
        import numpy as np
        N_HEADS = 16
        key = jax.random.key(seed)
        ks = jax.random.split(key, 9)
        B, T, C, S = (32, 8, 128, 512)
        w_scale = 1.0 / np.sqrt(C).astype(np.float32)
        return {'x': jax.random.normal(ks[0], (B, T, C), jnp.float32), 'cache_k': jax.random.normal(ks[1], (B, S, C), jnp.float32), 'cache_v': jax.random.normal(ks[2], (B, S, C), jnp.float32), 'cache_len': jax.random.randint(ks[3], (B,), 0, S - T, jnp.int32), 'wq': jax.random.normal(ks[4], (C, C), jnp.float32) * w_scale, 'wk': jax.random.normal(ks[5], (C, C), jnp.float32) * w_scale, 'wv': jax.random.normal(ks[6], (C, C), jnp.float32) * w_scale, 'wo': jax.random.normal(ks[7], (C, C), jnp.float32) * w_scale, 'bo': jnp.zeros((C,), jnp.float32)}
    _L3_xattn_all = _L3_xattn_setup()
    _L3_xattn_in = {k: v for k, v in _L3_xattn_all.items() if k in ('wq', 'wk', 'wv', 'wo', 'bo')}
    del _L3_xattn_all

    def _L3_ffn_setup():
        import jax, jax.numpy as jnp
        import numpy as np
        D_MODEL = 128
        N_HEADS = 16
        N_EXPERTS = 8
        TOP_K = 2
        EXPERT_HIDDEN = D_MODEL * 4 // N_EXPERTS

        def layer_norm(x, g, b, eps=1e-05):
            mu = jnp.mean(x, axis=-1, keepdims=True)
            var = jnp.var(x, axis=-1, keepdims=True)
            return (x - mu) * jax.lax.rsqrt(var + eps) * g + b
        key = jax.random.key(seed)
        ks = jax.random.split(key, 12)
        s = 1.0 / np.sqrt(D_MODEL)
        return {'x': jax.random.normal(ks[0], (2, 256, D_MODEL), dtype=jnp.float32), 'Wq': jax.random.normal(ks[1], (D_MODEL, D_MODEL), dtype=jnp.float32) * s, 'Wk': jax.random.normal(ks[2], (D_MODEL, D_MODEL), dtype=jnp.float32) * s, 'Wv': jax.random.normal(ks[3], (D_MODEL, D_MODEL), dtype=jnp.float32) * s, 'Wo': jax.random.normal(ks[4], (D_MODEL, D_MODEL), dtype=jnp.float32) * s, 'g1': jnp.ones((D_MODEL,), jnp.float32), 'b1': jnp.zeros((D_MODEL,), jnp.float32), 'g2': jnp.ones((D_MODEL,), jnp.float32), 'b2': jnp.zeros((D_MODEL,), jnp.float32), 'Wg': jax.random.normal(ks[5], (D_MODEL, N_EXPERTS), dtype=jnp.float32) * s, 'W1': jax.random.normal(ks[6], (N_EXPERTS, D_MODEL, EXPERT_HIDDEN), dtype=jnp.float32) * s, 'W2': jax.random.normal(ks[7], (N_EXPERTS, EXPERT_HIDDEN, D_MODEL), dtype=jnp.float32) * (1.0 / np.sqrt(EXPERT_HIDDEN))}
    _L3_ffn_all = _L3_ffn_setup()
    _L3_ffn_in = {k: v for k, v in _L3_ffn_all.items() if k in ('Wq', 'Wk', 'Wv', 'Wo', 'g1', 'b1', 'g2', 'b2', 'Wg', 'W1', 'W2')}
    del _L3_ffn_all
    return {'x': x, 'ctx_1024': ctx_1024, '_lenS2': _lenS2, 'mask_BxSxS2_ik0': mask_BxSxS2_ik0, 'L0_xattn_wq': _L0_xattn_in['wq'], 'L0_xattn_bq': _L0_xattn_in['bq'], 'L0_xattn_wk': _L0_xattn_in['wk'], 'L0_xattn_bk': _L0_xattn_in['bk'], 'L0_xattn_wv': _L0_xattn_in['wv'], 'L0_xattn_bv': _L0_xattn_in['bv'], 'L0_xattn_wo': _L0_xattn_in['wo'], 'L0_xattn_bo': _L0_xattn_in['bo'], 'L0_ffn_router_w': _L0_ffn_in['router_w'], 'L0_ffn_router_b': _L0_ffn_in['router_b'], 'L0_ffn_ln_g': _L0_ffn_in['ln_g'], 'L0_ffn_ln_b': _L0_ffn_in['ln_b'], 'L0_ffn_w1': _L0_ffn_in['w1'], 'L0_ffn_b1': _L0_ffn_in['b1'], 'L0_ffn_w2': _L0_ffn_in['w2'], 'L0_ffn_b2': _L0_ffn_in['b2'], 'L1_xattn_Wq': _L1_xattn_in['Wq'], 'L1_xattn_bq': _L1_xattn_in['bq'], 'L1_xattn_Wk': _L1_xattn_in['Wk'], 'L1_xattn_bk': _L1_xattn_in['bk'], 'L1_xattn_Wv': _L1_xattn_in['Wv'], 'L1_xattn_bv': _L1_xattn_in['bv'], 'L1_xattn_Wo': _L1_xattn_in['Wo'], 'L1_xattn_bo': _L1_xattn_in['bo'], 'L1_ffn_gate_w': _L1_ffn_in['gate_w'], 'L1_ffn_gate_b': _L1_ffn_in['gate_b'], 'L1_ffn_w1': _L1_ffn_in['w1'], 'L1_ffn_b1': _L1_ffn_in['b1'], 'L1_ffn_w2': _L1_ffn_in['w2'], 'L1_ffn_b2': _L1_ffn_in['b2'], 'L2_xattn_wq': _L2_xattn_in['wq'], 'L2_xattn_bq': _L2_xattn_in['bq'], 'L2_xattn_wk': _L2_xattn_in['wk'], 'L2_xattn_bk': _L2_xattn_in['bk'], 'L2_xattn_wv': _L2_xattn_in['wv'], 'L2_xattn_bv': _L2_xattn_in['bv'], 'L2_xattn_wo': _L2_xattn_in['wo'], 'L2_xattn_bo': _L2_xattn_in['bo'], 'L2_ffn_Wr': _L2_ffn_in['Wr'], 'L2_ffn_br': _L2_ffn_in['br'], 'L2_ffn_W1': _L2_ffn_in['W1'], 'L2_ffn_b1': _L2_ffn_in['b1'], 'L2_ffn_W2': _L2_ffn_in['W2'], 'L2_ffn_b2': _L2_ffn_in['b2'], 'L3_xattn_wq': _L3_xattn_in['wq'], 'L3_xattn_wk': _L3_xattn_in['wk'], 'L3_xattn_wv': _L3_xattn_in['wv'], 'L3_xattn_wo': _L3_xattn_in['wo'], 'L3_xattn_bo': _L3_xattn_in['bo'], 'L3_ffn_Wq': _L3_ffn_in['Wq'], 'L3_ffn_Wk': _L3_ffn_in['Wk'], 'L3_ffn_Wv': _L3_ffn_in['Wv'], 'L3_ffn_Wo': _L3_ffn_in['Wo'], 'L3_ffn_g1': _L3_ffn_in['g1'], 'L3_ffn_b1': _L3_ffn_in['b1'], 'L3_ffn_g2': _L3_ffn_in['g2'], 'L3_ffn_b2': _L3_ffn_in['b2'], 'L3_ffn_Wg': _L3_ffn_in['Wg'], 'L3_ffn_W1': _L3_ffn_in['W1'], 'L3_ffn_W2': _L3_ffn_in['W2']}

def reference(x, ctx_1024, _lenS2, mask_BxSxS2_ik0, L0_xattn_wq, L0_xattn_bq, L0_xattn_wk, L0_xattn_bk, L0_xattn_wv, L0_xattn_bv, L0_xattn_wo, L0_xattn_bo, L0_ffn_router_w, L0_ffn_router_b, L0_ffn_ln_g, L0_ffn_ln_b, L0_ffn_w1, L0_ffn_b1, L0_ffn_w2, L0_ffn_b2, L1_xattn_Wq, L1_xattn_bq, L1_xattn_Wk, L1_xattn_bk, L1_xattn_Wv, L1_xattn_bv, L1_xattn_Wo, L1_xattn_bo, L1_ffn_gate_w, L1_ffn_gate_b, L1_ffn_w1, L1_ffn_b1, L1_ffn_w2, L1_ffn_b2, L2_xattn_wq, L2_xattn_bq, L2_xattn_wk, L2_xattn_bk, L2_xattn_wv, L2_xattn_bv, L2_xattn_wo, L2_xattn_bo, L2_ffn_Wr, L2_ffn_br, L2_ffn_W1, L2_ffn_b1, L2_ffn_W2, L2_ffn_b2, L3_xattn_wq, L3_xattn_wk, L3_xattn_wv, L3_xattn_wo, L3_xattn_bo, L3_ffn_Wq, L3_ffn_Wk, L3_ffn_Wv, L3_ffn_Wo, L3_ffn_g1, L3_ffn_b1, L3_ffn_g2, L3_ffn_b2, L3_ffn_Wg, L3_ffn_W1, L3_ffn_W2):
    import jax
    import jax.numpy as jnp

    def _L0_xattn_ref(queries, context, wq, bq, wk, bk, wv, bv, wo, bo):
        import jax, jax.numpy as jnp
        import numpy as np
        D_MODEL = 128
        N_HEADS = 16
        HEAD_DIM = D_MODEL // N_HEADS
        B, NQ, D = queries.shape
        S = context.shape[1]
        H, HD = (N_HEADS, HEAD_DIM)
        scale = HD ** (-0.5)
        q = queries @ wq.T + bq
        k = context @ wk.T + bk
        v = context @ wv.T + bv
        q = q.reshape(B, NQ, H, HD).transpose(0, 2, 1, 3)
        k = k.reshape(B, S, H, HD).transpose(0, 2, 1, 3)
        v = v.reshape(B, S, H, HD).transpose(0, 2, 1, 3)
        attn = jnp.einsum('bhnd,bhsd->bhns', q, k) * scale
        attn = jax.nn.softmax(attn, axis=-1)
        out = jnp.einsum('bhns,bhsd->bhnd', attn, v)
        out = out.transpose(0, 2, 1, 3).reshape(B, NQ, D)
        return out @ wo.T + bo

    def _L0_ffn_ref(hidden_states, router_w, router_b, ln_g, ln_b, w1, b1, w2, b2):
        import jax, jax.numpy as jnp
        import numpy as np
        L, E, H, F, K = (4, 4, 128, 512, 2)
        B, S = (4, 256)
        EPS = 1e-05

        def _moe_layer(x, rw, rb, g, b, w1, b1, w2, b2):
            logits = jnp.einsum('bsh,he->bse', x, rw) + rb
            probs = jax.nn.softmax(logits, axis=-1)
            vals, idx = jax.lax.top_k(probs, K)
            vals = vals / vals.sum(axis=-1, keepdims=True)
            mu = x.mean(axis=-1, keepdims=True)
            xc = x - mu
            xhat = xc * jax.lax.rsqrt((xc * xc).mean(axis=-1, keepdims=True) + EPS)
            xe = xhat[None] * g[:, None, None, :] + b[:, None, None, :]
            h = jax.nn.gelu(jnp.einsum('ebsh,ehf->ebsf', xe, w1) + b1[:, None, None, :], approximate=False)
            y = jnp.einsum('ebsf,efh->ebsh', h, w2) + b2[:, None, None, :]
            expert_out = x[None] + y
            comb = jnp.einsum('bsk,bske->bse', vals, jax.nn.one_hot(idx, E, dtype=x.dtype))
            return jnp.einsum('bse,ebsh->bsh', comb, expert_out)
        x = hidden_states
        for l in range(L):
            x = _moe_layer(x, router_w[l], router_b[l], ln_g[l], ln_b[l], w1[l], b1[l], w2[l], b2[l])
        return x

    def _L1_xattn_ref(query, key, value, mask, Wq, bq, Wk, bk, Wv, bv, Wo, bo):
        import jax, jax.numpy as jnp
        import numpy as np
        import math
        B, S, D, H = (2, 256, 128, 16)
        DK = D // H

        def _split_heads(x):
            b, s, _ = x.shape
            return x.reshape(b, s, H, DK).transpose(0, 2, 1, 3)
        q = _split_heads(query @ Wq + bq)
        k = _split_heads(key @ Wk + bk)
        v = _split_heads(value @ Wv + bv)
        scores = jnp.einsum('bhqd,bhkd->bhqk', q, k) / math.sqrt(DK)
        scores = jnp.where(mask[:, None, :, :] == 0, jnp.float32(-1000000000.0), scores)
        p = jax.nn.softmax(scores, axis=-1)
        x = jnp.einsum('bhqk,bhkd->bhqd', p, v)
        x = x.transpose(0, 2, 1, 3).reshape(query.shape[0], -1, D)
        return x @ Wo + bo

    def _L1_ffn_ref(x, gate_w, gate_b, w1, b1, w2, b2):
        import jax, jax.numpy as jnp
        import numpy as np
        D_MODEL = 128
        FF = 512
        E = 8
        TOP_K = 2
        CAP_FACTOR = 1.25
        B, T = (4, 256)

        def _moe_forward(x, gate_w, gate_b, w1, b1, w2, b2):
            Bb, Tt, d = x.shape
            S = Bb * Tt
            C = int(CAP_FACTOR * S / E)
            xf = x.reshape(S, d)
            logits = xf @ gate_w + gate_b
            probs = jax.nn.softmax(logits, axis=1)
            topk_p, topk_i = jax.lax.top_k(probs, TOP_K)
            topk_pn = topk_p / jnp.sum(topk_p, axis=1, keepdims=True)
            rows = jnp.arange(S)
            w_te = jnp.zeros((S, E), xf.dtype).at[rows[:, None], topk_i].set(topk_pn)
            mask = jnp.zeros((S, E), bool).at[rows[:, None], topk_i].set(True)
            rank = jnp.cumsum(mask.astype(jnp.int32), axis=0)
            slot = jnp.where(mask & (rank <= C), rank - 1, C)
            e_grid = jnp.broadcast_to(jnp.arange(E), (S, E))
            t_grid = jnp.broadcast_to(rows[:, None], (S, E))
            buf = jnp.full((E, C + 1), S, jnp.int32).at[e_grid, slot].set(t_grid)
            idx = buf[:, :C]
            valid = idx < S
            x_pad = jnp.concatenate([xf, jnp.zeros((1, d), xf.dtype)], axis=0)
            xin = x_pad[idx]
            h = jax.nn.relu(jnp.einsum('ecd,edh->ech', xin, w1) + b1[:, None, :])
            out = jnp.einsum('ech,ehd->ecd', h, w2) + b2[:, None, :]
            w_pad = jnp.concatenate([w_te, jnp.zeros((1, E), xf.dtype)], axis=0)
            tok_w = w_pad[idx, jnp.arange(E)[:, None]]
            out = out * jnp.where(valid, tok_w, 0.0)[:, :, None]
            final = jnp.zeros((S + 1, d), xf.dtype).at[idx.reshape(-1)].add(out.reshape(-1, d))[:S]
            return final.reshape(Bb, Tt, d)
        return _moe_forward(x, gate_w, gate_b, w1, b1, w2, b2)

    def _L2_xattn_ref(query, key_value, wq, bq, wk, bk, wv, bv, wo, bo):
        import jax, jax.numpy as jnp
        import numpy as np
        B, SQ, SKV, E, H = (4, 256, 256, 128, 16)
        D = E // H
        b, sq, e = query.shape
        skv = key_value.shape[1]
        h, d = (wq.shape[0], wq.shape[1])
        q = query.reshape(b, sq, h, d)
        kv = key_value.reshape(b, skv, h, d)
        qh = jnp.einsum('bshd,hed->bshe', q, wq) + bq
        kh = jnp.einsum('bthd,hed->bthe', kv, wk) + bk
        vh = jnp.einsum('bthd,hed->bthe', kv, wv) + bv
        scores = jnp.einsum('bshd,bthd->bhst', qh, kh) / jnp.sqrt(jnp.asarray(d, qh.dtype))
        attn = jax.nn.softmax(scores, axis=-1)
        ctx = jnp.einsum('bhst,bthd->bshd', attn, vh)
        out = ctx.reshape(b, sq, e)
        return out @ wo.T + bo

    def _L2_ffn_ref(x, Wr, br, W1, b1, W2, b2):
        import jax, jax.numpy as jnp
        import numpy as np
        TOP_K = 2

        def _moe(x, Wr, br, W1, b1, W2, b2):
            B, S, D = x.shape
            E = Wr.shape[1]
            xt = x.reshape(-1, D)
            logits = xt @ Wr + br
            top_vals, top_idx = jax.lax.top_k(logits, TOP_K)
            mask = jnp.zeros_like(logits, dtype=bool).at[jnp.arange(xt.shape[0])[:, None], top_idx].set(True)
            sparse_logits = jnp.where(mask, logits, -jnp.inf)
            gate = jax.nn.softmax(sparse_logits, axis=-1)
            h = jax.nn.relu(jnp.einsum('td,edh->teh', xt, W1) + b1)
            y = jnp.einsum('teh,ehd->ted', h, W2) + b2
            out = jnp.einsum('ted,te->td', y, gate)
            return out.reshape(B, S, D)
        return _moe(x, Wr, br, W1, b1, W2, b2)

    def _L3_xattn_ref(x, cache_k, cache_v, cache_len, wq, wk, wv, wo, bo):
        import jax, jax.numpy as jnp
        import numpy as np
        N_HEADS = 16
        B, T, C = x.shape
        S = cache_k.shape[1]
        H = N_HEADS
        hd = C // H
        q = x @ wq.T
        k_new = x @ wk.T
        v_new = x @ wv.T
        pos = jnp.arange(S)
        past_mask = (pos[None, :] < cache_len[:, None])[..., None]
        past_k = jnp.where(past_mask, cache_k, 0.0)
        past_v = jnp.where(past_mask, cache_v, 0.0)
        k = jnp.concatenate([past_k, k_new], axis=1)
        v = jnp.concatenate([past_v, v_new], axis=1)

        def to_heads(t):
            return t.reshape(B, t.shape[1], H, hd).transpose(0, 2, 1, 3)
        qh, kh, vh = (to_heads(q), to_heads(k), to_heads(v))
        scores = jnp.einsum('bhqd,bhkd->bhqk', qh, kh) / np.sqrt(hd).astype(np.float32)
        max_cl = jnp.max(cache_len)
        key_valid = jnp.concatenate([pos < max_cl, jnp.ones((T,), bool)])
        NEG = jnp.float32(-1e+30)
        scores = jnp.where(key_valid[None, None, None, :], scores, NEG)
        attn = jax.nn.softmax(scores, axis=-1)
        out = jnp.einsum('bhqk,bhkd->bhqd', attn, vh)
        out = out.transpose(0, 2, 1, 3).reshape(B, T, C)
        return out @ wo.T + bo

    def _L3_ffn_ref(x, Wq, Wk, Wv, Wo, g1, b1, g2, b2, Wg, W1, W2):
        import jax, jax.numpy as jnp
        import numpy as np
        D_MODEL = 128
        N_HEADS = 16
        N_EXPERTS = 8
        TOP_K = 2
        EXPERT_HIDDEN = D_MODEL * 4 // N_EXPERTS

        def layer_norm(x, g, b, eps=1e-05):
            mu = jnp.mean(x, axis=-1, keepdims=True)
            var = jnp.var(x, axis=-1, keepdims=True)
            return (x - mu) * jax.lax.rsqrt(var + eps) * g + b
        B, S, D = x.shape
        H, dk = (N_HEADS, D // N_HEADS)
        xn = layer_norm(x, g1, b1)
        q = (xn @ Wq).reshape(B, S, H, dk).transpose(0, 2, 1, 3)
        k = (xn @ Wk).reshape(B, S, H, dk).transpose(0, 2, 1, 3)
        v = (xn @ Wv).reshape(B, S, H, dk).transpose(0, 2, 1, 3)
        scores = jnp.einsum('bhqd,bhkd->bhqk', q, k) / np.sqrt(dk)
        attn = jax.nn.softmax(scores, axis=-1)
        o = jnp.einsum('bhqk,bhkd->bhqd', attn, v)
        o = o.transpose(0, 2, 1, 3).reshape(B, S, D) @ Wo
        x = x + o
        xn2 = layer_norm(x, g2, b2)
        xf = xn2.reshape(B * S, D)
        gate = xf @ Wg
        topv, topi = jax.lax.top_k(gate, TOP_K)
        probs = jax.nn.softmax(topv, axis=-1)
        cw = jnp.sum(jax.nn.one_hot(topi, N_EXPERTS, dtype=xf.dtype) * probs[..., None], axis=1)
        h = jax.nn.relu(jnp.einsum('td,edh->teh', xf, W1))
        y = jnp.einsum('teh,ehd->ted', h, W2)
        moe = jnp.einsum('ted,te->td', y, cw).reshape(B, S, D)
        return x + moe
    x = x + _L0_xattn_ref(_layernorm(x, axis=-1), ctx_1024, L0_xattn_wq, L0_xattn_bq, L0_xattn_wk, L0_xattn_bk, L0_xattn_wv, L0_xattn_bv, L0_xattn_wo, L0_xattn_bo)
    x = x + _L0_ffn_ref(_layernorm(x, axis=-1), L0_ffn_router_w, L0_ffn_router_b, L0_ffn_ln_g, L0_ffn_ln_b, L0_ffn_w1, L0_ffn_b1, L0_ffn_w2, L0_ffn_b2)
    x = x + _L1_xattn_ref(_layernorm(x, axis=-1), ctx_1024, ctx_1024, mask_BxSxS2_ik0, L1_xattn_Wq, L1_xattn_bq, L1_xattn_Wk, L1_xattn_bk, L1_xattn_Wv, L1_xattn_bv, L1_xattn_Wo, L1_xattn_bo)
    x = x + _L1_ffn_ref(_layernorm(x, axis=-1), L1_ffn_gate_w, L1_ffn_gate_b, L1_ffn_w1, L1_ffn_b1, L1_ffn_w2, L1_ffn_b2)
    x = x + _L2_xattn_ref(_layernorm(x, axis=-1), ctx_1024, L2_xattn_wq, L2_xattn_bq, L2_xattn_wk, L2_xattn_bk, L2_xattn_wv, L2_xattn_bv, L2_xattn_wo, L2_xattn_bo)
    x = x + _L2_ffn_ref(_layernorm(x, axis=-1), L2_ffn_Wr, L2_ffn_br, L2_ffn_W1, L2_ffn_b1, L2_ffn_W2, L2_ffn_b2)
    x = x + _L3_xattn_ref(_layernorm(x, axis=-1), ctx_1024, ctx_1024, _lenS2, L3_xattn_wq, L3_xattn_wk, L3_xattn_wv, L3_xattn_wo, L3_xattn_bo)
    x = x + _L3_ffn_ref(_layernorm(x, axis=-1), L3_ffn_Wq, L3_ffn_Wk, L3_ffn_Wv, L3_ffn_Wo, L3_ffn_g1, L3_ffn_b1, L3_ffn_g2, L3_ffn_b2, L3_ffn_Wg, L3_ffn_W1, L3_ffn_W2)
    return x

_drawn_inputs = setup_inputs


def setup_inputs(seed=0):
    import zlib

    import numpy as np

    out = dict(_drawn_inputs(seed))
    spreads = {'L0_xattn_bq': (0.0, 0.1),
     'L0_xattn_bk': (0.0, 0.8),
     'L0_xattn_bv': (0.0, 0.1),
     'L0_xattn_bo': (0.0, 0.1),
     'L0_ffn_router_b': (0.0, 0.1),
     'L0_ffn_ln_g': (1.0, 0.6),
     'L0_ffn_ln_b': (0.0, 0.583),
     'L0_ffn_b1': (0.0, 0.1),
     'L0_ffn_b2': (0.0, 0.1),
     'L1_xattn_bq': (0.0, 0.302),
     'L1_xattn_bk': (0.0, 0.8),
     'L1_xattn_bv': (0.0, 0.1),
     'L1_xattn_bo': (0.0, 0.1),
     'L1_ffn_gate_b': (0.0, 0.1),
     'L1_ffn_b1': (0.0, 0.512),
     'L1_ffn_b2': (0.0, 0.1),
     'L2_xattn_bq': (0.0, 0.286),
     'L2_xattn_bk': (0.0, 0.8),
     'L2_xattn_bv': (0.0, 0.1),
     'L2_xattn_bo': (0.0, 0.1),
     'L2_ffn_br': (0.0, 0.1),
     'L2_ffn_b1': (0.0, 0.325),
     'L2_ffn_b2': (0.0, 0.1),
     'L3_xattn_bo': (0.0, 0.1),
     'L3_ffn_g1': (1.0, 0.2),
     'L3_ffn_b1': (0.0, 0.1),
     'L3_ffn_g2': (1.0, 0.2),
     'L3_ffn_b2': (0.0, 0.1)}
    factors = {}
    for name, (base, spread) in spreads.items():
        noise = np.random.default_rng([zlib.crc32(name.encode()), seed]).standard_normal(out[name].shape)
        drawn = base * np.exp(spread * noise) if base else spread * noise
        out[name] = jnp.asarray(drawn.astype(out[name].dtype))
    for name, factor in factors.items():
        out[name] = (out[name] * factor).astype(out[name].dtype)
    return out
```

```python
from contextlib import ExitStack

import concourse.bass as bass
from concourse import mybir

F32 = mybir.dt.float32
I32 = mybir.dt.int32
ALU = mybir.AluOpType
ACT = mybir.ActivationFunctionType
AX = mybir.AxisListType.X

P = 128
BATCH, SEQ = 16, 64
TILES = BATCH * SEQ // P
HEADS, HD = 16, 8
FF = 512
CH = FF // P
EPS = 1e-5
SCALE = HD ** -0.5
NEG_MASK = -1e9 / SCALE
NEG_CACHE = -1e30 / SCALE
CAPACITY = int(1.25 * BATCH * SEQ / 8)
LAYERS0, E0, E8 = 4, 4, 8

CACHE, SELF = 3, 4
GROUPS = [2, 2, 2, 4, 2]
GROUP_BASE = [TILES * sum(GROUPS[:a]) for a in range(5)]
B1_L0, LNG_L0, LNB_L0, B1_L1 = 0, 64, 80, 96
B1_L2, BQ, BK = 128, 160, 163
STEP_L1 = 2 * LAYERS0 * E0
STEP_L2 = STEP_L1 + 2 * E8


def build(nc, A, out):
    with ExitStack() as ctx:
        def sb(name, shape, dt=F32):
            return ctx.enter_context(nc.sbuf_tensor(name, shape, dt))

        def sem(name):
            return ctx.enter_context(nc.semaphore(name))

        x = sb("x", [P, TILES, P])
        cur = sb("cur", [P, TILES, P])
        xh = sb("xh", [P, TILES, P])
        curT = sb("curT", [P, TILES * P])
        xhT = sb("xhT", [P, TILES * P])
        xe = [sb(f"xe{i}", [P, TILES * P]) for i in range(2)]
        hs = [sb(f"hs{i}", [P, CH, 512]) for i in range(2)]
        w1s = [sb(f"w1s{i}", [P, FF]) for i in range(2)]
        w2s = [sb(f"w2s{i}", [P, CH, P]) for i in range(2)]
        ctx_tok = sb("ctx_tok", [P, TILES, P])
        ctxT = sb("ctxT", [P, TILES * P])
        cacheK = sb("cacheK", [P, TILES * P])
        cacheV = sb("cacheV", [SEQ, BATCH, P])
        nat = sb("nat", [P, 12, P])
        wat = sb("wat", [P, 20, P])
        rows8 = sb("rows8", [P, 3, HD])
        bt_rows = sb("bt_rows", [P, 2, P])
        bt = sb("bt", [P, 256])
        bcast = sb("bcast", [P, 7, P])
        bo = sb("bo", [1, 4, P])
        rbias = sb("rbias", [P, 4 * E0 + 2 * E8])
        rw = sb("rw", [P, 4 * E0 + 3 * E8])
        b2_l0 = sb("b2_l0", [E0, LAYERS0, P])
        b2_l12 = sb("b2_l12", [E8, 2, P])
        w1c = sb("w1c", [P, E8, FF // E8])
        w2c = sb("w2c", [P, CH, P])
        esel = sb("esel", [E8, E8, FF // E8])
        ident = sb("ident", [P, P])
        ones = sb("ones", [P, P])
        tri = sb("tri", [P, P])
        m16 = sb("m16", [P, HEADS])
        m4 = sb("m4", [P, 4])
        epow = sb("epow", [P, 2 * TILES])
        lay_gb = sb("lay_gb", [P, 2, E0])
        lay_b1 = sb("lay_b1", [P, E0 * CH])
        order = sb("order", [P, E8])
        neg = sb("neg", [P, 2])
        iota_k = sb("iota_k", [P, SEQ])
        iota_p = sb("iota_p", [P, 1])
        len_i = sb("len_i", [P, BATCH], I32)
        len_f = sb("len_f", [P, BATCH])
        len_max = sb("len_max", [P, 1])
        past_k = sb("past_k", [P, BATCH, SEQ])
        past_v = sb("past_v", [P, BATCH])
        kill_cache = sb("kill_cache", [P, SEQ], I32)
        mask = sb("mask", [P, TILES, SEQ], I32)
        kill = [sb(f"kill{i}", [P, SEQ], I32) for i in range(2)]
        xn = [sb(f"xn{i}", [P, P]) for i in range(2)]
        stat = [sb(f"stat{i}", [P, 6]) for i in range(2)]
        mv = [sb(f"mv{i}", [P, 2]) for i in range(2)]
        ve = [sb(f"ve{i}", [P, 1]) for i in range(2)]
        rstd = [sb(f"rstd{i}", [P, 1]) for i in range(2)]
        xnT = [sb(f"xnT{i}", [P, P]) for i in range(2)]
        kvT = [sb(f"kvT{i}", [P, P]) for i in range(2)]
        qT = [sb(f"qT{i}", [P, P]) for i in range(2)]
        kT = [sb(f"kT{i}", [P, P]) for i in range(2)]
        kbd = [sb(f"kbd{i}", [P, 2 * 4 * P]) for i in range(2)]
        vbd = [sb(f"vbd{i}", [P, 2, HEADS // 2, 2 * (HD + 1)]) for i in range(2)]
        vca = [sb(f"vca{i}", [P, 2, HEADS, HD + 1]) for i in range(2)]
        prob = [sb(f"prob{i}", [P, HEADS * P]) for i in range(2)]
        probT = sb("probT", [P, HEADS, P])
        smax = sb("smax", [P, HEADS])
        rsum = sb("rsum", [P, HEADS])
        on = sb("on", [P, HEADS, HD])
        oT = sb("oT", [P, P])
        stat8 = sb("stat8", [P, TILES, 6])
        mv8 = sb("mv8", [P, TILES, 2])
        ve8 = sb("ve8", [P, TILES])
        rstd8 = sb("rstd8", [P, TILES])
        g_log = sb("g_log", [P, TILES, E8])
        g_two = sb("g_two", [P, TILES, E8])
        g_key = sb("g_key", [P, TILES, E8])
        g_sel = sb("g_sel", [P, TILES, E8])
        g_exp = sb("g_exp", [P, TILES, E8])
        g_max = sb("g_max", [P, TILES])
        g_tmp = sb("g_tmp", [P, TILES])
        g_sum = sb("g_sum", [P, TILES])
        seen = sb("seen", [P, TILES, E8])
        comb = sb("comb", [P, TILES, E8])
        combT = sb("combT", [E8, TILES * P])

        ps = ctx.enter_context(nc.psum_tensor("ps", [P, 8, 512], F32))
        scores = ps[:, 0:4, :]
        hid = [ps[:, c, :] for c in range(4)]
        bankA, bankB = ps[:, 6, :], ps[:, 7, :]

        names = """in_x in_ctx in_wt in_bias in_w2nd in_mask in_w1a in_w1b in_w2a in_w2b
            c_id0 c_id c_m4a c_pool c_m16 c_dve c_bd c_past c_cache c_wT c_w_sb c_bT c_b_sb c_cT c_c_sb
            a_stat a_mv a_ve a_rstd a_xn a_xT a_xT_sb a_qkv a_qk_sb a_kv a_kbd a_vpast a_v a_s a_kill a_masked a_max a_sub a_exp
            a_pT a_pT_sb a_o a_rs a_on a_oT a_oT_sb a_y a_res a_aff
            n_stat n_mv n_ve n_rstd n_aff n_done n_T n_T_sb g_logits g_ln g_sub g_ex g_comb g_rank g_cT g_cT_sb g_b2 g_init
            e_xe e_h e_h_sb e_y e_acc l0_x l3_res l3_gate l3_gated l3_h l3_h_sb l3_y l3_x stored""".split()
        names += ["in_cv", 'g_csum', 'lay_pool', 'lay_act']
        S = {n: sem(n) for n in names}
        block = ctx.enter_context(nc.Block())

        def sview(a):
            k = P if a == CACHE else SEQ
            return scores[:, :, 0:4 * k].rearrange("p i (j k) -> p i j k", k=k)

        def pview(a, par):
            k = P if a == CACHE else SEQ
            return prob[par][:, 0:HEADS * k].rearrange("p (i j k) -> p i j k", i=4, k=k)

        def kview(a, par):
            k = P if a == CACHE else SEQ
            return kbd[par][:, 0:8 * k].rearrange("p (b j k) -> p b j k", b=2, k=k)

        def attention_tiles(a, eng, body):
            def at(t):
                ok = [k if 0 <= t + d < TILES else None for d, k in ((1, t + 1), (0, t), (-1, t - 1), (2, t + 2))]
                body(*ok, t % 2)
            at(-2)
            at(-1)
            at(0)
            at(1)
            with eng.Fori(0, 2) as pair:
                t = 2 * pair + 2
                body(t + 1, t, t - 1, t + 2, 0)
                body(t + 2, t + 1, t, t + 3, 1)
            for t in range(6, TILES + 1):
                at(t)

        def V(a, t):
            return TILES * a + t + 1

        def wait(eng, name, value):
            if not isinstance(value, int) or value > 0:
                eng.wait_ge(S[name], value)

        @block.sync
        def _(sp):
            sp.dma_start(x[:], A["x"].rearrange("b s d -> (b s) d").rearrange("(t p) d -> p t d", p=P)).then_inc(S["in_x"], 16)
            sp.dma_start(ctx_tok[:], A["ctx_1024"].rearrange("b s d -> (b s) d").rearrange("(t p) d -> p t d", p=P)).then_inc(S["in_ctx"], 16)
            slots = [("L0_xattn_wq", 0), ("L0_xattn_wk", 1), ("L0_xattn_wv", 2), ("L0_xattn_wo", 3), ("L2_xattn_wo", 7),
                     ("L3_xattn_wq", 8), ("L3_xattn_wk", 9), ("L3_xattn_wv", 10), ("L3_xattn_wo", 11)]
            for n, slot in slots:
                sp.dma_start(nat[:, slot, :], A[n]).then_inc(S["in_wt"], 16)
            for n, v in enumerate(("wq", "wk", "wv")):
                sp.dma_start(rows8[:, n, :], A[f"L2_xattn_{v}"].rearrange("h e d -> (h e) d")).then_inc(S["in_wt"], 16)
            for n, v in enumerate(("Wq", "Wk", "Wv", "Wo")):
                sp.dma_start(wat[:, 4 + n, :], A[f"L1_xattn_{v}"]).then_inc(S["in_wt"], 16)
                sp.dma_start(wat[:, 16 + n, :], A[f"L3_ffn_{v}"]).then_inc(S["in_wt"], 16)
            sp.dma_start(mask[:], A["mask_BxSxS2_ik0"].rearrange("b q k -> (b q) k").rearrange("(t p) k -> p t k", p=P)).then_inc(S["in_mask"], 16)
            w1_0, w2_0 = A["L0_ffn_w1"].rearrange("l e h f -> (l e) h f"), A["L0_ffn_w2"].rearrange("l e (c f) h -> (l e) f c h", f=P)
            done = 0
            for w1, w2, count in ((w1_0, w2_0, LAYERS0 * E0),
                                  (A["L1_ffn_w1"], A["L1_ffn_w2"].rearrange("e (c f) h -> e f c h", f=P), E8),
                                  (A["L2_ffn_W1"], A["L2_ffn_W2"].rearrange("e (c f) h -> e f c h", f=P), E8)):
                def pair(e, free):
                    for i in range(2):
                        if free is not None:
                            sp.wait_ge(S["e_y"], free + 2 * i)
                        n = "ab"[i]
                        sp.dma_start(w1s[i][:], w1[bass.ds(e + i, 1), :, :].rearrange("o h f -> (o h) f")).then_inc(S["in_w1" + n], 16)
                        sp.dma_start(w2s[i][:], w2[bass.ds(e + i, 1), :, :, :].rearrange("o f c h -> (o f) c h")).then_inc(S["in_w2" + n], 16)
                if done == 0:
                    pair(0, None)
                    with sp.Fori(1, count // 2) as e:
                        pair(2 * e, 4 * e - 2)
                else:
                    with sp.Fori(0, count // 2) as e:
                        pair(2 * e, 4 * e + 2 * done - 2)
                done += count
                if count == LAYERS0 * E0:
                    sp.dma_start(w1c[:], A["L3_ffn_W1"].rearrange("e h f -> h e f")).then_inc(S["in_w2nd"], 16)
                    sp.dma_start(w2c[:], A["L3_ffn_W2"].rearrange("(c g) f h -> (g f) c h", c=CH)).then_inc(S["in_w2nd"], 16)
            dst = out.rearrange("b s d -> (b s) d").rearrange("(t p) d -> p t d", p=P)
            for h in range(2):
                sp.wait_ge(S["l3_x"], h + 1)
                sp.dma_start(dst[:, 4 * h:4 * h + 4, :], x[:, 4 * h:4 * h + 4, :]).then_inc(S["stored"], 16)
            sp.wait_ge(S["stored"], 32)

        @block.gpsimd
        def _(pool):
            def ld(dst, src, s="in_bias"):
                pool.dma_start(dst, src).then_inc(S[s], 16)

            pool.memset(ident[:], 0.0).then_inc(S["c_id0"], 1)
            pool.memset(ones[:], 1.0).then_inc(S["c_id0"], 1)
            pool.memset(m16[:], 1.0).then_inc(S["c_id0"], 1)
            pool.memset(esel[:], 1.0).then_inc(S["c_id0"], 1)
            pool.memset(bt_rows[:], 0.0).then_inc(S["c_id0"], 1)
            pool.wait_ge(S["c_id0"], 5)
            pool.affine_select(out=ident[:], in_=ident[:], compare_op=ALU.not_equal, fill=1.0, base=0,
                               pattern=[[-1, P]], channel_multiplier=1).then_inc(S["c_id"], 1)
            pool.affine_select(out=m16[:], in_=m16[:], compare_op=ALU.is_ge, fill=0.0, base=0,
                               pattern=[[-HD, HEADS]], channel_multiplier=1).then_inc(S["c_id"], 1)
            pool.wait_ge(S["c_id"], 2)
            pool.affine_select(out=m16[:], in_=m16[:], compare_op=ALU.is_ge, fill=0.0, base=HD - 1,
                               pattern=[[HD, HEADS]], channel_multiplier=-1).then_inc(S["c_id"], 1)

            def row(v, n):
                return v.rearrange("(a n) -> a n", a=1) if n else v
            ld(bt_rows[0:64, 0, :], A["L0_ffn_b1"].rearrange("l e (c f) -> (l e c) f", f=P))
            ld(bt_rows[64:80, 0, :], A["L0_ffn_ln_g"].rearrange("l e h -> (l e) h"))
            ld(bt_rows[80:96, 0, :], A["L0_ffn_ln_b"].rearrange("l e h -> (l e) h"))
            ld(bt_rows[96:128, 0, :], A["L1_ffn_b1"].rearrange("e (c f) -> (e c) f", f=P))
            ld(bt_rows[0:32, 1, :], A["L2_ffn_b1"].rearrange("e (c f) -> (e c) f", f=P))
            for n, v in enumerate(("bq", "bk")):
                ld(bt_rows[32 + 3 * n:33 + 3 * n, 1, :], row(A[f"L0_xattn_{v}"], 1))
                ld(bt_rows[33 + 3 * n:34 + 3 * n, 1, :], row(A[f"L1_xattn_{v}"], 1))
                ld(bt_rows[34 + 3 * n:35 + 3 * n, 1, :], A[f"L2_xattn_{v}"].rearrange("(a h) e -> a (h e)", a=1))

            def every(v):
                return v.partition_broadcast(P)
            ld(len_i[:], every(A["_lenS2"]))
            ld(bcast[:, 0, :], every(A["L0_xattn_bv"]))
            ld(bcast[:, 1, :], every(A["L1_xattn_bv"]))
            ld(bcast[:, 2, :], every(A["L2_xattn_bv"].rearrange("h e -> (h e)")))
            for n, v in enumerate(("g1", "b1", "g2", "b2")):
                ld(bcast[:, 3 + n, :], every(A[f"L3_ffn_{v}"]))
            for l in range(4):
                ld(bo[:, l, :], row(A[f"L{l}_xattn_bo"], 1))
            ld(rbias[:, 0:16], every(A["L0_ffn_router_b"].rearrange("l e -> (l e)")))
            ld(rbias[:, 16:24], every(A["L1_ffn_gate_b"]))
            ld(rbias[:, 24:32], every(A["L2_ffn_br"]))
            ld(rw[:, 0:16].rearrange("p (l e) -> p l e", e=E0), A["L0_ffn_router_w"].rearrange("l h e -> h l e"))
            ld(rw[:, 16:24], A["L1_ffn_gate_w"])
            ld(rw[:, 24:32], A["L2_ffn_Wr"])
            ld(rw[:, 32:40], A["L3_ffn_Wg"])
            ld(b2_l0[:], A["L0_ffn_b2"].rearrange("l e h -> e l h"))
            ld(b2_l12[:, 0, :], A["L1_ffn_b2"])
            ld(b2_l12[:, 1, :], A["L2_ffn_b2"])
            pool.dma_start(cacheV[:], A["ctx_1024"].rearrange("b s d -> s b d")).then_inc(S["in_cv"], 16)

            pool.affine_select(out=tri[:], in_=ones[:], compare_op=ALU.is_ge, fill=0.0, base=0,
                               pattern=[[1, P]], channel_multiplier=-1).then_inc(S["c_pool"], 1)
            pool.affine_select(out=esel[:], in_=esel[:], compare_op=ALU.is_equal, fill=0.0, base=0,
                               pattern=[[-1, E8], [0, FF // E8]], channel_multiplier=1).then_inc(S["c_pool"], 1)
            pool.memset(epow[:, 0:TILES], -0.5).then_inc(S["c_pool"], 1)
            pool.memset(epow[:, TILES:2 * TILES], EPS).then_inc(S["c_pool"], 1)
            pool.memset(neg[:, 0:1], NEG_MASK).then_inc(S["c_pool"], 1)
            pool.memset(neg[:, 1:2], NEG_CACHE).then_inc(S["c_pool"], 1)
            pool.iota(order[:], pattern=[[-1, E8]], base=E8, channel_multiplier=0,
                      allow_small_or_imprecise_dtypes=True).then_inc(S["c_pool"], 1)
            pool.iota(iota_k[:], pattern=[[1, SEQ]], base=0, channel_multiplier=0,
                      allow_small_or_imprecise_dtypes=True).then_inc(S["c_pool"], 1)
            pool.iota(iota_p[:], pattern=[[0, 1]], base=0, channel_multiplier=1,
                      allow_small_or_imprecise_dtypes=True).then_inc(S["c_pool"], 1)
            for i in range(2):
                pool.memset(vbd[i][:], 0.0).then_inc(S["c_pool"], 1)
                pool.memset(vca[i][:], 1.0).then_inc(S["c_pool"], 1)
            pool.wait_ge(S["c_pool"], 13)
            for i in range(2):
                pool.memset(vbd[i][0:SEQ, :, :, HD:HD + 1], 1.0).then_inc(S["c_pool"], 1)
                pool.memset(vbd[i][SEQ:P, :, :, 2 * HD + 1:2 * HD + 2], 1.0).then_inc(S["c_pool"], 1)
            pool.wait_ge(S["c_pool"], 17)
            pool.wait_ge(S["c_c_sb"], 2)
            pool.wait_ge(S["c_dve"], 1)

            def mult(o, a, b):
                return pool.tensor_tensor(o, a, b, ALU.mult)

            def power(v, s, e, n, name, val):
                pool.wait_ge(S[name + "mv"], val)
                pool.tensor_tensor(e, v, epow[:, TILES:TILES + n], ALU.add).then_inc(S[name + "ve"], 1)
                pool.wait_ge(S[name + "ve"], val)
                pool.tensor_tensor(s, e, epow[:, 0:n], ALU.pow).then_inc(S[name + "rstd"], 1)

            def attention(a):
                def body(n, c, p, nn, par):
                    o = 1 - par
                    if n is not None:
                        if a < CACHE:
                            wait(pool, "a_qkv", V(a, n) - 2)
                            pool.tensor_copy(kvT[o][:], ctxT[:, bass.ds(n * P, P)]).then_inc(S["a_kv"], 1)
                        if a == CACHE:
                            if not isinstance(n, int) or n >= 2:
                                pool.wait_ge(S["a_o"], V(a, n) - 2)
                            pool.tensor_copy(vca[o][0:SEQ, :, :, 0:HD],
                                             cacheV[:, bass.ds(n * 2, 2), :].rearrange("k b (h d) -> k b h d", d=HD)
                                             ).then_inc(S["a_vpast"], 1)
                        pool.wait_ge(S["a_qk_sb"], V(a, n))
                        wait(pool, "a_s", V(a, n) - 2)
                        kv = kview(a, o)
                        k0 = SEQ if a == CACHE else 0
                        hm = m4[:, :, None].broadcast_to([P, 4, SEQ])
                        for b in range(2):
                            if a == CACHE:
                                old = cacheK[:, bass.ds(n * P + b * SEQ, SEQ)]
                                mult(kv[:, b, :, 0:SEQ], old[:, None, :].broadcast_to([P, 4, SEQ]), hm)
                            last = mult(kv[:, b, :, k0:k0 + SEQ],
                                        kT[o][:, None, b * SEQ:(b + 1) * SEQ].broadcast_to([P, 4, SEQ]), hm)
                        last.then_inc(S["a_kbd"], 1)
                    if nn is not None:
                        power(mv[par][:, 1:2], rstd[par][:], ve[par][:], 1, "a_", V(a, nn))
                attention_tiles(a, pool, body)

            def norm(k):
                power(mv8[:, :, 1], rstd8[:], ve8[:], TILES, "n_", k + 1)

            attention(0)
            norm(0)
            with pool.Fori(0, LAYERS0) as l:
                norm(l + 1)
                pool.tensor_copy(lay_gb[:], bt[:, LNG_L0:LNB_L0 + 16].rearrange("p (w l e) -> p w l e", w=2, e=E0)[:, :, bass.ds(l, 1), :]
                                 .rearrange("p w o e -> p w (o e)")).then_inc(S["lay_pool"], 1)
                pool.wait_ge(S["lay_pool"], l + 1)
                pool.wait_ge(S["n_T_sb"], 4 * l + 4)
                for e in range(E0):
                    g = l * E0 + e
                    if e >= 2:
                        pool.wait_ge(S["e_h"], 8 * (g - 2) + 8)
                    pool.nop(nofuse=True)
                    pool.tensor_scalar(xe[e % 2][:], xhT[:], lay_gb[:, 0, e:e + 1], lay_gb[:, 1, e:e + 1],
                                       ALU.mult, ALU.add).then_inc(S["e_xe"], 1)
            attention(1)
            norm(5)
            attention(2)
            norm(6)
            pool.wait_ge(S["c_past"], 2)
            mult(cacheK[:].rearrange("p (b k) -> p b k", k=SEQ), ctxT[:].rearrange("p (b k) -> p b k", k=SEQ),
                 past_k[:]).then_inc(S["c_cache"], 1)
            pool.wait_ge(S["in_cv"], 16)
            mult(cacheV[:], cacheV[:], past_v[0:SEQ, :, None].broadcast_to([SEQ, BATCH, P])).then_inc(S["c_cache"], 1)
            pool.wait_ge(S["c_cache"], 2)
            attention(CACHE)
            norm(7)
            attention(SELF)
            norm(8)
            pool.wait_ge(S["a_res"], TILES * 5)
            pool.tensor_tensor(x[:], x[:], cur[:], ALU.add).then_inc(S["l3_res"], 1)

        @block.scalar
        def _(act):
            def copy(o, i):
                return act.activation(o, i, ACT.Copy)

            act.wait_ge(S["c_bT"], 1)
            copy(bt[:], ps[:, 4, 0:256]).then_inc(S["c_b_sb"], 1)
            for g in range(2):
                act.wait_ge(S["c_cT"], g + 1)
                copy(ctxT[:, 512 * g:512 * g + 512], ps[:, 5 + g, :]).then_inc(S["c_c_sb"], 1)
            for g in range(3):
                act.wait_ge(S["c_wT"], g + 1)
                dst = wat[:, [0, 8, 12][g]:[0, 8, 12][g] + 4, :]
                copy(dst, ps[:, g, :].rearrange("p (m n) -> p m n", n=P)).then_inc(S["c_w_sb"], 1)

            def attention(a):
                def body(n, c, p, nn, par):
                    o = 1 - par
                    if n is not None:
                        act.wait_ge(S["a_xT"], V(a, n))
                        copy(xnT[o][:], bankA[:, 0:P]).then_inc(S["a_xT_sb"], 1)
                        act.wait_ge(S["a_qkv"], V(a, n))
                        wait(act, "a_s", V(a, n) - 2)
                        wait(act, "a_kbd", V(a, n) - 2)
                        if a < CACHE:
                            act.activation(qT[o][:], bankA[:, 0:P], ACT.Identity, bias=bt[:, BQ + a:BQ + a + 1])
                            last = act.activation(kT[o][:], bankA[:, P:2 * P], ACT.Identity, bias=bt[:, BK + a:BK + a + 1])
                        else:
                            copy(qT[o][:], bankA[:, 0:P])
                            last = copy(kT[o][:], bankA[:, P:2 * P])
                        last.then_inc(S["a_qk_sb"], 1)
                    if p is not None:
                        act.wait_ge(S["a_oT"], V(a, p))
                        copy(oT[:], bankB[:, 256:384]).then_inc(S["a_oT_sb"], 1)
                    if c is not None:
                        act.wait_ge(S["a_sub"], V(a, c))
                        pv = pview(a, par)
                        act.activation(pv, pv, ACT.Exp, scale=SCALE).then_inc(S["a_exp"], 1)
                        wait(act, "a_o", V(a, c) - 1)
                        for q in range(GROUPS[a]):
                            act.wait_ge(S["a_pT"], GROUP_BASE[a] + GROUPS[a] * c + q + 1)
                            copy(probT[:, 4 * q:4 * q + 4, :], ps[:, 4 + q % 2, :].rearrange("p (c n) -> p c n", n=P)
                                 ).then_inc(S["a_pT_sb"], 1)
                attention_tiles(a, act, body)

            def transposed(call, dst):
                for g in range(2):
                    act.wait_ge(S["n_T"], 2 * call + g + 1)
                    copy(dst[:, 512 * g:512 * g + 512], ps[:, 6 + g, :]).then_inc(S["n_T_sb"], 1)

            def gates(m, e):
                act.wait_ge(S["g_sub"], m + 1)
                act.activation(g_exp[:, :, 0:e], g_exp[:, :, 0:e], ACT.Exp).then_inc(S["g_ex"], 1)

            def gates_T(m, e):
                for g in range(2):
                    act.wait_ge(S["g_cT"], 2 * m + g + 1)
                    copy(combT[0:e, 512 * g:512 * g + 512], ps[0:e, 6 + g, :]).then_inc(S["g_cT_sb"], 1)

            def hidden(step, parity, col, func, first=False):
                if not first:
                    wait(act, "e_y", step - 1)
                for c in range(CH):
                    act.wait_ge(S["e_h"], 4 * step + c + 1)
                    act.activation(hs[parity][:, c, :], hid[c], func, bias=lay_b1[:, col + c:col + c + 1]).then_inc(S["e_h_sb"], 1)

            def biases(col, n, count, used=None):
                if used is not None:
                    act.wait_ge(S["e_h_sb"], used)
                    act.nop(nofuse=True)
                act.activation(lay_b1[:, 0:n], bt[:, bass.ds(col, n)], ACT.Copy).then_inc(S["lay_act"], 1)
                act.wait_ge(S["lay_act"], count)

            attention(0)
            with act.Fori(0, LAYERS0) as l:
                transposed(2 * l, curT)
                transposed(2 * l + 1, xhT)
                biases(B1_L0 + 16 * l, 16, l + 1)
                gates(l, E0)
                for s in range(2 * E0):
                    hidden(8 * l + s, s % 2, s // 2 * CH, ACT.Gelu, first=(s < 2))
                    if s == 0:
                        gates_T(l, E0)
            for a, m, base, table in ((1, 4, STEP_L1, B1_L1), (2, 5, STEP_L2, B1_L2)):
                attention(a)
                transposed(m + 4, xhT)
                gates(m, E8)
                laid = LAYERS0 + E8 * (m - 4) + 1
                biases(table, CH, laid, CH * base)
                hidden(base, 0, 0, ACT.Relu)
                gates_T(m, E8)
                hidden(base + 1, 1, 0, ACT.Relu)
                with act.Fori(1, E8) as e:
                    biases(table + CH * e, CH, laid + e, CH * (base + 2 * e))
                    for h in range(2):
                        hidden(base + 2 * e + h, h, 0, ACT.Relu)
            attention(CACHE)
            attention(SELF)
            transposed(10, xhT)
            gates(6, E8)
            for s in range(2):
                for c in range(CH):
                    act.wait_ge(S["l3_h"], 4 * s + c + 1)
                    act.activation(hs[s][:, c, :], hid[c], ACT.Relu).then_inc(S["l3_h_sb"], 1)
                if s == 0:
                    gates_T(6, E8)

        @block.tensor
        def _(pe):
            pe.wait_ge(S["c_id"], 3)
            pe.wait_ge(S["in_bias"], 16 * BIAS_LOADS)
            for n in range(2):
                last = pe.transpose(ps[:, 4, n * P:(n + 1) * P], bt_rows[:, n, :], ident[:])
            last.then_inc(S["c_bT"], 1)
            pe.wait_ge(S["in_ctx"], 16)
            for t in range(TILES):
                last = pe.transpose(ps[:, 5 + t // 4, (t % 4) * P:(t % 4 + 1) * P], ctx_tok[:, t, :], ident[:])
                if t % 4 == 3:
                    last.then_inc(S["c_cT"], 1)
            pe.wait_ge(S["in_wt"], 16 * 20)
            pe.wait_ge(S["c_bd"], 3)
            for m in range(12):
                last = pe.transpose(ps[:, m // 4, (m % 4) * P:(m % 4 + 1) * P], nat[:, m, :], ident[:])
                if m % 4 == 3:
                    last.then_inc(S["c_wT"], 1)
            pe.wait_ge(S["c_w_sb"], 3)
            pe.wait_ge(S["c_c_sb"], 2)
            pe.wait_ge(S["c_b_sb"], 1)

            def attention(a):
                wq, wk, wv, wo = (wat[:, 4 * a + n, :] for n in range(4))

                def front_x(n, o):
                    pe.wait_ge(S["a_xn"], V(a, n))
                    wait(pe, "a_qk_sb", V(a, n) - 1)
                    wait(pe, "a_v", V(a, n) - 1)
                    pe.transpose(bankA[:, 0:P], xn[o][:], ident[:]).then_inc(S["a_xT"], 1)

                def front_qkv(n, o):
                    kv = kvT[o] if a < CACHE else xnT[o]
                    if a < CACHE:
                        pe.wait_ge(S["a_kv"], V(a, n))
                    pe.wait_ge(S["a_xT_sb"], V(a, n))
                    pe.matmul(bankA[:, 0:P], lhsT=wq, rhs=xnT[o][:], start=True, stop=True)
                    pe.matmul(bankA[:, P:2 * P], lhsT=wk, rhs=kv[:], start=True, stop=True)
                    for b in range(2):
                        for half in ((1,) if a == CACHE else (0, 1)):
                            last = pe.matmul(bankA[64 * half:64 * half + 64, (2 + b) * P:(3 + b) * P],
                                             lhsT=kv[:, 64 * b:64 * b + 64], rhs=wv, start=True, stop=True)
                    last.then_inc(S["a_qkv"], 1)

                def score(n, o):
                    pe.wait_ge(S["a_qk_sb"], V(a, n))
                    pe.wait_ge(S["a_kbd"], V(a, n))
                    wait(pe, "a_sub", V(a, n) - 1)
                    kv = kview(a, o)
                    for i in range(4):
                        r = slice(32 * i, 32 * i + 32)
                        for b in range(2):
                            last = pe.matmul(sview(a)[64 * b:64 * b + 64, i, :, :], lhsT=qT[o][r, 64 * b:64 * b + 64],
                                             rhs=kv[r, b, :, :], start=True, stop=True)
                    last.then_inc(S["a_s"], 1)

                def turn(c, par):
                    pe.wait_ge(S["a_exp"], V(a, c))
                    for q in range(GROUPS[a]):
                        done = GROUP_BASE[a] + GROUPS[a] * c + q
                        wait(pe, "a_pT_sb", done - 1)
                        for k in range(4):
                            ch = 4 * q + k
                            last = pe.transpose(ps[:, 4 + q % 2, k * P:(k + 1) * P], prob[par][:, ch * P:(ch + 1) * P], ident[:])
                        last.then_inc(S["a_pT"], 1)

                def values(p, o):
                    pe.wait_ge(S["a_pT_sb"], GROUP_BASE[a] + GROUPS[a] * (p + 1))
                    pe.wait_ge(S["a_v"], V(a, p))
                    if a == CACHE:
                        pe.wait_ge(S["a_vpast"], p + 1)
                    wait(pe, "a_res", V(a, p) - 1)
                    chunks = 4 * GROUPS[a]
                    w = HEADS * (HD + 1) // chunks
                    v = vca[o] if a == CACHE else vbd[o]
                    for c in range(chunks):
                        for b in range(2):
                            last = pe.matmul(bankB[64 * b:64 * b + 64, w * c:w * c + w], lhsT=probT[:, c, 64 * b:64 * b + 64],
                                             rhs=v[:, b, c, :], start=True, stop=True)
                    last.then_inc(S["a_o"], 1)

                def out_T(p):
                    pe.wait_ge(S["a_on"], V(a, p))
                    pe.transpose(bankB[:, 256:384], on[:].rearrange("p h d -> p (h d)"), ident[:]).then_inc(S["a_oT"], 1)

                def out_y(p):
                    pe.wait_ge(S["a_oT_sb"], V(a, p))
                    last = pe.matmul(bankB[:, 384:512], lhsT=oT[:], rhs=wo, start=True, stop=(a == SELF))
                    if a != SELF:
                        last = pe.matmul(bankB[:, 384:512], lhsT=ones[0:1, :], rhs=bo[:, a, :], start=False, stop=True)
                    last.then_inc(S["a_y"], 1)

                def body(n, c, p, nn, par):
                    o = 1 - par
                    if n is not None:
                        front_x(n, o)
                    if p is not None:
                        values(p, o)
                    if n is not None:
                        front_qkv(n, o)
                    if p is not None:
                        out_T(p)
                    if n is not None:
                        score(n, o)
                    if p is not None:
                        out_y(p)
                    if c is not None:
                        turn(c, par)
                attention_tiles(a, pe, body)
                pe.wait_ge(S["a_res"], TILES * (a + 1))

            def turn_tokens(call, src):
                for g in range(2):
                    for k in range(4):
                        last = pe.transpose(ps[:, 6 + g, k * P:(k + 1) * P], src[:, 4 * g + k, :], ident[:])
                    last.then_inc(S["n_T"], 1)
                pe.wait_ge(S["n_T_sb"], 2 * call + 2)

            def router(srcT, cols, e):
                for t in range(TILES):
                    last = pe.matmul(ps[:, 6, t * e:(t + 1) * e], lhsT=srcT[:, t * P:(t + 1) * P], rhs=rw[:, cols],
                                     start=True, stop=True)
                last.then_inc(S["g_logits"], 1)

            def rank():
                pe.wait_ge(S["g_rank"], 1)
                pe.matmul(bankA[:, 64:128], lhsT=tri[:], rhs=g_sel[:].rearrange("p t e -> p (t e)"), start=True, stop=False)
                pe.matmul(bankA[:, 64:128], lhsT=ones[:], rhs=seen[:].rearrange("p t e -> p (t e)"), start=False, stop=True
                          ).then_inc(S["g_rank"], 1)

            def gates_T(m, e):
                pe.wait_ge(S["g_comb"], m + 1)
                for g in range(2):
                    for k in range(4):
                        last = pe.transpose(ps[0:e, 6 + g, k * P:(k + 1) * P], comb[:, 4 * g + k, 0:e], ident[:])
                    last.then_inc(S["g_cT"], 1)
                pe.wait_ge(S["g_cT_sb"], 2 * m + 2)

            def gated_bias(b2, e):
                for t in range(TILES):
                    last = pe.matmul(ps[:, 6 + t // 4, (t % 4) * P:(t % 4 + 1) * P], lhsT=combT[0:e, t * P:(t + 1) * P],
                                     rhs=b2, start=True, stop=True)
                last.then_inc(S["g_b2"], 1)

            def hidden(step, half, slot, loads, src, first=False):
                if half == 0:
                    pe.wait_ge(S["in_w1" + "ab"[slot]], loads)
                for c in range(CH):
                    if not first:
                        wait(pe, "e_h_sb", 4 * step + c - 3)
                    pe.matmul(hid[c], lhsT=w1s[slot][:, c * P:(c + 1) * P], rhs=src[:, 512 * half:512 * half + 512],
                              start=True, stop=True).then_inc(S["e_h"], 1)

            def outputs(step, half, slot, loads, first=False):
                pe.wait_ge(S["e_h_sb"], 4 * step + 4)
                if half == 0:
                    pe.wait_ge(S["in_w2" + "ab"[slot]], loads)
                if not first:
                    wait(pe, "e_acc", step - 1)
                for k in range(4):
                    for c in range(CH):
                        last = pe.matmul(ps[:, 4 + half, k * P:(k + 1) * P], lhsT=hs[half][:, c, k * P:(k + 1) * P],
                                         rhs=w2s[slot][:, c, :], start=(c == 0), stop=(c == CH - 1))
                last.then_inc(S["e_y"], 1)

            attention(0)
            with pe.Fori(0, LAYERS0) as l:
                pe.wait_ge(S["n_done"], l + 2)
                turn_tokens(2 * l, cur)
                turn_tokens(2 * l + 1, xh)
                router(curT, bass.ds(l * E0, E0), E0)
                for s in range(2 * E0 + 1):
                    if s < 2 * E0:
                        e = s // 2
                        if s % 2 == 0:
                            pe.wait_ge(S["e_xe"], E0 * l + e + 1)
                        hidden(8 * l + s, s % 2, e % 2, 16 * (2 * l + e // 2 + 1), xe[e % 2], first=(s == 0))
                    if s == 0:
                        gates_T(l, E0)
                        gated_bias(b2_l0[:, bass.ds(l, 1), :].rearrange("e o h -> e (o h)"), E0)
                    else:
                        outputs(8 * l + s - 1, (s - 1) % 2, (s - 1) // 2 % 2, 16 * (2 * l + (s - 1) // 4 + 1), first=(s < 3))
                pe.wait_ge(S["g_init"], l + 1)
            for a, m, base in ((1, 4, STEP_L1), (2, 5, STEP_L2)):
                pe.wait_ge(S["e_acc"], base)
                attention(a)
                pe.wait_ge(S["n_done"], m + 2)
                turn_tokens(m + 4, xh)
                router(xhT, slice(16 + 8 * (m - 4), 24 + 8 * (m - 4)), E8)
                hidden(base, 0, 0, 16 * (base // 4 + 1), xhT)
                if m == 4:
                    rank()
                gates_T(m, E8)
                gated_bias(b2_l12[:, m - 4, :], E8)

                def pair(e, final, base=base):
                    for k in range(4):
                        st = base + 2 * e
                        if not (final and k == 3):
                            loads = 16 * (base // 4 + 1) + (8 * (e + (2 if k == 3 else 0)))
                            hidden(st + k + 1, (k + 1) % 2, (k + 1) // 2 % 2, loads, xhT)
                        outputs(st + k, k % 2, k // 2, 16 * (base // 4 + 1) + 8 * e)
                with pe.Fori(0, E8 // 2 - 1) as e:
                    pair(2 * e, False)
                pair(E8 - 2, True)
                pe.wait_ge(S["g_init"], m + 1)
            pe.wait_ge(S["e_acc"], STEP_L2 + 2 * E8)
            attention(CACHE)
            attention(SELF)
            pe.wait_ge(S["n_done"], 9)
            turn_tokens(10, xh)
            router(xhT, slice(32, 40), E8)
            pe.wait_ge(S["in_w2nd"], 32)

            def hidden3(s):
                for c in range(CH):
                    wait(pe, "l3_h_sb", 4 * s + c - 3)
                    pe.matmul(hid[c], lhsT=w1c[:].rearrange("p e f -> p (e f)")[:, c * P:(c + 1) * P],
                              rhs=xhT[:, 512 * s:512 * s + 512], start=True, stop=True).then_inc(S["l3_h"], 1)
            hidden3(0)
            gates_T(6, E8)
            for s in range(2):
                for c in range(CH):
                    k = 4 * s + c
                    wait(pe, "l3_gated", k - 1)
                    pe.matmul(ps[:, 4 + k % 2, :], lhsT=esel[:].rearrange("e g f -> e (g f)")[:, c * P:(c + 1) * P],
                              rhs=combT[:, 512 * s:512 * s + 512], start=True, stop=True).then_inc(S["l3_gate"], 1)
                if s == 0:
                    hidden3(1)
                pe.wait_ge(S["l3_gated"], 4 * s + 4)
                for k in range(4):
                    for c in range(CH):
                        last = pe.matmul(ps[:, 6 + s, k * P:(k + 1) * P], lhsT=hs[s][:, c, k * P:(k + 1) * P],
                                         rhs=w2c[:, c, :], start=(c == 0), stop=(c == CH - 1))
                last.then_inc(S["l3_y"], 1)

        @block.vector
        def _(dve):
            def link(ins, name, value):
                ins.then_inc(S[name], 1)
                dve.wait_ge(S[name], value)

            dve.wait_ge(S["c_id"], 3)
            dve.tensor_reduce(m4[:], m16[:].rearrange("p (i j) -> p j i", j=4), AX, ALU.add).then_inc(S["c_dve"], 1)
            dve.wait_ge(S["in_wt"], 16 * 20)
            for n in range(3):
                dve.tensor_tensor(nat[:, 4 + n, :].rearrange("p (h d) -> p h d", d=HD),
                                  rows8[:, n:n + 1, :].broadcast_to([P, HEADS, HD]),
                                  m16[:, :, None].broadcast_to([P, HEADS, HD]), ALU.mult).then_inc(S["c_bd"], 1)
            dve.wait_ge(S["in_bias"], 16 * BIAS_LOADS)
            dve.wait_ge(S["c_pool"], 17)
            link(dve.tensor_copy(len_f[:], len_i[:]), "c_dve", 2)
            link(dve.tensor_reduce(len_max[:], len_f[:], AX, ALU.max), "c_dve", 3)
            dve.tensor_tensor(past_k[:], iota_k[:, None, :].broadcast_to([P, BATCH, SEQ]),
                              len_f[:, :, None].broadcast_to([P, BATCH, SEQ]), ALU.is_lt).then_inc(S["c_past"], 1)
            dve.tensor_tensor(past_v[:], iota_p[:, 0:1].broadcast_to([P, BATCH]), len_f[:], ALU.is_lt).then_inc(S["c_past"], 1)
            dve.tensor_scalar(kill_cache[:], iota_k[:], len_max[:, 0:1], None, ALU.is_ge).then_inc(S["c_past"], 1)
            dve.wait_ge(S["in_x"], 16)
            dve.wait_ge(S["in_mask"], 16)

            def attention(a):
                src = cur if a == SELF else x

                def stats(t, par):
                    link(dve.bn_stats(stat[par][:], src[:, bass.ds(t, 1), :].rearrange("p o d -> p (o d)")), "a_stat", V(a, t))
                    dve.nop(nofuse=True)
                    dve.bn_aggr(mv[par][:], stat[par][:]).then_inc(S["a_mv"], 1)

                def normal(t, par):
                    dve.wait_ge(S["a_mv"], V(a, t))
                    dve.wait_ge(S["a_rstd"], V(a, t))
                    wait(dve, "a_xT", V(a, t) - 2)
                    o = dve.tensor_scalar(xn[par][:], src[:, bass.ds(t, 1), :].rearrange("p o d -> p (o d)"),
                                          mv[par][:, 0:1], rstd[par][:, 0:1], ALU.subtract, ALU.mult)
                    if a == SELF:
                        link(o, "a_aff", 2 * t + 1)
                        link(dve.tensor_tensor(xn[par][:], xn[par][:], bcast[:, 3, :], ALU.mult), "a_aff", 2 * t + 2)
                        o = dve.tensor_tensor(xn[par][:], xn[par][:], bcast[:, 4, :], ALU.add)
                    o.then_inc(S["a_xn"], 1)

                def softmax_head(c, par):
                    dve.wait_ge(S["a_s"], V(a, c))
                    s, k = sview(a), (P if a == CACHE else SEQ)
                    full = [P, 4, 4, SEQ]
                    if a == 1:
                        link(dve.tensor_scalar(kill[par][:], mask[:, bass.ds(c, 1), :].rearrange("p o k -> p (o k)"),
                                               0, None, ALU.is_equal), "a_kill", c + 1)
                        dve.nop(nofuse=True)
                        link(dve.copy_predicated(s, kill[par][:, None, None, :].broadcast_to(full),
                                                 neg[:, 0:1, None, None].broadcast_to(full)), "a_masked", c + 1)
                    if a == CACHE:
                        dve.nop(nofuse=True)
                        link(dve.copy_predicated(s[:, :, :, 0:SEQ], kill_cache[:, None, None, :].broadcast_to(full),
                                                 neg[:, 1:2, None, None].broadcast_to(full)), "a_masked", TILES + c + 1)
                    mx = smax[:].rearrange("p (i j) -> p i j", j=4)
                    link(dve.tensor_reduce(mx, s, AX, ALU.max), "a_max", V(a, c))
                    if a > 0 or not isinstance(c, int) or c >= 2:
                        if isinstance(c, int) and c < 2:
                            dve.wait_ge(S["a_pT"], GROUP_BASE[a])
                        else:
                            dve.wait_ge(S["a_pT"], GROUP_BASE[a] + GROUPS[a] * (c - 1))
                    dve.tensor_tensor(pview(a, par), s, mx[:, :, :, None].broadcast_to([P, 4, 4, k]), ALU.subtract
                                      ).then_inc(S["a_sub"], 1)

                def out_norm(p):
                    dve.wait_ge(S["a_o"], V(a, p))
                    o = bankB[:, 0:HEADS * (HD + 1)].rearrange("p (h w) -> p h w", w=HD + 1)
                    link(dve.reciprocal(rsum[:], o[:, :, HD]), "a_rs", V(a, p))
                    dve.tensor_tensor(on[:], o[:, :, 0:HD], rsum[:, :, None].broadcast_to([P, HEADS, HD]), ALU.mult
                                      ).then_inc(S["a_on"], 1)

                def value_slot(n, o):
                    dve.wait_ge(S["a_qkv"], V(a, n))
                    dve.wait_ge(S["a_qk_sb"], V(a, n))
                    wait(dve, "a_o", V(a, n) - 2)
                    ps_v = bankA[:, 2 * P:4 * P]
                    if a == CACHE:
                        last = dve.tensor_copy(vca[o][SEQ:P, :, :, 0:HD],
                                               ps_v[SEQ:P, :].rearrange("p (b h d) -> p b h d", b=2, d=HD))
                    else:
                        for half in range(2):
                            r = slice(64 * half, 64 * half + 64)
                            dst = vbd[o][r, :, :, (HD + 1) * half:(HD + 1) * half + HD]
                            v = ps_v[r, :].rearrange("p (b c g d) -> p b c g d", b=2, g=2, d=HD)[:, :, :, half, :]
                            if a == SELF:
                                last = dve.tensor_copy(dst, v)
                            else:
                                for b in range(2):
                                    bv = bcast[r, a, :].rearrange("p (c g d) -> p c g d", g=2, d=HD)[:, :, half, :]
                                    last = dve.tensor_tensor(dst[:, b, :, :], v[:, b, :, :], bv, ALU.add)
                    last.then_inc(S["a_v"], 1)

                def residual(p):
                    dve.wait_ge(S["a_y"], V(a, p))
                    tile = src[:, bass.ds(p, 1), :].rearrange("p o d -> p (o d)")
                    dve.tensor_tensor(tile, bankB[:, 384:512], tile, ALU.add).then_inc(S["a_res"], 1)

                def body(n, c, p, nn, par):
                    if c is not None:
                        softmax_head(c, par)
                    if p is not None:
                        out_norm(p)
                    if nn is not None:
                        stats(nn, par)
                    if n is not None:
                        value_slot(n, 1 - par)
                    if p is not None:
                        residual(p)
                    if nn is not None:
                        normal(nn, par)
                attention_tiles(a, dve, body)
                dve.wait_ge(S["a_res"], TILES * (a + 1))

            def norm(k, src, dst):
                for t in range(TILES):
                    last = dve.bn_stats(stat8[:, t, :], src[:, t, :])
                link(last, "n_stat", k + 1)
                dve.nop(nofuse=True)
                for t in range(TILES):
                    last = dve.bn_aggr(mv8[:, t, :], stat8[:, t, :])
                last.then_inc(S["n_mv"], 1)
                dve.wait_ge(S["n_rstd"], k + 1)
                for t in range(TILES):
                    last = dve.tensor_scalar(dst[:, t, :], src[:, t, :], mv8[:, t, 0:1], rstd8[:, t:t + 1], ALU.subtract, ALU.mult)
                return last

            def gate(m, e, bias, ranked=False):
                full = [P, TILES, e]
                lg, two, key, sel, ex, cb = (v[:, :, 0:e] for v in (g_log, g_two, g_key, g_sel, g_exp, comb))
                n = [0]

                def chain(ins):
                    n[0] += 1
                    link(ins, "g_ln", GATE_LINKS * m + n[0])

                def wide(v):
                    return v[:, :, None].broadcast_to(full)

                def first_of(values, hot):
                    chain(dve.tensor_reduce(g_tmp[:], values, AX, ALU.max))
                    chain(dve.tensor_tensor(key, values, wide(g_tmp[:]), ALU.is_equal))
                    chain(dve.tensor_tensor(key, key, order[:, None, 0:e].broadcast_to(full), ALU.mult))
                    chain(dve.tensor_reduce(g_sum[:], key, AX, ALU.max))
                    chain(dve.tensor_tensor(hot, key, wide(g_sum[:]), ALU.is_equal))

                dve.wait_ge(S["g_logits"], m + 1)
                lp = ps[:, 6, 0:TILES * e].rearrange("p (t e) -> p t e", e=e)
                if bias is None:
                    chain(dve.tensor_copy(lg, lp))
                else:
                    chain(dve.tensor_tensor(lg, lp, bias.broadcast_to(full), ALU.add))
                chain(dve.tensor_reduce(g_max[:], lg, AX, ALU.max))
                dve.tensor_tensor(ex, lg, wide(g_max[:]), ALU.subtract).then_inc(S["g_sub"], 1)
                first_of(lg, sel)
                chain(dve.scalar_tensor_tensor(out=two, in0=sel, scalar=-3e38, in1=lg, op0=ALU.mult, op1=ALU.add))
                first_of(two, two)
                chain(dve.tensor_tensor(sel, sel, two, ALU.add))
                dve.wait_ge(S["g_ex"], m + 1)
                chain(dve.tensor_tensor(ex, ex, sel, ALU.mult))
                chain(dve.tensor_reduce(g_sum[:], ex, AX, ALU.add))
                chain(dve.reciprocal(g_sum[:], g_sum[:]))
                if not ranked:
                    link(dve.tensor_tensor(cb, ex, wide(g_sum[:]), ALU.mult), "g_comb", m + 1)
                else:
                    link(dve.memset(seen[:, 0, :], 0.0), "n_aff", 1)
                    for t in range(1, TILES):
                        link(dve.tensor_tensor(seen[:, t, :], seen[:, t - 1, :], g_sel[:, t - 1, :], ALU.add), "n_aff", t + 1)
                    dve.tensor_tensor(cb, ex, wide(g_sum[:]), ALU.mult).then_inc(S["g_rank"], 1)
                    dve.wait_ge(S["g_rank"], 2)
                    link(dve.tensor_scalar(key, bankA[:, 64:128].rearrange("p (t e) -> p t e", e=e), float(CAPACITY), None,
                                           ALU.is_le), "n_aff", TILES + 1)
                    link(dve.tensor_tensor(cb, cb, key, ALU.mult), "g_comb", m + 1)
                assert n[0] == GATE_LINKS

            def gated_sum(step, half, e, dst, first=False):
                dve.wait_ge(S["e_y"], step + 1)
                if not first:
                    wait(dve, "e_acc", step - 1)
                for k in range(4):
                    t = 4 * half + k
                    last = dve.scalar_tensor_tensor(out=dst[:, t, :], in0=ps[:, 4 + half, k * P:(k + 1) * P],
                                                    scalar=comb[:, t, bass.ds(e, 1)], in1=dst[:, t, :],
                                                    op0=ALU.mult, op1=ALU.add)
                last.then_inc(S["e_acc"], 1)

            attention(0)
            norm(0, x, cur).then_inc(S["n_done"], 1)
            dve.wait_ge(S["n_done"], 1)
            with dve.Fori(0, LAYERS0) as l:
                norm(l + 1, cur, xh).then_inc(S["n_done"], 1)
                gate(l, E0, rbias[:, None, bass.ds(l * E0, E0)])
                link(dve.tensor_reduce(g_tmp[:], comb[:, :, 0:E0], AX, ALU.add), "g_csum", l + 1)
                dve.wait_ge(S["g_b2"], l + 1)
                for t in range(TILES):
                    last = dve.scalar_tensor_tensor(out=cur[:, t, :], in0=cur[:, t, :], scalar=g_tmp[:, t:t + 1],
                                                    in1=ps[:, 6 + t // 4, (t % 4) * P:(t % 4 + 1) * P],
                                                    op0=ALU.mult, op1=ALU.add)
                link(last, "g_init", l + 1)
                for s in range(2 * E0):
                    gated_sum(8 * l + s, s % 2, s // 2, cur, first=(s < 2))
                dve.wait_ge(S["e_acc"], 8 * l + 8)
            dve.wait_ge(S["e_acc"], STEP_L1)
            link(dve.tensor_tensor(x[:], x[:], cur[:], ALU.add), "l0_x", 1)
            for a, m, base in ((1, 4, STEP_L1), (2, 5, STEP_L2)):
                attention(a)
                norm(m + 1, x, xh).then_inc(S["n_done"], 1)
                c0 = 16 + 8 * (m - 4)
                gate(m, E8, rbias[:, None, c0:c0 + 8], ranked=(m == 4))
                dve.wait_ge(S["g_b2"], m + 1)
                for g in range(2):
                    last = dve.tensor_tensor(x[:, 4 * g:4 * g + 4, :], ps[:, 6 + g, :].rearrange("p (t d) -> p t d", d=P),
                                             x[:, 4 * g:4 * g + 4, :], ALU.add)
                link(last, "g_init", m + 1)
                with dve.Fori(0, E8) as e:
                    for h in range(2):
                        gated_sum(base + 2 * e + h, h, e, x)
                dve.wait_ge(S["e_acc"], base + 2 * E8)
            attention(CACHE)
            norm(7, x, cur).then_inc(S["n_done"], 1)
            dve.wait_ge(S["n_done"], 8)
            attention(SELF)
            link(norm(8, cur, xh), "n_aff", TILES + 2)
            for v, op in ((5, ALU.mult), (6, ALU.add)):
                last = dve.tensor_tensor(xh[:], xh[:], bcast[:, v:v + 1, :].broadcast_to([P, TILES, P]), op)
                if v == 5:
                    link(last, "n_aff", TILES + 3)
            last.then_inc(S["n_done"], 1)
            gate(6, E8, None)
            for s in range(2):
                for c in range(CH):
                    k = 4 * s + c
                    dve.wait_ge(S["l3_h_sb"], k + 1)
                    dve.wait_ge(S["l3_gate"], k + 1)
                    dve.tensor_tensor(hs[s][:, c, :], ps[:, 4 + k % 2, :], hs[s][:, c, :], ALU.mult).then_inc(S["l3_gated"], 1)
                dve.wait_ge(S["l3_res"], 1)
                dve.wait_ge(S["l3_y"], s + 1)
                dve.tensor_tensor(x[:, 4 * s:4 * s + 4, :], ps[:, 6 + s, :].rearrange("p (t d) -> p t d", d=P),
                                  x[:, 4 * s:4 * s + 4, :], ALU.add).then_inc(S["l3_x"], 1)


BIAS_LOADS = 5 + 6 + 1 + 3 + 4 + 4 + 3 + 4 + 3
GATE_LINKS = 17


def kernel(**inputs):
    import numpy as _np
    import concourse.bacc as _bacc
    from concourse import mybir as _mybir
    from concourse.bass_utils import run_bass_kernel_spmd as _run

    nc = _bacc.Bacc("TRN2", target_bir_lowering=False, num_devices=1)
    arrays, aps = {}, {}
    for name, value in inputs.items():
        a = _np.ascontiguousarray(value)
        arrays[f"in_{name}_dram"] = a
        aps[name] = nc.dram_tensor(f"in_{name}_dram", a.shape, _mybir.dt.from_np(a.dtype), kind="ExternalInput").ap()
    shape = tuple(inputs["x"].shape)
    o = nc.dram_tensor("out_0_dram", shape, _mybir.dt.from_np(_np.dtype("float32")), kind="ExternalOutput").ap()
    build(nc, aps, o)
    r = _run(nc, [arrays], core_ids=[0])
    return r.results[0]["out_0_dram"]
```

```python
from contextlib import ExitStack

import concourse.bass as bass
from concourse import mybir

F32 = mybir.dt.float32
I32 = mybir.dt.int32
ALU = mybir.AluOpType
ACT = mybir.ActivationFunctionType
AX = mybir.AxisListType.X

P = 128
BATCH, SEQ = 16, 64
TILES = BATCH * SEQ // P
HEADS, HD = 16, 8
FF = 512
CH = FF // P
EPS = 1e-5
SCALE = HD ** -0.5
NEG_MASK = -1e9 / SCALE
NEG_CACHE = -1e30 / SCALE
CAPACITY = int(1.25 * BATCH * SEQ / 8)
LAYERS0, E0, E8 = 4, 4, 8

CACHE, SELF = 3, 4
SCORES_FIRST = CACHE
GROUPS = [2, 2, 2, 4, 2]
GROUP_BASE = [TILES * sum(GROUPS[:a]) for a in range(5)]
B1_L0, LNG_L0, LNB_L0, B1_L1 = 0, 64, 80, 96
B1_L2, BQ, BK, BV = 128, 160, 166, 172
STEP_L1 = 2 * LAYERS0 * E0
STEP_L2 = STEP_L1 + 2 * E8


def build(nc, A, out):
    with ExitStack() as ctx:
        def sb(name, shape, dt=F32):
            return ctx.enter_context(nc.sbuf_tensor(name, shape, dt))

        def sem(name):
            return ctx.enter_context(nc.semaphore(name))

        x = sb("x", [P, TILES, P])
        cur = sb("cur", [P, TILES, P])
        xh = sb("xh", [P, TILES, P])
        curT = sb("curT", [P, TILES * P])
        xhT = sb("xhT", [P, TILES * P])
        xe = [sb(f"xe{i}", [P, TILES * P]) for i in range(2)]
        hs = [sb(f"hs{i}", [P, CH, 512]) for i in range(2)]
        w1s = [sb(f"w1s{i}", [P, FF]) for i in range(2)]
        w2s = [sb(f"w2s{i}", [P, CH, P]) for i in range(2)]
        ctx_tok = sb("ctx_tok", [P, TILES, P])
        ctxT = sb("ctxT", [P, TILES * P])
        keys_all = sb("keys_all", [P, 2, TILES * SEQ])
        cacheV = sb("cacheV", [SEQ, BATCH, P])
        nat = sb("nat", [P, 12, P])
        wat = sb("wat", [P, 20, P])
        rows8 = sb("rows8", [P, 3, HD])
        bt_rows = sb("bt_rows", [P, 2, P])
        bt = sb("bt", [P, 256])
        bcast = sb("bcast", [P, 4, P])
        bo = sb("bo", [1, 4, P])
        out_bias = sb("out_bias", [P, 4, P])
        bv_wide = sb("bv_wide", [P, 3, P])
        rbias = sb("rbias", [P, 4 * E0 + 2 * E8])
        rw = sb("rw", [P, 4 * E0 + 3 * E8])
        b2_l0 = sb("b2_l0", [E0, LAYERS0, P])
        b2_l12 = sb("b2_l12", [E8, 2, P])
        w1c = sb("w1c", [P, E8, FF // E8])
        w2c = sb("w2c", [P, CH, P])
        esel = sb("esel", [E8, E8, FF // E8])
        ident = sb("ident", [P, P])
        ones = sb("ones", [P, P])
        tri = sb("tri", [P, P])
        m16 = sb("m16", [P, HEADS])
        m8 = sb("m8", [P, HEADS // 2])
        epow = sb("epow", [P, 2 * TILES])
        lay_gb = sb("lay_gb", [P, 2, E0])
        lay_b1 = sb("lay_b1", [P, E0 * CH])
        order = sb("order", [P, E8])
        neg = sb("neg", [P, 2])
        iota_k = sb("iota_k", [P, SEQ])
        iota_p = sb("iota_p", [P, 1])
        len_i = sb("len_i", [P, BATCH], I32)
        len_f = sb("len_f", [P, BATCH])
        len_max = sb("len_max", [P, 1])
        len_half = sb("len_half", [P, TILES])
        past_k = sb("past_k", [P, TILES, SEQ])
        past_v = sb("past_v", [P, BATCH])
        kill_cache = sb("kill_cache", [P, SEQ], I32)
        mask = sb("mask", [P, TILES, SEQ], I32)
        kill = [sb(f"kill{i}", [P, SEQ], I32) for i in range(2)]
        xn = [sb(f"xn{i}", [P, P]) for i in range(2)]
        stat = [sb(f"stat{i}", [P, 6]) for i in range(2)]
        mv = [sb(f"mv{i}", [P, 2]) for i in range(2)]
        ve = [sb(f"ve{i}", [P, 1]) for i in range(2)]
        rstd = [sb(f"rstd{i}", [P, 1]) for i in range(2)]
        xnT = [sb(f"xnT{i}", [P, 2, 2, SEQ]) for i in range(2)]
        qT = [sb(f"qT{i}", [P, 2, P]) for i in range(2)]
        kT = [sb(f"kT{i}", [P, 2, SEQ]) for i in range(2)]
        kbd = [sb(f"kbd{i}", [P, HEADS * P]) for i in range(2)]
        values_all = sb("values_all", [P, BATCH, HEADS // 2, 2 * (HD + 1)])
        vbd = [sb(f"vbd{i}", [P, 2, HEADS // 2, 2 * (HD + 1)]) for i in range(2)]
        vca = [sb(f"vca{i}", [P, 2, HEADS, HD + 1]) for i in range(2)]
        prob = [sb(f"prob{i}", [P, HEADS * P]) for i in range(2)]
        probT = sb("probT", [P, HEADS, P])
        smax = sb("smax", [P, HEADS])
        rsum = sb("rsum", [P, HEADS])
        on = sb("on", [P, HEADS, HD])
        oT = sb("oT", [P, P])
        stat8 = sb("stat8", [P, TILES, 6])
        mv8 = sb("mv8", [P, TILES, 2])
        ve8 = sb("ve8", [P, TILES])
        rstd8 = sb("rstd8", [P, TILES])
        g_log = sb("g_log", [P, TILES, E8])
        g_two = sb("g_two", [P, TILES, E8])
        g_key = sb("g_key", [P, TILES, E8])
        g_sel = sb("g_sel", [P, TILES, E8])
        g_exp = sb("g_exp", [P, TILES, E8])
        g_max = sb("g_max", [P, TILES])
        g_tmp = sb("g_tmp", [P, TILES])
        g_sum = sb("g_sum", [P, TILES])
        seen = sb("seen", [P, TILES, E8])
        comb = sb("comb", [P, TILES, E8])
        combT = sb("combT", [E8, TILES * P])

        ps = ctx.enter_context(nc.psum_tensor("ps", [P, 8, 512], F32))
        hid = [ps[:, c, :] for c in range(4)]
        bankA, bankB = ps[:, 6, :], ps[:, 7, :]

        names = """in_x in_ctx in_w0 in_tab in_bo in_len in_wt in_bias in_w2nd in_mask in_w1a in_w1b in_w2a in_w2b
            c_rows c_id0 c_id c_pool c_dve c_bd c_past c_cache c_wT c_w_sb c_bvw c_bT c_b_sb c_cT c_c_sb
            a_stat a_mv a_ve a_rstd a_xn a_xT a_xT_sb a_qk a_qk_sb a_kv a_kbd a_vpast a_v a_s a_kill a_masked a_max a_sub a_exp
            a_pT a_pT_sb a_o a_rs a_on a_oT a_oT_sb a_y a_res a_aff
            n_stat n_mv n_ve n_rstd n_aff n_done n_T n_T_sb g_logits g_ln g_sub g_ex g_comb g_rank g_cT g_cT_sb g_b2 g_init
            k_ps k_sb v_ps v_sb a_vb ob_ps ob_sb a_vm a_bo e_xe e_h e_h_sb e_y e_acc l0_x l3_res l3_gate l3_gated l3_h l3_h_sb l3_y l3_x stored""".split()
        names += ["in_cv", 'g_csum', 'lay_pool', 'lay_act']
        S = {n: sem(n) for n in names}
        block = ctx.enter_context(nc.Block())

        def shape(a):
            return (4, 4, P) if a == CACHE else (2, 8, SEQ)

        def sview(a, par):
            n, j, k = shape(a)
            b0 = 0 if a == CACHE else 2 * par
            return ps[:, b0:b0 + n, :].rearrange("p i (j k) -> p i j k", k=k)

        tile_values = bankA[:, 2 * P:4 * P]

        def pview(a, par):
            n, j, k = shape(a)
            return prob[par][:, 0:HEADS * k].rearrange("p (i j k) -> p i j k", i=n, k=k)

        def kview(a, par):
            k = shape(a)[2]
            return kbd[par][:, 0:HEADS * k].rearrange("p (s j k) -> p s j k", s=2, k=k)

        def attention_tiles(a, eng, body):
            def at(t):
                ok = [t + d if 0 <= t + d < TILES else None for d in (2, 1, 0, -1, 3)]
                body(*ok, t % 2)
            for t in range(-3, 1):
                at(t)
            with eng.Fori(0, 2) as pair:
                t = 2 * pair + 1
                body(t + 2, t + 1, t, t - 1, t + 3, 1)
                body(t + 3, t + 2, t + 1, t, t + 4, 0)
            for t in range(5, TILES + 1):
                at(t)

        def V(a, t):
            return TILES * a + t + 1

        def W(a, t, half=1):
            if a == CACHE:
                return TILES * a + 2 * t + half + 1
            return TILES * (a + (a > CACHE)) + t + 1

        def halves(a):
            return [(0, slice(0, 2)), (1, slice(2, 4))] if a == CACHE else [(1, slice(0, 2))]

        def wait(eng, name, value):
            if not isinstance(value, int) or value > 0:
                eng.wait_ge(S[name], value)

        @block.sync
        def _(sp):
            sp.dma_start(ctx_tok[:], A["ctx_1024"].rearrange("b s d -> (b s) d").rearrange("(t p) d -> p t d", p=P)).then_inc(S["in_ctx"], 16)
            for slot, n in enumerate(("wq", "wk", "wv", "wo")):
                sp.dma_start(nat[:, slot, :], A[f"L0_xattn_{n}"]).then_inc(S["in_w0"], 16)
            sp.wait_ge(S["c_rows"], 1)
            sp.dma_start(bt_rows[0:32, 1, :], A["L2_ffn_b1"].rearrange("e (c f) -> (e c) f", f=P)).then_inc(S["in_tab"], 16)
            sp.dma_start(x[:], A["x"].rearrange("b s d -> (b s) d").rearrange("(t p) d -> p t d", p=P)).then_inc(S["in_x"], 16)

            sp.dma_start(len_i[:], A["_lenS2"].partition_broadcast(P)).then_inc(S["in_len"], 16)
            small = [(rbias[:, 0:16], A["L0_ffn_router_b"].rearrange("l e -> (l e)").partition_broadcast(P)),
                     (rw[:, 0:16].rearrange("p (l e) -> p l e", e=E0), A["L0_ffn_router_w"].rearrange("l h e -> h l e")),
                     (b2_l0[:], A["L0_ffn_b2"].rearrange("l e h -> e l h")),
                     (rbias[:, 16:24], A["L1_ffn_gate_b"].partition_broadcast(P)),
                     (rbias[:, 24:32], A["L2_ffn_br"].partition_broadcast(P)),
                     (rw[:, 16:24], A["L1_ffn_gate_w"]), (rw[:, 24:32], A["L2_ffn_Wr"]), (rw[:, 32:40], A["L3_ffn_Wg"]),
                     (b2_l12[:, 0, :], A["L1_ffn_b2"]), (b2_l12[:, 1, :], A["L2_ffn_b2"])]
            small += [(bcast[:, n, :], A[f"L3_ffn_{v}"].partition_broadcast(P)) for n, v in enumerate(("g1", "b1", "g2", "b2"))]
            small += [(bt_rows[0:64, 0, :], A["L0_ffn_b1"].rearrange("l e (c f) -> (l e c) f", f=P)),
                      (bt_rows[64:80, 0, :], A["L0_ffn_ln_g"].rearrange("l e h -> (l e) h")),
                      (bt_rows[80:96, 0, :], A["L0_ffn_ln_b"].rearrange("l e h -> (l e) h")),
                      (bt_rows[96:128, 0, :], A["L1_ffn_b1"].rearrange("e (c f) -> (e c) f", f=P))]
            assert len(small) == SMALL_LOADS
            for dst, src in small:
                sp.dma_start(dst, src).then_inc(S["in_bias"], 16)
            slots = [("L2_xattn_wo", 7), ("L3_xattn_wq", 8), ("L3_xattn_wk", 9), ("L3_xattn_wv", 10), ("L3_xattn_wo", 11)]
            for n, slot in slots:
                sp.dma_start(nat[:, slot, :], A[n]).then_inc(S["in_wt"], 16)
            for n, v in enumerate(("wq", "wk", "wv")):
                sp.dma_start(rows8[:, n, :], A[f"L2_xattn_{v}"].rearrange("h e d -> (h e) d")).then_inc(S["in_wt"], 16)
            for n, v in enumerate(("Wq", "Wk", "Wv", "Wo")):
                sp.dma_start(wat[:, 4 + n, :], A[f"L1_xattn_{v}"]).then_inc(S["in_wt"], 16)
                sp.dma_start(wat[:, 16 + n, :], A[f"L3_ffn_{v}"]).then_inc(S["in_wt"], 16)
            sp.dma_start(mask[:], A["mask_BxSxS2_ik0"].rearrange("b q k -> (b q) k").rearrange("(t p) k -> p t k", p=P)).then_inc(S["in_mask"], 16)
            w1_0, w2_0 = A["L0_ffn_w1"].rearrange("l e h f -> (l e) h f"), A["L0_ffn_w2"].rearrange("l e (c f) h -> (l e) f c h", f=P)
            done = 0
            for w1, w2, count in ((w1_0, w2_0, LAYERS0 * E0),
                                  (A["L1_ffn_w1"], A["L1_ffn_w2"].rearrange("e (c f) h -> e f c h", f=P), E8),
                                  (A["L2_ffn_W1"], A["L2_ffn_W2"].rearrange("e (c f) h -> e f c h", f=P), E8)):
                def pair(e, free):
                    for i in range(2):
                        if free is not None:
                            sp.wait_ge(S["e_y"], free + 2 * i)
                        n = "ab"[i]
                        sp.dma_start(w1s[i][:], w1[bass.ds(e + i, 1), :, :].rearrange("o h f -> (o h) f")).then_inc(S["in_w1" + n], 16)
                        sp.dma_start(w2s[i][:], w2[bass.ds(e + i, 1), :, :, :].rearrange("o f c h -> (o f) c h")).then_inc(S["in_w2" + n], 16)
                if done == 0:
                    pair(0, None)
                    with sp.Fori(1, count // 2) as e:
                        pair(2 * e, 4 * e - 2)
                else:
                    with sp.Fori(0, count // 2) as e:
                        pair(2 * e, 4 * e + 2 * done - 2)
                done += count
                if count == LAYERS0 * E0:
                    sp.dma_start(w1c[:], A["L3_ffn_W1"].rearrange("e h f -> h e f")).then_inc(S["in_w2nd"], 16)
                    sp.dma_start(w2c[:], A["L3_ffn_W2"].rearrange("(c g) f h -> (g f) c h", c=CH)).then_inc(S["in_w2nd"], 16)
            dst = out.rearrange("b s d -> (b s) d").rearrange("(t p) d -> p t d", p=P)
            for h in range(2):
                sp.wait_ge(S["l3_x"], h + 1)
                sp.dma_start(dst[:, 4 * h:4 * h + 4, :], x[:, 4 * h:4 * h + 4, :]).then_inc(S["stored"], 16)
            sp.wait_ge(S["stored"], 32)

        @block.gpsimd
        def _(pool):
            pool.memset(bt_rows[:], 0.0).then_inc(S["c_rows"], 1)
            pool.memset(ident[:], 0.0).then_inc(S["c_id0"], 1)
            pool.memset(ones[:], 1.0).then_inc(S["c_id0"], 1)
            pool.memset(m16[:], 1.0).then_inc(S["c_id0"], 1)
            pool.memset(esel[:], 1.0).then_inc(S["c_id0"], 1)
            for i in range(2):
                pool.memset(qT[i][:], 0.0).then_inc(S["c_id0"], 1)
            pool.wait_ge(S["c_id0"], 6)
            pool.affine_select(out=ident[:], in_=ident[:], compare_op=ALU.not_equal, fill=1.0, base=0,
                               pattern=[[-1, P]], channel_multiplier=1).then_inc(S["c_id"], 1)
            pool.affine_select(out=m16[:], in_=m16[:], compare_op=ALU.is_ge, fill=0.0, base=0,
                               pattern=[[-HD, HEADS]], channel_multiplier=1).then_inc(S["c_id"], 1)
            pool.wait_ge(S["c_id"], 2)
            pool.affine_select(out=m16[:], in_=m16[:], compare_op=ALU.is_ge, fill=0.0, base=HD - 1,
                               pattern=[[HD, HEADS]], channel_multiplier=-1).then_inc(S["c_id"], 1)

            for l in range(4):
                pool.dma_start(bo[:, l, :], A[f"L{l}_xattn_bo"].rearrange("(a n) -> a n", a=1)).then_inc(S["in_bo"], 16)
            pool.dma_start(cacheV[:], A["ctx_1024"].rearrange("b s d -> s b d")).then_inc(S["in_cv"], 16)

            pool.affine_select(out=tri[:], in_=ones[:], compare_op=ALU.is_ge, fill=0.0, base=0,
                               pattern=[[1, P]], channel_multiplier=-1).then_inc(S["c_pool"], 1)
            pool.affine_select(out=esel[:], in_=esel[:], compare_op=ALU.is_equal, fill=0.0, base=0,
                               pattern=[[-1, E8], [0, FF // E8]], channel_multiplier=1).then_inc(S["c_pool"], 1)
            pool.memset(epow[:, 0:TILES], -0.5).then_inc(S["c_pool"], 1)
            pool.memset(epow[:, TILES:2 * TILES], EPS).then_inc(S["c_pool"], 1)
            pool.memset(neg[:, 0:1], NEG_MASK).then_inc(S["c_pool"], 1)
            pool.memset(neg[:, 1:2], NEG_CACHE).then_inc(S["c_pool"], 1)
            pool.iota(order[:], pattern=[[-1, E8]], base=E8, channel_multiplier=0,
                      allow_small_or_imprecise_dtypes=True).then_inc(S["c_pool"], 1)
            pool.iota(iota_k[:], pattern=[[1, SEQ]], base=0, channel_multiplier=0,
                      allow_small_or_imprecise_dtypes=True).then_inc(S["c_pool"], 1)
            pool.iota(iota_p[:], pattern=[[0, 1]], base=0, channel_multiplier=1,
                      allow_small_or_imprecise_dtypes=True).then_inc(S["c_pool"], 1)
            for i in range(2):
                pool.memset(vca[i][:], 1.0).then_inc(S["c_pool"], 1)
            pool.memset(values_all[:], 0.0).then_inc(S["c_pool"], 1)
            pool.wait_ge(S["c_pool"], 12)
            pool.memset(values_all[0:SEQ, :, :, HD:HD + 1], 1.0).then_inc(S["c_pool"], 1)
            pool.memset(values_all[SEQ:P, :, :, 2 * HD + 1:2 * HD + 2], 1.0).then_inc(S["c_pool"], 1)
            pool.wait_ge(S["c_pool"], 14)
            pool.wait_ge(S["c_b_sb"], 1)
            pool.tensor_copy(bv_wide[:], bt[:, BV:BV + 3, None].broadcast_to([P, 3, P])).then_inc(S["c_bvw"], 1)
            pool.wait_ge(S["c_dve"], 1)

            def mult(o, a, b):
                return pool.tensor_tensor(o, a, b, ALU.mult)

            def power(v, s, e, n, name, val):
                pool.wait_ge(S[name + "mv"], val)
                pool.tensor_tensor(e, v, epow[:, TILES:TILES + n], ALU.add).then_inc(S[name + "ve"], 1)
                pool.wait_ge(S[name + "ve"], val)
                pool.tensor_tensor(s, e, epow[:, 0:n], ALU.pow).then_inc(S[name + "rstd"], 1)

            def attention(a):
                def body(f, s, c, p, nn, par):
                    if f is not None:
                        wait(pool, "a_s", W(a, f) - (4 if a == CACHE else 2))
                        if isinstance(f, int) and f == 0:
                            if a < CACHE:
                                pool.wait_ge(S["k_sb"], 2 * (a + 1))
                            if a < SELF:
                                pool.wait_ge(S["ob_sb"], a + 1)
                        kv, full = kview(a, par), [P, 2, HEADS // 2, SEQ]
                        hm = m8[:, None, :, None].broadcast_to(full)
                        if a <= CACHE:
                            old = keys_all[:, :, bass.ds(f * SEQ, SEQ)]
                            last = mult(kv[:, :, :, 0:SEQ], old[:, :, None, :].broadcast_to(full), hm)
                        if a < CACHE:
                            last.then_inc(S["a_kbd"], 1)
                        if a != SELF:
                            pool.wait_ge(S["a_xn"], V(a, f))
                            tile = x[:, bass.ds(f, 1), :]
                            pool.tensor_tensor(tile, tile, out_bias[:, a:a + 1, :], ALU.add).then_inc(S["a_bo"], 1)
                    if nn is not None:
                        o = 1 - par
                        power(mv[o][:, 1:2], rstd[o][:], ve[o][:], 1, "a_", V(a, nn))
                    if f is not None and a >= CACHE:
                        pool.wait_ge(S["a_qk_sb"], V(a, f))
                        k0 = SEQ if a == CACHE else 0
                        mult(kv[:, :, :, k0:k0 + SEQ], kT[par][:, :, None, :].broadcast_to(full), hm).then_inc(S["a_kbd"], 1)
                    if c is not None and a < CACHE:
                        wait(pool, "a_o", V(a, c) - 2)
                        pool.nop(nofuse=True)
                        pool.tensor_copy(vbd[par][:], values_all[:, bass.ds(c * 2, 2), :, :]).then_inc(S["a_vb"], 1)
                    if c is not None and a == CACHE:
                        wait(pool, "a_o", V(a, c) - 2)
                        pool.nop(nofuse=True)
                        pool.tensor_copy(vca[par][0:SEQ, :, :, 0:HD],
                                         cacheV[:, bass.ds(c * 2, 2), :].rearrange("k b (h d) -> k b h d", d=HD)
                                         ).then_inc(S["a_vpast"], 1)
                attention_tiles(a, pool, body)

            def norm(k):
                power(mv8[:, :, 1], rstd8[:], ve8[:], TILES, "n_", k + 1)

            attention(0)
            pool.wait_ge(S["in_wt"], 16 * WEIGHT_LOADS)
            for n in range(3):
                mult(nat[:, 4 + n, :].rearrange("p (h d) -> p h d", d=HD), rows8[:, n:n + 1, :].broadcast_to([P, HEADS, HD]),
                     m16[:, :, None].broadcast_to([P, HEADS, HD])).then_inc(S["c_bd"], 1)
            norm(0)
            with pool.Fori(0, LAYERS0) as l:
                norm(l + 1)
                pool.wait_ge(S["c_b_sb"], 2)
                pool.tensor_copy(lay_gb[:], bt[:, LNG_L0:LNB_L0 + 16].rearrange("p (w l e) -> p w l e", w=2, e=E0)[:, :, bass.ds(l, 1), :]
                                 .rearrange("p w o e -> p w (o e)")).then_inc(S["lay_pool"], 1)
                pool.wait_ge(S["lay_pool"], l + 1)
                pool.wait_ge(S["n_T_sb"], 4 * l + 4)
                for e in range(E0):
                    g = l * E0 + e
                    if e >= 2:
                        pool.wait_ge(S["e_h"], 8 * (g - 2) + 8)
                    pool.nop(nofuse=True)
                    pool.tensor_scalar(xe[e % 2][:], xhT[:], lay_gb[:, 0, e:e + 1], lay_gb[:, 1, e:e + 1],
                                       ALU.mult, ALU.add).then_inc(S["e_xe"], 1)
            attention(1)
            norm(5)
            attention(2)
            norm(6)
            pool.wait_ge(S["c_past"], 4)
            pool.wait_ge(S["k_sb"], 8)
            for s in range(2):
                mult(keys_all[:, s], keys_all[:, s], past_k[:].rearrange("p t k -> p (t k)")).then_inc(S["c_cache"], 1)
            pool.wait_ge(S["in_cv"], 16)
            mult(cacheV[:], cacheV[:], past_v[0:SEQ, :, None].broadcast_to([SEQ, BATCH, P])).then_inc(S["c_cache"], 1)
            pool.wait_ge(S["c_cache"], 3)
            attention(CACHE)
            norm(7)
            attention(SELF)
            norm(8)
            pool.wait_ge(S["a_res"], TILES * 5)
            pool.tensor_tensor(x[:], x[:], cur[:], ALU.add).then_inc(S["l3_res"], 1)

        @block.scalar
        def _(act):
            def copy(o, i):
                return act.activation(o, i, ACT.Copy)

            def ld(dst, src, s):
                act.dma_start(dst, src).then_inc(S[s], 16)

            act.wait_ge(S["c_rows"], 1)
            for n, v in enumerate(("bq", "bk")):
                for a, w in enumerate((A[f"L0_xattn_{v}"], A[f"L1_xattn_{v}"], A[f"L2_xattn_{v}"].rearrange("h e -> (h e)"))):
                    row0 = BQ - 128 + 6 * n + 2 * a
                    ld(bt_rows[row0:row0 + 2, 1, :].rearrange("p (half d) -> p half d", half=2),
                       w.rearrange("(s d) -> s d", s=2)[:, None, :].broadcast_to([2, 2, SEQ]), "in_tab")
            for a, w in enumerate((A["L0_xattn_bv"], A["L1_xattn_bv"], A["L2_xattn_bv"].rearrange("h e -> (h e)"))):
                ld(bt_rows[BV - 128 + a:BV - 127 + a, 1, :], w.rearrange("(a n) -> a n", a=1), "in_tab")
            for g in range(2):
                act.wait_ge(S["c_cT"], g + 1)
                copy(ctxT[:, 512 * g:512 * g + 512], ps[:, 5 + g, :]).then_inc(S["c_c_sb"], 1)

            def weights(g):
                act.wait_ge(S["c_wT"], g + 1)
                slot = [0, 8, 12][g]
                copy(wat[:, slot:slot + 4, :], (bankB if g else ps[:, 0, :]).rearrange("p (m n) -> p m n", n=P)
                     ).then_inc(S["c_w_sb"], 1)

            def context(a):
                if a == 0:
                    act.wait_ge(S["c_bT"], 1)
                    copy(bt[:, P:2 * P], bankB[:, 0:P]).then_inc(S["c_b_sb"], 1)
                    act.wait_ge(S["c_b_sb"], 1)
                act.wait_ge(S["k_ps"], a + 1)
                for s in range(2):
                    if a == CACHE:
                        copy(keys_all[:, s], ps[:, 4 + s, :]).then_inc(S["k_sb"], 1)
                    else:
                        act.activation(keys_all[:, s], ps[:, 4 + s, :], ACT.Identity,
                                       bias=bt[:, BK + 2 * a + s:BK + 2 * a + s + 1]).then_inc(S["k_sb"], 1)
                if a < CACHE:
                    for g in range(4):
                        act.wait_ge(S["v_ps"], 4 * a + g + 1)
                        for half in range(2):
                            r = slice(64 * half, 64 * half + 64)
                            v = ps[r, g, :].rearrange("p (b c g d) -> p b c g d", b=4, g=2, d=HD)[:, :, :, half, :]
                            last = copy(values_all[r, 4 * g:4 * g + 4, :, (HD + 1) * half:(HD + 1) * half + HD], v)
                        last.then_inc(S["v_sb"], 1)
                act.wait_ge(S["ob_ps"], a + 1)
                copy(out_bias[:, a, :], bankA[:, 0:P]).then_inc(S["ob_sb"], 1)
                if a == 1:
                    copy(bt[:, 0:P], bankA[:, P:2 * P]).then_inc(S["c_b_sb"], 1)

            weights(0)
            act.wait_ge(S["c_pool"], 14)
            context(0)

            def attention(a):
                def body(f, s, c, p, nn, par):
                    if f is not None:
                        wait(act, "a_s", W(a, f) - (4 if a == CACHE else 2))
                        act.wait_ge(S["a_xT"], V(a, f))
                        turned = bankA[:, 0:P].rearrange("p (b k) -> p b k", b=2)
                        if a == SELF:
                            copy(xnT[par][:], turned[:, :, None, :].broadcast_to([P, 2, 2, SEQ])).then_inc(S["a_xT_sb"], 1)
                        else:
                            copy(xnT[par][:, :, 0, :], turned).then_inc(S["a_xT_sb"], 1)
                    if c is not None:
                        for half, banks in halves(a):
                            act.wait_ge(S["a_sub"], W(a, c, half))
                            pv = pview(a, par)[:, banks]
                            act.activation(pv, pv, ACT.Exp, scale=SCALE).then_inc(S["a_exp"], 1)
                    if f is not None:
                        if a >= CACHE:
                            wait(act, "a_kbd", V(a, f) - 2)
                        act.wait_ge(S["a_qk"], V(a, f))
                        q = bankA[:, 0:P].rearrange("p (s k) -> p s k", s=2)
                        for b in range(2):
                            r = slice(64 * b, 64 * b + 64)
                            if a < CACHE:
                                for s in range(2):
                                    last = act.activation(qT[par][r, s, r], q[r, s, :], ACT.Identity,
                                                          bias=bt[r, BQ + 2 * a + s:BQ + 2 * a + s + 1])
                            else:
                                copy(qT[par][r, :, r], q[r, :, :])
                        if a >= CACHE:
                            last = copy(kT[par][:], bankA[:, P:2 * P].rearrange("p (s k) -> p s k", s=2))
                        last.then_inc(S["a_qk_sb"], 1)
                    if s is not None and a >= CACHE:
                        act.wait_ge(S["a_vm"], TILES * (a - CACHE) + s + 1)
                        wait(act, "a_o", V(a, s) - 2)
                        o = 1 - par
                        if a == CACHE:
                            last = copy(vca[o][SEQ:P, :, :, 0:HD],
                                        tile_values[SEQ:P, :].rearrange("p (b h d) -> p b h d", b=2, d=HD))
                        else:
                            for half in range(2):
                                r = slice(64 * half, 64 * half + 64)
                                last = copy(vbd[o][r, :, :, (HD + 1) * half:(HD + 1) * half + HD],
                                            tile_values[r, :].rearrange("p (b c g d) -> p b c g d", b=2, g=2, d=HD)
                                            [:, :, :, half, :])
                        last.then_inc(S["a_v"], 1)

                    def turned_probs(q):
                        act.wait_ge(S["a_pT"], GROUP_BASE[a] + GROUPS[a] * c + q + 1)
                        copy(probT[:, 4 * q:4 * q + 4, :], ps[:, 4 + q % 2, :].rearrange("p (c n) -> p c n", n=P)
                             ).then_inc(S["a_pT_sb"], 1)
                    def turned_out():
                        if p is not None:
                            act.wait_ge(S["a_oT"], V(a, p))
                            copy(oT[:], bankB[:, 256:384]).then_inc(S["a_oT_sb"], 1)
                    if a == CACHE:
                        turned_out()
                    if c is not None:
                        wait(act, "a_o", V(a, c) - 1)
                        turned_probs(0)
                    if a != CACHE:
                        turned_out()
                    if c is not None:
                        for q in range(1, GROUPS[a]):
                            turned_probs(q)
                attention_tiles(a, act, body)

            def transposed(call, dst):
                for g in range(2):
                    act.wait_ge(S["n_T"], 2 * call + g + 1)
                    copy(dst[:, 512 * g:512 * g + 512], ps[:, 6 + g, :]).then_inc(S["n_T_sb"], 1)

            def gates(m, e):
                act.wait_ge(S["g_sub"], m + 1)
                act.activation(g_exp[:, :, 0:e], g_exp[:, :, 0:e], ACT.Exp).then_inc(S["g_ex"], 1)

            def gates_T(m, e):
                for g in range(2):
                    act.wait_ge(S["g_cT"], 2 * m + g + 1)
                    copy(combT[0:e, 512 * g:512 * g + 512], ps[0:e, 6 + g, :]).then_inc(S["g_cT_sb"], 1)

            def hidden(step, parity, col, func, first=False):
                if not first:
                    wait(act, "e_y", step - 1)
                for c in range(CH):
                    act.wait_ge(S["e_h"], 4 * step + c + 1)
                    act.activation(hs[parity][:, c, :], hid[c], func, bias=lay_b1[:, col + c:col + c + 1]).then_inc(S["e_h_sb"], 1)

            def biases(col, n, count, used=None):
                if used is not None:
                    act.wait_ge(S["e_h_sb"], used)
                    act.nop(nofuse=True)
                act.activation(lay_b1[:, 0:n], bt[:, bass.ds(col, n)], ACT.Copy).then_inc(S["lay_act"], 1)
                act.wait_ge(S["lay_act"], count)

            attention(0)
            context(1)
            weights(1)
            act.wait_ge(S["c_b_sb"], 2)
            with act.Fori(0, LAYERS0) as l:
                transposed(2 * l, curT)
                transposed(2 * l + 1, xhT)
                biases(B1_L0 + 16 * l, 16, l + 1)
                gates(l, E0)
                for s in range(2 * E0):
                    hidden(8 * l + s, s % 2, s // 2 * CH, ACT.Gelu, first=(s < 2))
                    if s == 0:
                        gates_T(l, E0)
            for a, m, base, table in ((1, 4, STEP_L1, B1_L1), (2, 5, STEP_L2, B1_L2)):
                attention(a)
                context(a + 1)
                if a == 1:
                    weights(2)
                transposed(m + 4, xhT)
                gates(m, E8)
                laid = LAYERS0 + E8 * (m - 4) + 1
                biases(table, CH, laid, CH * base)
                hidden(base, 0, 0, ACT.Relu)
                gates_T(m, E8)
                hidden(base + 1, 1, 0, ACT.Relu)
                with act.Fori(1, E8) as e:
                    biases(table + CH * e, CH, laid + e, CH * (base + 2 * e))
                    for h in range(2):
                        hidden(base + 2 * e + h, h, 0, ACT.Relu)
            attention(CACHE)
            attention(SELF)
            transposed(10, xhT)
            gates(6, E8)
            for s in range(2):
                for c in range(CH):
                    act.wait_ge(S["l3_h"], 4 * s + c + 1)
                    act.activation(hs[s][:, c, :], hid[c], ACT.Relu).then_inc(S["l3_h_sb"], 1)
                if s == 0:
                    gates_T(6, E8)

        @block.tensor
        def _(pe):
            pe.wait_ge(S["c_id"], 3)
            pe.wait_ge(S["in_ctx"], 16)
            for t in range(TILES):
                last = pe.transpose(ps[:, 5 + t // 4, (t % 4) * P:(t % 4 + 1) * P], ctx_tok[:, t, :], ident[:])
                if t % 4 == 3:
                    last.then_inc(S["c_cT"], 1)
            pe.wait_ge(S["in_w0"], 16 * 4)

            def weights(g):
                if g == 1:
                    pe.wait_ge(S["c_bd"], 3)
                for m in range(4):
                    last = pe.transpose((bankB if g else ps[:, 0, :])[:, m * P:(m + 1) * P], nat[:, 4 * g + m, :], ident[:])
                last.then_inc(S["c_wT"], 1)

            def context(a):
                wk, wv, wo = (wat[:, 4 * a + n, :] for n in (1, 2, 3))
                if a == 0:
                    pe.wait_ge(S["in_tab"], 16 * 10)
                    pe.transpose(bankB[:, 0:P], bt_rows[:, 1, :], ident[:]).then_inc(S["c_bT"], 1)
                if a == 1:
                    pe.transpose(bankA[:, P:2 * P], bt_rows[:, 0, :], ident[:])
                seqs = ctxT[:].rearrange("p (t b k) -> p b t k", b=2, k=SEQ)
                for s in range(2):
                    for b in range(2):
                        last = pe.matmul(ps[64 * b:64 * b + 64, 4 + s, :].rearrange("p (t k) -> p t k", k=SEQ),
                                         lhsT=(ident if a == CACHE else wk)[:, 64 * s:64 * s + 64], rhs=seqs[:, b],
                                         start=True, stop=True)
                last.then_inc(S["k_ps"], 1)
                if a < CACHE:
                    for b in range(BATCH):
                        for half in range(2):
                            last = pe.matmul(ps[64 * half:64 * half + 64, b // 4, (b % 4) * P:(b % 4 + 1) * P],
                                             lhsT=ctxT[:, SEQ * b:SEQ * b + SEQ], rhs=wv, start=True, stop=True)
                        if b % 4 == 3:
                            last.then_inc(S["v_ps"], 1)
                    if a == 0:
                        pe.wait_ge(S["c_bvw"], 1)
                        pe.wait_ge(S["in_bo"], 16 * 4)
                    pe.matmul(bankA[:, 0:P], lhsT=bv_wide[:, a, :], rhs=wo, start=True, stop=False)
                pe.matmul(bankA[:, 0:P], lhsT=ones[0:1, :], rhs=bo[:, a, :], start=(a == CACHE), stop=True
                          ).then_inc(S["ob_ps"], 1)

            def context_read(a):
                pe.wait_ge(S["k_sb"], 2 * a + 2)
                if a < CACHE:
                    pe.wait_ge(S["v_sb"], 4 * a + 4)
                pe.wait_ge(S["ob_sb"], a + 1)

            weights(0)
            pe.wait_ge(S["c_w_sb"], 1)
            pe.wait_ge(S["c_c_sb"], 2)
            context(0)
            context_read(0)

            def attention(a):
                wq, wk, wv, wo = (wat[:, 4 * a + n, :] for n in range(4))

                def front_x(f, par):
                    pe.wait_ge(S["a_xn"], V(a, f))
                    wait(pe, "a_qk_sb", V(a, f) - 1)
                    if a >= CACHE:
                        wait(pe, "a_v", TILES * (a - CACHE) + f - 1)
                    pe.transpose(bankA[:, 0:P], xn[par][:], ident[:]).then_inc(S["a_xT"], 1)

                def front_qk(f, par):
                    for n, w in enumerate((wq, wk) if a >= CACHE else (wq,)):
                        for s in range(2):
                            for b in range(2):
                                last = pe.matmul(bankA[64 * b:64 * b + 64, n * P + 64 * s:n * P + 64 * s + 64],
                                                 lhsT=w[:, 64 * s:64 * s + 64], rhs=xnT[par][:, b, 0, :], start=True, stop=True)
                    last.then_inc(S["a_qk"], 1)

                def new_values(s, o):
                    for b in range(2):
                        dst = tile_values[:, b * P:(b + 1) * P]
                        if a == CACHE:
                            last = pe.matmul(dst[SEQ:P, :], lhsT=xnT[o][:, b, 0, :], rhs=wv, start=True, stop=True)
                        else:
                            last = pe.matmul(dst, lhsT=xnT[o][:, b, :, :].rearrange("p d k -> p (d k)"), rhs=wv,
                                             start=True, stop=True)
                    last.then_inc(S["a_vm"], 1)

                def score(s, o, between=None):
                    pe.wait_ge(S["a_kbd"], V(a, s))
                    pe.wait_ge(S["a_qk_sb"], V(a, s))
                    if a != CACHE:
                        wait(pe, "a_sub", W(a, s) - 2)
                    kv, (n, j, k) = kview(a, o), shape(a)
                    for i in range(n):
                        half, h0 = i * j // 8, i * j % 8
                        if a == CACHE and h0 == 0:
                            pe.wait_ge(S["a_sub"], W(a, s, half) - 2)
                        last = pe.matmul(sview(a, o)[:, i, :, :], lhsT=qT[o][:, half, :], rhs=kv[:, half, h0:h0 + j, :],
                                         start=True, stop=True)
                        if a == CACHE and i == 1:
                            last.then_inc(S["a_s"], 1)
                        if i == 0 and between is not None:
                            out_y(between)
                    last.then_inc(S["a_s"], 1)

                def turn(c, par, groups):
                    for q in groups:
                        done = GROUP_BASE[a] + GROUPS[a] * c + q
                        if q % 2 == 0:
                            pe.wait_ge(S["a_exp"], W(a, c, q // 2 if a == CACHE else 1))
                        wait(pe, "a_pT_sb", done - 1)
                        for k in range(4):
                            ch = 4 * q + k
                            last = pe.transpose(ps[:, 4 + q % 2, k * P:(k + 1) * P], prob[par][:, ch * P:(ch + 1) * P], ident[:])
                        last.then_inc(S["a_pT"], 1)

                def values(p, o):
                    pe.wait_ge(S["a_pT_sb"], GROUP_BASE[a] + GROUPS[a] * (p + 1))
                    if a >= CACHE:
                        pe.wait_ge(S["a_v"], TILES * (a - CACHE) + p + 1)
                    else:
                        pe.wait_ge(S["a_vb"], V(a, p))
                    if a == CACHE:
                        pe.wait_ge(S["a_vpast"], p + 1)
                    wait(pe, "a_res", V(a, p) - 1)
                    chunks = 4 * GROUPS[a]
                    w = HEADS * (HD + 1) // chunks
                    v = vca[o] if a == CACHE else vbd[o]
                    for c in range(chunks):
                        for b in range(2):
                            last = pe.matmul(bankB[64 * b:64 * b + 64, w * c:w * c + w], lhsT=probT[:, c, 64 * b:64 * b + 64],
                                             rhs=v[:, b, c, :], start=True, stop=True)
                    last.then_inc(S["a_o"], 1)

                def out_T(p):
                    pe.wait_ge(S["a_on"], V(a, p))
                    pe.transpose(bankB[:, 256:384], on[:].rearrange("p h d -> p (h d)"), ident[:]).then_inc(S["a_oT"], 1)

                def out_y(p):
                    pe.wait_ge(S["a_oT_sb"], V(a, p))
                    pe.matmul(bankB[:, 384:512], lhsT=oT[:], rhs=wo, start=True, stop=True).then_inc(S["a_y"], 1)

                def body(f, s, c, p, nn, par):
                    if s is not None and a >= SCORES_FIRST:
                        score(s, 1 - par)
                    if f is not None:
                        front_x(f, par)
                    if p is not None:
                        values(p, 1 - par)
                    if f is not None:
                        pe.wait_ge(S["a_xT_sb"], V(a, f))
                    if s is not None and a >= CACHE:
                        new_values(s, 1 - par)
                    if f is not None:
                        front_qk(f, par)
                    if c is not None:
                        if a == CACHE and p is not None:
                            out_T(p)
                        turn(c, par, (0,))
                        if a == CACHE and p is not None:
                            out_y(p)
                    if p is not None and (a != CACHE or c is None):
                        out_T(p)
                    if c is not None:
                        turn(c, par, range(1, GROUPS[a]))
                    if f is not None and a < SCORES_FIRST:
                        score(f, par, p)
                    elif p is not None and (a != CACHE or c is None):
                        out_y(p)
                attention_tiles(a, pe, body)
                pe.wait_ge(S["a_res"], TILES * (a + 1))

            def turn_tokens(call, src):
                for g in range(2):
                    for k in range(4):
                        last = pe.transpose(ps[:, 6 + g, k * P:(k + 1) * P], src[:, 4 * g + k, :], ident[:])
                    last.then_inc(S["n_T"], 1)
                pe.wait_ge(S["n_T_sb"], 2 * call + 2)

            def router(srcT, cols, e):
                for t in range(TILES):
                    last = pe.matmul(ps[:, 6, t * e:(t + 1) * e], lhsT=srcT[:, t * P:(t + 1) * P], rhs=rw[:, cols],
                                     start=True, stop=True)
                last.then_inc(S["g_logits"], 1)

            def rank():
                pe.wait_ge(S["g_rank"], 1)
                pe.matmul(bankA[:, 64:128], lhsT=tri[:], rhs=g_sel[:].rearrange("p t e -> p (t e)"), start=True, stop=False)
                pe.matmul(bankA[:, 64:128], lhsT=ones[:], rhs=seen[:].rearrange("p t e -> p (t e)"), start=False, stop=True
                          ).then_inc(S["g_rank"], 1)

            def gates_T(m, e):
                pe.wait_ge(S["g_comb"], m + 1)
                for g in range(2):
                    for k in range(4):
                        last = pe.transpose(ps[0:e, 6 + g, k * P:(k + 1) * P], comb[:, 4 * g + k, 0:e], ident[:])
                    last.then_inc(S["g_cT"], 1)
                pe.wait_ge(S["g_cT_sb"], 2 * m + 2)

            def gated_bias(b2, e):
                for t in range(TILES):
                    last = pe.matmul(ps[:, 6 + t // 4, (t % 4) * P:(t % 4 + 1) * P], lhsT=combT[0:e, t * P:(t + 1) * P],
                                     rhs=b2, start=True, stop=True)
                last.then_inc(S["g_b2"], 1)

            def hidden(step, half, slot, loads, src, first=False):
                if half == 0:
                    pe.wait_ge(S["in_w1" + "ab"[slot]], loads)
                for c in range(CH):
                    if not first:
                        wait(pe, "e_h_sb", 4 * step + c - 3)
                    pe.matmul(hid[c], lhsT=w1s[slot][:, c * P:(c + 1) * P], rhs=src[:, 512 * half:512 * half + 512],
                              start=True, stop=True).then_inc(S["e_h"], 1)

            def outputs(step, half, slot, loads, first=False):
                pe.wait_ge(S["e_h_sb"], 4 * step + 4)
                if half == 0:
                    pe.wait_ge(S["in_w2" + "ab"[slot]], loads)
                if not first:
                    wait(pe, "e_acc", step - 1)
                for k in range(4):
                    for c in range(CH):
                        last = pe.matmul(ps[:, 4 + half, k * P:(k + 1) * P], lhsT=hs[half][:, c, k * P:(k + 1) * P],
                                         rhs=w2s[slot][:, c, :], start=(c == 0), stop=(c == CH - 1))
                last.then_inc(S["e_y"], 1)

            attention(0)
            pe.wait_ge(S["in_wt"], 16 * WEIGHT_LOADS)
            pe.wait_ge(S["in_bias"], 16 * SMALL_LOADS)
            context(1)
            weights(1)
            context_read(1)
            pe.wait_ge(S["c_b_sb"], 2)
            pe.wait_ge(S["c_w_sb"], 2)
            with pe.Fori(0, LAYERS0) as l:
                pe.wait_ge(S["n_done"], l + 2)
                turn_tokens(2 * l, cur)
                turn_tokens(2 * l + 1, xh)
                router(curT, bass.ds(l * E0, E0), E0)
                for s in range(2 * E0 + 1):
                    if s < 2 * E0:
                        e = s // 2
                        if s % 2 == 0:
                            pe.wait_ge(S["e_xe"], E0 * l + e + 1)
                        hidden(8 * l + s, s % 2, e % 2, 16 * (2 * l + e // 2 + 1), xe[e % 2], first=(s == 0))
                    if s == 0:
                        gates_T(l, E0)
                        gated_bias(b2_l0[:, bass.ds(l, 1), :].rearrange("e o h -> e (o h)"), E0)
                    else:
                        outputs(8 * l + s - 1, (s - 1) % 2, (s - 1) // 2 % 2, 16 * (2 * l + (s - 1) // 4 + 1), first=(s < 3))
                pe.wait_ge(S["g_init"], l + 1)
            for a, m, base in ((1, 4, STEP_L1), (2, 5, STEP_L2)):
                pe.wait_ge(S["e_acc"], base)
                attention(a)
                context(a + 1)
                if a == 1:
                    weights(2)
                context_read(a + 1)
                pe.wait_ge(S["c_w_sb"], 3)
                pe.wait_ge(S["n_done"], m + 2)
                turn_tokens(m + 4, xh)
                router(xhT, slice(16 + 8 * (m - 4), 24 + 8 * (m - 4)), E8)
                hidden(base, 0, 0, 16 * (base // 4 + 1), xhT)
                if m == 4:
                    rank()
                gates_T(m, E8)
                gated_bias(b2_l12[:, m - 4, :], E8)

                def pair(e, final, base=base):
                    for k in range(4):
                        st = base + 2 * e
                        if not (final and k == 3):
                            loads = 16 * (base // 4 + 1) + (8 * (e + (2 if k == 3 else 0)))
                            hidden(st + k + 1, (k + 1) % 2, (k + 1) // 2 % 2, loads, xhT)
                        outputs(st + k, k % 2, k // 2, 16 * (base // 4 + 1) + 8 * e)
                with pe.Fori(0, E8 // 2 - 1) as e:
                    pair(2 * e, False)
                pair(E8 - 2, True)
                pe.wait_ge(S["g_init"], m + 1)
            pe.wait_ge(S["e_acc"], STEP_L2 + 2 * E8)
            attention(CACHE)
            attention(SELF)
            pe.wait_ge(S["n_done"], 9)
            turn_tokens(10, xh)
            router(xhT, slice(32, 40), E8)
            pe.wait_ge(S["in_w2nd"], 32)

            def hidden3(s):
                for c in range(CH):
                    wait(pe, "l3_h_sb", 4 * s + c - 3)
                    pe.matmul(hid[c], lhsT=w1c[:].rearrange("p e f -> p (e f)")[:, c * P:(c + 1) * P],
                              rhs=xhT[:, 512 * s:512 * s + 512], start=True, stop=True).then_inc(S["l3_h"], 1)
            hidden3(0)
            gates_T(6, E8)
            for s in range(2):
                for c in range(CH):
                    k = 4 * s + c
                    wait(pe, "l3_gated", k - 1)
                    pe.matmul(ps[:, 4 + k % 2, :], lhsT=esel[:].rearrange("e g f -> e (g f)")[:, c * P:(c + 1) * P],
                              rhs=combT[:, 512 * s:512 * s + 512], start=True, stop=True).then_inc(S["l3_gate"], 1)
                if s == 0:
                    hidden3(1)
                pe.wait_ge(S["l3_gated"], 4 * s + 4)
                for k in range(4):
                    for c in range(CH):
                        last = pe.matmul(ps[:, 6 + s, k * P:(k + 1) * P], lhsT=hs[s][:, c, k * P:(k + 1) * P],
                                         rhs=w2c[:, c, :], start=(c == 0), stop=(c == CH - 1))
                last.then_inc(S["l3_y"], 1)

        @block.vector
        def _(dve):
            def link(ins, name, value):
                ins.then_inc(S[name], 1)
                dve.wait_ge(S[name], value)

            dve.wait_ge(S["c_id"], 3)
            dve.tensor_reduce(m8[:], m16[:].rearrange("p (i j) -> p j i", j=HEADS // 2), AX, ALU.add).then_inc(S["c_dve"], 1)
            dve.wait_ge(S["in_len"], 16)
            dve.wait_ge(S["c_pool"], 14)
            link(dve.tensor_copy(len_f[:], len_i[:]), "c_dve", 2)
            link(dve.tensor_reduce(len_max[:], len_f[:], AX, ALU.max), "c_dve", 3)
            for b in range(2):
                r = slice(64 * b, 64 * b + 64)
                dve.tensor_copy(len_half[r, :], len_f[r, :].rearrange("p (t b) -> p b t", b=2)[:, b]).then_inc(S["c_past"], 1)
            dve.wait_ge(S["c_past"], 2)
            dve.tensor_tensor(past_k[:], iota_k[:, None, :].broadcast_to([P, TILES, SEQ]),
                              len_half[:, :, None].broadcast_to([P, TILES, SEQ]), ALU.is_lt).then_inc(S["c_past"], 1)
            dve.tensor_tensor(past_v[:], iota_p[:, 0:1].broadcast_to([P, BATCH]), len_f[:], ALU.is_lt).then_inc(S["c_past"], 1)
            dve.tensor_scalar(kill_cache[:], iota_k[:], len_max[:, 0:1], None, ALU.is_ge).then_inc(S["c_past"], 1)
            dve.wait_ge(S["in_x"], 16)

            def attention(a):
                src = cur if a == SELF else x
                if a == 1:
                    dve.wait_ge(S["in_mask"], 16)

                def stats(t, par):
                    link(dve.bn_stats(stat[par][:], src[:, bass.ds(t, 1), :].rearrange("p o d -> p (o d)")), "a_stat", V(a, t))
                    dve.nop(nofuse=True)
                    dve.bn_aggr(mv[par][:], stat[par][:]).then_inc(S["a_mv"], 1)

                def normal(t, par):
                    dve.wait_ge(S["a_mv"], V(a, t))
                    dve.wait_ge(S["a_rstd"], V(a, t))
                    wait(dve, "a_xT", V(a, t) - 2)
                    o = dve.tensor_scalar(xn[par][:], src[:, bass.ds(t, 1), :].rearrange("p o d -> p (o d)"),
                                          mv[par][:, 0:1], rstd[par][:, 0:1], ALU.subtract, ALU.mult)
                    if a == SELF:
                        link(o, "a_aff", 2 * t + 1)
                        link(dve.tensor_tensor(xn[par][:], xn[par][:], bcast[:, 0, :], ALU.mult), "a_aff", 2 * t + 2)
                        o = dve.tensor_tensor(xn[par][:], xn[par][:], bcast[:, 1, :], ALU.add)
                    o.then_inc(S["a_xn"], 1)

                def maxima(s, par):
                    for half, banks in halves(a):
                        dve.wait_ge(S["a_s"], W(a, s, half))
                        sc, (n, j, k) = sview(a, par)[:, banks], shape(a)
                        full = [P, 2, j, SEQ]
                        if a == 1:
                            link(dve.tensor_scalar(kill[par][:], mask[:, bass.ds(s, 1), :].rearrange("p o k -> p (o k)"),
                                                   0, None, ALU.is_equal), "a_kill", s + 1)
                            dve.nop(nofuse=True)
                            link(dve.copy_predicated(sc, kill[par][:, None, None, :].broadcast_to(full),
                                                     neg[:, 0:1, None, None].broadcast_to(full)), "a_masked", s + 1)
                        if a == CACHE:
                            dve.nop(nofuse=True)
                            link(dve.copy_predicated(sc[:, :, :, 0:SEQ], kill_cache[:, None, None, :].broadcast_to(full),
                                                     neg[:, 1:2, None, None].broadcast_to(full)), "a_masked",
                                 TILES + 2 * s + half + 1)
                        dve.tensor_reduce(smax[:].rearrange("p (i j) -> p i j", j=j)[:, banks], sc, AX, ALU.max
                                          ).then_inc(S["a_max"], 1)

                def shifted(c, par):
                    n, j, k = shape(a)
                    if a > 0 or not isinstance(c, int) or c >= 1:
                        dve.wait_ge(S["a_pT"], GROUP_BASE[a] + (GROUPS[a] * (c - 1) + 1 if not isinstance(c, int) or c >= 1 else 0))
                    for half, banks in halves(a):
                        dve.wait_ge(S["a_max"], W(a, c, half))
                        dve.tensor_tensor(pview(a, par)[:, banks], sview(a, par)[:, banks],
                                          smax[:].rearrange("p (i j) -> p i j", j=j)[:, banks, :, None]
                                          .broadcast_to([P, 2, j, k]), ALU.subtract).then_inc(S["a_sub"], 1)

                def out_norm(p):
                    dve.wait_ge(S["a_o"], V(a, p))
                    o = bankB[:, 0:HEADS * (HD + 1)].rearrange("p (h w) -> p h w", w=HD + 1)
                    link(dve.reciprocal(rsum[:], o[:, :, HD]), "a_rs", V(a, p))
                    dve.tensor_tensor(on[:], o[:, :, 0:HD], rsum[:, :, None].broadcast_to([P, HEADS, HD]), ALU.mult
                                      ).then_inc(S["a_on"], 1)

                def residual(p):
                    dve.wait_ge(S["a_y"], V(a, p))
                    if a != SELF:
                        dve.wait_ge(S["a_bo"], V(a, p))
                    tile = src[:, bass.ds(p, 1), :].rearrange("p o d -> p (o d)")
                    dve.tensor_tensor(tile, bankB[:, 384:512], tile, ALU.add).then_inc(S["a_res"], 1)

                def body(f, s, c, p, nn, par):
                    if c is not None:
                        shifted(c, par)
                    if nn is not None:
                        stats(nn, 1 - par)
                    if s is not None and a == CACHE:
                        maxima(s, 1 - par)
                    if p is not None:
                        out_norm(p)
                    if nn is not None:
                        normal(nn, 1 - par)
                    if s is not None and a != CACHE:
                        maxima(s, 1 - par)
                    if p is not None:
                        residual(p)
                attention_tiles(a, dve, body)
                dve.wait_ge(S["a_res"], TILES * (a + 1))

            def norm(k, src, dst):
                for t in range(TILES):
                    last = dve.bn_stats(stat8[:, t, :], src[:, t, :])
                link(last, "n_stat", k + 1)
                dve.nop(nofuse=True)
                for t in range(TILES):
                    last = dve.bn_aggr(mv8[:, t, :], stat8[:, t, :])
                last.then_inc(S["n_mv"], 1)
                dve.wait_ge(S["n_rstd"], k + 1)
                for t in range(TILES):
                    last = dve.tensor_scalar(dst[:, t, :], src[:, t, :], mv8[:, t, 0:1], rstd8[:, t:t + 1], ALU.subtract, ALU.mult)
                return last

            def gate(m, e, bias, ranked=False):
                full = [P, TILES, e]
                lg, two, key, sel, ex, cb = (v[:, :, 0:e] for v in (g_log, g_two, g_key, g_sel, g_exp, comb))
                n = [0]

                def chain(ins):
                    n[0] += 1
                    link(ins, "g_ln", GATE_LINKS * m + n[0])

                def wide(v):
                    return v[:, :, None].broadcast_to(full)

                def first_of(values, hot):
                    chain(dve.tensor_reduce(g_tmp[:], values, AX, ALU.max))
                    chain(dve.tensor_tensor(key, values, wide(g_tmp[:]), ALU.is_equal))
                    chain(dve.tensor_tensor(key, key, order[:, None, 0:e].broadcast_to(full), ALU.mult))
                    chain(dve.tensor_reduce(g_sum[:], key, AX, ALU.max))
                    chain(dve.tensor_tensor(hot, key, wide(g_sum[:]), ALU.is_equal))

                dve.wait_ge(S["g_logits"], m + 1)
                lp = ps[:, 6, 0:TILES * e].rearrange("p (t e) -> p t e", e=e)
                if bias is None:
                    chain(dve.tensor_copy(lg, lp))
                else:
                    chain(dve.tensor_tensor(lg, lp, bias.broadcast_to(full), ALU.add))
                chain(dve.tensor_reduce(g_max[:], lg, AX, ALU.max))
                dve.tensor_tensor(ex, lg, wide(g_max[:]), ALU.subtract).then_inc(S["g_sub"], 1)
                first_of(lg, sel)
                chain(dve.scalar_tensor_tensor(out=two, in0=sel, scalar=-3e38, in1=lg, op0=ALU.mult, op1=ALU.add))
                first_of(two, two)
                chain(dve.tensor_tensor(sel, sel, two, ALU.add))
                dve.wait_ge(S["g_ex"], m + 1)
                chain(dve.tensor_tensor(ex, ex, sel, ALU.mult))
                chain(dve.tensor_reduce(g_sum[:], ex, AX, ALU.add))
                chain(dve.reciprocal(g_sum[:], g_sum[:]))
                if not ranked:
                    link(dve.tensor_tensor(cb, ex, wide(g_sum[:]), ALU.mult), "g_comb", m + 1)
                else:
                    link(dve.memset(seen[:, 0, :], 0.0), "n_aff", 1)
                    for t in range(1, TILES):
                        link(dve.tensor_tensor(seen[:, t, :], seen[:, t - 1, :], g_sel[:, t - 1, :], ALU.add), "n_aff", t + 1)
                    dve.tensor_tensor(cb, ex, wide(g_sum[:]), ALU.mult).then_inc(S["g_rank"], 1)
                    dve.wait_ge(S["g_rank"], 2)
                    link(dve.tensor_scalar(key, bankA[:, 64:128].rearrange("p (t e) -> p t e", e=e), float(CAPACITY), None,
                                           ALU.is_le), "n_aff", TILES + 1)
                    link(dve.tensor_tensor(cb, cb, key, ALU.mult), "g_comb", m + 1)
                assert n[0] == GATE_LINKS

            def gated_sum(step, half, e, dst, first=False):
                dve.wait_ge(S["e_y"], step + 1)
                if not first:
                    wait(dve, "e_acc", step - 1)
                for k in range(4):
                    t = 4 * half + k
                    last = dve.scalar_tensor_tensor(out=dst[:, t, :], in0=ps[:, 4 + half, k * P:(k + 1) * P],
                                                    scalar=comb[:, t, bass.ds(e, 1)], in1=dst[:, t, :],
                                                    op0=ALU.mult, op1=ALU.add)
                last.then_inc(S["e_acc"], 1)

            attention(0)
            dve.wait_ge(S["in_bias"], 16 * SMALL_LOADS)
            norm(0, x, cur).then_inc(S["n_done"], 1)
            dve.wait_ge(S["n_done"], 1)
            with dve.Fori(0, LAYERS0) as l:
                norm(l + 1, cur, xh).then_inc(S["n_done"], 1)
                gate(l, E0, rbias[:, None, bass.ds(l * E0, E0)])
                link(dve.tensor_reduce(g_tmp[:], comb[:, :, 0:E0], AX, ALU.add), "g_csum", l + 1)
                dve.wait_ge(S["g_b2"], l + 1)
                for t in range(TILES):
                    last = dve.scalar_tensor_tensor(out=cur[:, t, :], in0=cur[:, t, :], scalar=g_tmp[:, t:t + 1],
                                                    in1=ps[:, 6 + t // 4, (t % 4) * P:(t % 4 + 1) * P],
                                                    op0=ALU.mult, op1=ALU.add)
                link(last, "g_init", l + 1)
                for s in range(2 * E0):
                    gated_sum(8 * l + s, s % 2, s // 2, cur, first=(s < 2))
                dve.wait_ge(S["e_acc"], 8 * l + 8)
            dve.wait_ge(S["e_acc"], STEP_L1)
            link(dve.tensor_tensor(x[:], x[:], cur[:], ALU.add), "l0_x", 1)
            for a, m, base in ((1, 4, STEP_L1), (2, 5, STEP_L2)):
                attention(a)
                norm(m + 1, x, xh).then_inc(S["n_done"], 1)
                c0 = 16 + 8 * (m - 4)
                gate(m, E8, rbias[:, None, c0:c0 + 8], ranked=(m == 4))
                dve.wait_ge(S["g_b2"], m + 1)
                for g in range(2):
                    last = dve.tensor_tensor(x[:, 4 * g:4 * g + 4, :], ps[:, 6 + g, :].rearrange("p (t d) -> p t d", d=P),
                                             x[:, 4 * g:4 * g + 4, :], ALU.add)
                link(last, "g_init", m + 1)
                with dve.Fori(0, E8) as e:
                    for h in range(2):
                        gated_sum(base + 2 * e + h, h, e, x)
                dve.wait_ge(S["e_acc"], base + 2 * E8)
            attention(CACHE)
            norm(7, x, cur).then_inc(S["n_done"], 1)
            dve.wait_ge(S["n_done"], 8)
            attention(SELF)
            link(norm(8, cur, xh), "n_aff", TILES + 2)
            for v, op in ((2, ALU.mult), (3, ALU.add)):
                last = dve.tensor_tensor(xh[:], xh[:], bcast[:, v:v + 1, :].broadcast_to([P, TILES, P]), op)
                if v == 2:
                    link(last, "n_aff", TILES + 3)
            last.then_inc(S["n_done"], 1)
            gate(6, E8, None)
            for s in range(2):
                for c in range(CH):
                    k = 4 * s + c
                    dve.wait_ge(S["l3_h_sb"], k + 1)
                    dve.wait_ge(S["l3_gate"], k + 1)
                    dve.tensor_tensor(hs[s][:, c, :], ps[:, 4 + k % 2, :], hs[s][:, c, :], ALU.mult).then_inc(S["l3_gated"], 1)
                dve.wait_ge(S["l3_res"], 1)
                dve.wait_ge(S["l3_y"], s + 1)
                dve.tensor_tensor(x[:, 4 * s:4 * s + 4, :], ps[:, 6 + s, :].rearrange("p (t d) -> p t d", d=P),
                                  x[:, 4 * s:4 * s + 4, :], ALU.add).then_inc(S["l3_x"], 1)


SMALL_LOADS = 18
WEIGHT_LOADS = 16
GATE_LINKS = 17


def kernel(**inputs):
    import numpy as _np
    import concourse.bacc as _bacc
    from concourse import mybir as _mybir
    from concourse.bass_utils import run_bass_kernel_spmd as _run

    nc = _bacc.Bacc("TRN2", target_bir_lowering=False, num_devices=1)
    arrays, aps = {}, {}
    for name, value in inputs.items():
        a = _np.ascontiguousarray(value)
        arrays[f"in_{name}_dram"] = a
        aps[name] = nc.dram_tensor(f"in_{name}_dram", a.shape, _mybir.dt.from_np(a.dtype), kind="ExternalInput").ap()
    shape = tuple(inputs["x"].shape)
    o = nc.dram_tensor("out_0_dram", shape, _mybir.dt.from_np(_np.dtype("float32")), kind="ExternalOutput").ap()
    build(nc, aps, o)
    r = _run(nc, [arrays], core_ids=[0])
    return r.results[0]["out_0_dram"]
```

```python
from contextlib import ExitStack

import concourse.bass as bass
from concourse import mybir

F32 = mybir.dt.float32
I32 = mybir.dt.int32
F32R = mybir.dt.float32r
ALU = mybir.AluOpType
ACT = mybir.ActivationFunctionType
AX = mybir.AxisListType.X

P = 128
BATCH, SEQ = 16, 64
TILES = BATCH * SEQ // P
HEADS, HD = 16, 8
FF = 512
CH = FF // P
EPS = 1e-5
SCALE = HD ** -0.5
NEG_MASK = -1e9 / SCALE
NEG_CACHE = -1e30 / SCALE
CAPACITY = int(1.25 * BATCH * SEQ / 8)
LAYERS0, E0, E8 = 4, 4, 8

CACHE, SELF = 3, 4
SCORES_FIRST = CACHE
GROUPS = [2, 2, 2, 4, 2]
GROUP_BASE = [TILES * sum(GROUPS[:a]) for a in range(5)]
B1_L0, LNG_L0, LNB_L0, B1_L1 = 0, 64, 80, 96
B1_L2, BQ, BK, BV = 128, 160, 166, 172
UNITS = 2 * LAYERS0
HALF = TILES // 2
GATE_L1, GATE_L2, GATE_L3 = UNITS, UNITS + 1, UNITS + 2
NORM_A, NORM_U0, NORM_B, NORM_L1 = 0, 1, 2, UNITS + 2
NORM_L2, NORM_MID, NORM_L3 = NORM_L1 + 2, NORM_L1 + 4, NORM_L1 + 6
STEP_L1 = 2 * LAYERS0 * E0
STEP_L2 = STEP_L1 + 2 * E8


def build(nc, A, out):
    with ExitStack() as ctx:
        def sb(name, shape, dt=F32):
            return ctx.enter_context(nc.sbuf_tensor(name, shape, dt))

        def sem(name):
            return ctx.enter_context(nc.semaphore(name))

        x = sb("x", [P, TILES, P])
        cur = sb("cur", [P, TILES, P])
        xh = sb("xh", [P, TILES, P])
        xhT = sb("xhT", [P, TILES * P])
        xe = [sb(f"xe{i}", [P, HALF * P]) for i in range(2)]
        xr = [[sb(f"xr{i}_{n}", [P, HALF * P], F32R) for n in ("hi", "lo")] for i in range(2)]
        w1r = [[sb(f"w1r{i}_{n}", [P, FF], F32R) for n in ("hi", "lo")] for i in range(E0)]
        hs = [sb(f"hs{i}", [P, CH, 512]) for i in range(2)]
        w1s = [sb(f"w1s{i}", [P, FF]) for i in range(E0)]
        w2s = [sb(f"w2s{i}", [P, CH, P]) for i in range(E0)]
        ctx_tok = sb("ctx_tok", [P, TILES, P])
        curT = ctx_tok[:].rearrange("p t d -> p (t d)")
        ctxT = sb("ctxT", [P, TILES * P])
        keys_all = sb("keys_all", [P, 2, TILES * SEQ])
        cacheV = sb("cacheV", [SEQ, BATCH, P])
        nat = sb("nat", [P, 12, P])
        wat = sb("wat", [P, 20, P])
        rows8 = sb("rows8", [P, 3, HD])
        bt_rows = sb("bt_rows", [P, 2, P])
        bt = sb("bt", [P, 256])
        bcast = sb("bcast", [P, 4, P])
        bo = sb("bo", [1, 4, P])
        out_bias = sb("out_bias", [P, 4, P])
        bv_wide = sb("bv_wide", [P, 3, P])
        rbias = sb("rbias", [P, 4 * E0 + 2 * E8])
        rw = sb("rw", [P, 4 * E0 + 3 * E8])
        b2_l0 = sb("b2_l0", [E0, LAYERS0, P])
        b2_l12 = sb("b2_l12", [E8, 2, P])
        w1c = sb("w1c", [P, E8, FF // E8])
        w2c = sb("w2c", [P, CH, P])
        esel = sb("esel", [E8, E8, FF // E8])
        ident = sb("ident", [P, P])
        ones = sb("ones", [P, P])
        tri = sb("tri", [P, P])
        m16 = sb("m16", [P, HEADS])
        m8 = sb("m8", [P, HEADS // 2])
        epow = sb("epow", [P, 2 * TILES])
        lay_gb = sb("lay_gb", [P, 2, E0])
        lay_b1 = sb("lay_b1", [P, E0 * CH])
        order = sb("order", [P, E8])
        neg = sb("neg", [P, 2])
        iota_k = sb("iota_k", [P, SEQ])
        iota_p = sb("iota_p", [P, 1])
        len_i = sb("len_i", [P, BATCH], I32)
        len_f = sb("len_f", [P, BATCH])
        len_max = sb("len_max", [P, 1])
        len_half = sb("len_half", [P, TILES])
        past_k = sb("past_k", [P, TILES, SEQ])
        past_v = sb("past_v", [P, BATCH])
        kill_cache = sb("kill_cache", [P, SEQ], I32)
        mask = sb("mask", [P, TILES, SEQ], I32)
        kill = [sb(f"kill{i}", [P, SEQ], I32) for i in range(2)]
        xn = [sb(f"xn{i}", [P, P]) for i in range(2)]
        stat = [sb(f"stat{i}", [P, 6]) for i in range(2)]
        mv = [sb(f"mv{i}", [P, 2]) for i in range(2)]
        ve = [sb(f"ve{i}", [P, 1]) for i in range(2)]
        rstd = [sb(f"rstd{i}", [P, 1]) for i in range(2)]
        xnT = [sb(f"xnT{i}", [P, 2, 2, SEQ]) for i in range(2)]
        qT = [sb(f"qT{i}", [P, 2, P]) for i in range(2)]
        kT = [sb(f"kT{i}", [P, 2, SEQ]) for i in range(2)]
        kbd = [sb(f"kbd{i}", [P, HEADS * P]) for i in range(2)]
        values_all = sb("values_all", [P, BATCH, HEADS // 2, 2 * (HD + 1)])
        vbd = [sb(f"vbd{i}", [P, 2, HEADS // 2, 2 * (HD + 1)]) for i in range(2)]
        vca = [sb(f"vca{i}", [P, 2, HEADS, HD + 1]) for i in range(2)]
        prob = [sb(f"prob{i}", [P, HEADS * P]) for i in range(2)]
        probT = sb("probT", [P, HEADS, P])
        smax = sb("smax", [P, HEADS])
        rsum = sb("rsum", [P, HEADS])
        on = sb("on", [P, HEADS, HD])
        oT = sb("oT", [P, P])
        stat8 = sb("stat8", [P, TILES, 6])
        mv8 = sb("mv8", [P, TILES, 2])
        ve8 = sb("ve8", [P, TILES])
        rstd8 = sb("rstd8", [P, TILES])
        g_log = sb("g_log", [P, TILES, E8])
        g_two = sb("g_two", [P, TILES, E8])
        g_key = sb("g_key", [P, TILES, E8])
        g_sel = sb("g_sel", [P, TILES, E8])
        g_exp = sb("g_exp", [P, TILES, E8])
        g_max = sb("g_max", [P, TILES])
        g_tmp = sb("g_tmp", [P, TILES])
        g_sum = sb("g_sum", [P, TILES])
        seen = sb("seen", [P, TILES, E8])
        comb = sb("comb", [P, TILES, E8])
        combT = sb("combT", [E8, TILES * P])

        ps = ctx.enter_context(nc.psum_tensor("ps", [P, 8, 512], F32))
        hid = [ps[:, c, :] for c in range(4)]
        gate_r = [[xr[s][part][0:E8, :] for part in range(2)] for s in range(2)]
        sel_r = w1r[0][0][0:E8, :]
        l3_banks = (4, 5, 0, 1, 2, 3)
        bankA, bankB = ps[:, 6, :], ps[:, 7, :]

        names = """in_x in_ctx in_w0 in_tab in_bo in_len in_wt in_bias in_w2nd in_mask in_w1_0 in_w1_1 in_w1_2 in_w1_3 in_w2_0 in_w2_1 in_w2_2 in_w2_3
            c_rows c_id0 c_id c_pool c_dve c_bd c_past c_cache c_wT c_w_sb c_bvw c_bT c_b_sb c_cT c_c_sb
            a_stat a_mv a_ve a_rstd a_xn a_xT a_xT_sb a_qk a_qk_sb a_kbd a_vpast a_v a_s a_kill c_hide a_masked a_max a_sub a_exp
            a_pT a_pT_sb a_o a_rs a_on a_oT a_oT_sb a_y a_res a_aff
            n_stat n_mv n_ve n_rstd n_aff n_done n_T n_T_sb g_logits g_ln g_sub g_ex g_comb g_rank g_cT g_cT_sb g_b2 g_init
            k_ps k_sb v_ps v_sb a_vb ob_ps ob_sb a_vm a_bo e_xf e_xe e_whi e_w x_hi x_lo e_h e_h_sb e_y e_acc l0_x l3_res l3_gate l3_gated l3_sel l3_ghi l3_glo l3_h l3_h_sb l3_y l3_x stored""".split()
        names += ["in_cv", 'g_csum', 'lay_pool', 'lay_act']
        S = {n: sem(n) for n in names}
        block = ctx.enter_context(nc.Block())

        def shape(a):
            return (4, 4, P) if a == CACHE else (2, 8, SEQ)

        def sview(a, par):
            n, j, k = shape(a)
            b0 = 0 if a == CACHE else 2 * par
            return ps[:, b0:b0 + n, :].rearrange("p i (j k) -> p i j k", k=k)

        tile_values = bankA[:, 2 * P:4 * P]

        def pview(a, par):
            n, j, k = shape(a)
            return prob[par][:, 0:HEADS * k].rearrange("p (i j k) -> p i j k", i=n, k=k)

        def kview(a, par):
            k = shape(a)[2]
            return kbd[par][:, 0:HEADS * k].rearrange("p (s j k) -> p s j k", s=2, k=k)

        def attention_tiles(a, eng, body, extra=None, steps="all"):
            def at(t):
                ok = [t + d if 0 <= t + d < TILES else None for d in (2, 1, 0, -1, 3)]
                body(*ok, t % 2)
                if extra is not None:
                    extra(t)
            for t in range(-1 if steps == "rest" else -3, -1 if steps == "head" else 1):
                at(t)
            if steps == "head":
                return
            with eng.Fori(0, 2) as pair:
                t = 2 * pair + 1
                body(t + 2, t + 1, t, t - 1, t + 3, 1)
                body(t + 3, t + 2, t + 1, t, t + 4, 0)
            for t in range(5, TILES + 1):
                at(t)

        def V(a, t):
            return TILES * a + t + 1

        def W(a, t, half=1):
            if a == CACHE:
                return TILES * a + 2 * t + half + 1
            return TILES * (a + (a > CACHE)) + t + 1

        def halves(a):
            return [(0, slice(0, 2)), (1, slice(2, 4))] if a == CACHE else [(1, slice(0, 2))]

        def split_ahead(l, h, e, last):
            if h == 0 and e < 2:
                return l, e + 2
            if h == 1 and e >= 2 and not last:
                return l + 1, e - 2
            return None

        def wait(eng, name, value):
            if not isinstance(value, int) or value > 0:
                eng.wait_ge(S[name], value)

        @block.sync
        def _(sp):
            sp.dma_start(ctx_tok[:], A["ctx_1024"].rearrange("b s d -> (b s) d").rearrange("(t p) d -> p t d", p=P)).then_inc(S["in_ctx"], 16)
            for slot, n in enumerate(("wq", "wk", "wv", "wo")):
                sp.dma_start(nat[:, slot, :], A[f"L0_xattn_{n}"]).then_inc(S["in_w0"], 16)
            sp.wait_ge(S["c_rows"], 1)
            sp.dma_start(bt_rows[0:32, 1, :], A["L2_ffn_b1"].rearrange("e (c f) -> (e c) f", f=P)).then_inc(S["in_tab"], 16)
            sp.dma_start(x[:], A["x"].rearrange("b s d -> (b s) d").rearrange("(t p) d -> p t d", p=P)).then_inc(S["in_x"], 16)

            sp.dma_start(len_i[:], A["_lenS2"].partition_broadcast(P)).then_inc(S["in_len"], 16)
            small = [(rbias[:, 0:16], A["L0_ffn_router_b"].rearrange("l e -> (l e)").partition_broadcast(P)),
                     (rw[:, 0:16].rearrange("p (l e) -> p l e", e=E0), A["L0_ffn_router_w"].rearrange("l h e -> h l e")),
                     (b2_l0[:], A["L0_ffn_b2"].rearrange("l e h -> e l h")),
                     (rbias[:, 16:24], A["L1_ffn_gate_b"].partition_broadcast(P)),
                     (rbias[:, 24:32], A["L2_ffn_br"].partition_broadcast(P)),
                     (rw[:, 16:24], A["L1_ffn_gate_w"]), (rw[:, 24:32], A["L2_ffn_Wr"]), (rw[:, 32:40], A["L3_ffn_Wg"]),
                     (b2_l12[:, 0, :], A["L1_ffn_b2"]), (b2_l12[:, 1, :], A["L2_ffn_b2"])]
            small += [(bcast[:, n, :], A[f"L3_ffn_{v}"].partition_broadcast(P)) for n, v in enumerate(("g1", "b1", "g2", "b2"))]
            small += [(bt_rows[0:64, 0, :], A["L0_ffn_b1"].rearrange("l e (c f) -> (l e c) f", f=P)),
                      (bt_rows[64:80, 0, :], A["L0_ffn_ln_g"].rearrange("l e h -> (l e) h")),
                      (bt_rows[80:96, 0, :], A["L0_ffn_ln_b"].rearrange("l e h -> (l e) h")),
                      (bt_rows[96:128, 0, :], A["L1_ffn_b1"].rearrange("e (c f) -> (e c) f", f=P))]
            assert len(small) == SMALL_LOADS
            for dst, src in small:
                sp.dma_start(dst, src).then_inc(S["in_bias"], 16)
            slots = [("L2_xattn_wo", 7), ("L3_xattn_wq", 8), ("L3_xattn_wk", 9), ("L3_xattn_wv", 10), ("L3_xattn_wo", 11)]
            for n, slot in slots:
                sp.dma_start(nat[:, slot, :], A[n]).then_inc(S["in_wt"], 16)
            for n, v in enumerate(("wq", "wk", "wv")):
                sp.dma_start(rows8[:, n, :], A[f"L2_xattn_{v}"].rearrange("h e d -> (h e) d")).then_inc(S["in_wt"], 16)
            for n, v in enumerate(("Wq", "Wk", "Wv", "Wo")):
                sp.dma_start(wat[:, 4 + n, :], A[f"L1_xattn_{v}"]).then_inc(S["in_wt"], 16)
                sp.dma_start(wat[:, 16 + n, :], A[f"L3_ffn_{v}"]).then_inc(S["in_wt"], 16)
            sp.dma_start(mask[:], A["mask_BxSxS2_ik0"].rearrange("b q k -> (b q) k").rearrange("(t p) k -> p t k", p=P)).then_inc(S["in_mask"], 16)
            def expert(w1, w2, e, i):
                sp.dma_start(w1s[i][:], w1[bass.ds(e, 1), :, :].rearrange("o h f -> (o h) f")).then_inc(S[f"in_w1_{i}"], 16)
                sp.dma_start(w2s[i][:], w2[bass.ds(e, 1), :, :, :].rearrange("o f c h -> (o f) c h")).then_inc(S[f"in_w2_{i}"], 16)

            w1_0, w2_0 = A["L0_ffn_w1"].rearrange("l e h f -> (l e) h f"), A["L0_ffn_w2"].rearrange("l e (c f) h -> (l e) f c h", f=P)
            for e in range(E0):
                expert(w1_0, w2_0, e, e)
            with sp.Fori(1, LAYERS0) as l:
                for e in range(E0):
                    sp.wait_ge(S["e_y"], 2 * E0 * l - E0 + e + 1)
                    expert(w1_0, w2_0, E0 * l + e, e)
            sp.dma_start(w1c[:], A["L3_ffn_W1"].rearrange("e h f -> h e f")).then_inc(S["in_w2nd"], 16)
            sp.dma_start(w2c[:], A["L3_ffn_W2"].rearrange("(c g) f h -> (g f) c h", c=CH)).then_inc(S["in_w2nd"], 16)
            for w1, w2, base in ((A["L1_ffn_w1"], A["L1_ffn_w2"].rearrange("e (c f) h -> e f c h", f=P), STEP_L1),
                                 (A["L2_ffn_W1"], A["L2_ffn_W2"].rearrange("e (c f) h -> e f c h", f=P), STEP_L2)):
                with sp.Fori(0, E8 // 2) as pair:
                    for i in range(2):
                        sp.wait_ge(S["e_y"], base + 4 * pair + 2 * i - 2)
                        expert(w1, w2, 2 * pair + i, i)
            dst = out.rearrange("b s d -> (b s) d").rearrange("(t p) d -> p t d", p=P)
            for h in range(2):
                sp.wait_ge(S["l3_x"], h + 1)
                sp.dma_start(dst[:, 4 * h:4 * h + 4, :], x[:, 4 * h:4 * h + 4, :]).then_inc(S["stored"], 16)
            sp.wait_ge(S["stored"], 32)

        @block.gpsimd
        def _(pool):
            pool.memset(bt_rows[:], 0.0).then_inc(S["c_rows"], 1)
            pool.memset(ident[:], 0.0).then_inc(S["c_id0"], 1)
            pool.memset(ones[:], 1.0).then_inc(S["c_id0"], 1)
            pool.memset(m16[:], 1.0).then_inc(S["c_id0"], 1)
            pool.memset(esel[:], 1.0).then_inc(S["c_id0"], 1)
            for i in range(2):
                pool.memset(qT[i][:], 0.0).then_inc(S["c_id0"], 1)
            pool.wait_ge(S["c_id0"], 6)
            pool.affine_select(out=ident[:], in_=ident[:], compare_op=ALU.not_equal, fill=1.0, base=0,
                               pattern=[[-1, P]], channel_multiplier=1).then_inc(S["c_id"], 1)
            pool.affine_select(out=m16[:], in_=m16[:], compare_op=ALU.is_ge, fill=0.0, base=0,
                               pattern=[[-HD, HEADS]], channel_multiplier=1).then_inc(S["c_id"], 1)
            pool.wait_ge(S["c_id"], 2)
            pool.affine_select(out=m16[:], in_=m16[:], compare_op=ALU.is_ge, fill=0.0, base=HD - 1,
                               pattern=[[HD, HEADS]], channel_multiplier=-1).then_inc(S["c_id"], 1)

            pool.affine_select(out=tri[:], in_=ones[:], compare_op=ALU.is_ge, fill=0.0, base=0,
                               pattern=[[1, P]], channel_multiplier=-1).then_inc(S["c_pool"], 1)
            pool.affine_select(out=esel[:], in_=esel[:], compare_op=ALU.is_equal, fill=0.0, base=0,
                               pattern=[[-1, E8], [0, FF // E8]], channel_multiplier=1).then_inc(S["c_pool"], 1)
            pool.memset(epow[:, 0:TILES], -0.5).then_inc(S["c_pool"], 1)
            pool.memset(epow[:, TILES:2 * TILES], EPS).then_inc(S["c_pool"], 1)
            pool.memset(neg[:, 0:1], NEG_MASK).then_inc(S["c_pool"], 1)
            pool.memset(neg[:, 1:2], NEG_CACHE).then_inc(S["c_pool"], 1)
            pool.iota(order[:], pattern=[[-1, E8]], base=E8, channel_multiplier=0,
                      allow_small_or_imprecise_dtypes=True).then_inc(S["c_pool"], 1)
            pool.iota(iota_k[:], pattern=[[1, SEQ]], base=0, channel_multiplier=0,
                      allow_small_or_imprecise_dtypes=True).then_inc(S["c_pool"], 1)
            pool.iota(iota_p[:], pattern=[[0, 1]], base=0, channel_multiplier=1,
                      allow_small_or_imprecise_dtypes=True).then_inc(S["c_pool"], 1)
            for i in range(2):
                pool.memset(vca[i][:], 1.0).then_inc(S["c_pool"], 1)
            pool.memset(values_all[:], 0.0).then_inc(S["c_pool"], 1)
            pool.wait_ge(S["c_pool"], 12)
            pool.memset(values_all[0:SEQ, :, :, HD:HD + 1], 1.0).then_inc(S["c_pool"], 1)
            pool.memset(values_all[SEQ:P, :, :, 2 * HD + 1:2 * HD + 2], 1.0).then_inc(S["c_pool"], 1)
            pool.wait_ge(S["c_pool"], 14)
            for l in range(4):
                pool.dma_start(bo[:, l, :], A[f"L{l}_xattn_bo"].rearrange("(a n) -> a n", a=1)).then_inc(S["in_bo"], 16)
            pool.dma_start(cacheV[:], A["ctx_1024"].rearrange("b s d -> s b d")).then_inc(S["in_cv"], 16)
            pool.wait_ge(S["c_b_sb"], 1)
            pool.tensor_copy(bv_wide[:], bt[:, BV:BV + 3, None].broadcast_to([P, 3, P])).then_inc(S["c_bvw"], 1)
            pool.wait_ge(S["c_dve"], 1)

            def mult(o, a, b):
                return pool.tensor_tensor(o, a, b, ALU.mult)

            def power(v, s, e, n, name, val):
                pool.wait_ge(S[name + "mv"], val)
                pool.tensor_tensor(e, v, epow[:, TILES:TILES + n], ALU.add).then_inc(S[name + "ve"], 1)
                pool.wait_ge(S[name + "ve"], val)
                pool.tensor_tensor(s, e, epow[:, 0:n], ALU.pow).then_inc(S[name + "rstd"], 1)

            def attention(a, extra, steps="all"):
                def body(f, s, c, p, nn, par):
                    if f is not None:
                        wait(pool, "a_s", W(a, f) - (4 if a == CACHE else 2))
                        if isinstance(f, int) and f == 0:
                            if a < CACHE:
                                pool.wait_ge(S["k_sb"], 2 * (a + 1))
                            if a < SELF:
                                pool.wait_ge(S["ob_sb"], a + 1)
                        kv, full = kview(a, par), [P, 2, HEADS // 2, SEQ]
                        hm = m8[:, None, :, None].broadcast_to(full)
                        if a <= CACHE:
                            old = keys_all[:, :, bass.ds(f * SEQ, SEQ)]
                            last = mult(kv[:, :, :, 0:SEQ], old[:, :, None, :].broadcast_to(full), hm)
                        if a < CACHE:
                            last.then_inc(S["a_kbd"], 1)
                        if a == 1:
                            if isinstance(f, int) and f == 0:
                                pool.wait_ge(S["c_hide"], 1)
                            wait(pool, "a_masked", f - 1)
                            pool.nop(nofuse=True)
                            pool.tensor_copy(kill[par][:], mask[:, bass.ds(f, 1), :].rearrange("p o k -> p (o k)")
                                             ).then_inc(S["a_kill"], 1)
                        if a != SELF:
                            pool.wait_ge(S["a_xn"], V(a, f))
                            tile = x[:, bass.ds(f, 1), :]
                            pool.tensor_tensor(tile, tile, out_bias[:, a:a + 1, :], ALU.add).then_inc(S["a_bo"], 1)
                    if nn is not None:
                        o = 1 - par
                        power(mv[o][:, 1:2], rstd[o][:], ve[o][:], 1, "a_", V(a, nn))
                    if f is not None and a >= CACHE:
                        pool.wait_ge(S["a_qk_sb"], V(a, f))
                        k0 = SEQ if a == CACHE else 0
                        mult(kv[:, :, :, k0:k0 + SEQ], kT[par][:, :, None, :].broadcast_to(full), hm).then_inc(S["a_kbd"], 1)
                    if c is not None and a < CACHE:
                        wait(pool, "a_o", V(a, c) - 2)
                        pool.nop(nofuse=True)
                        pool.tensor_copy(vbd[par][:], values_all[:, bass.ds(c * 2, 2), :, :]).then_inc(S["a_vb"], 1)
                    if c is not None and a == CACHE:
                        wait(pool, "a_o", V(a, c) - 2)
                        pool.nop(nofuse=True)
                        pool.tensor_copy(vca[par][0:SEQ, :, :, 0:HD],
                                         cacheV[:, bass.ds(c * 2, 2), :].rearrange("k b (h d) -> k b h d", d=HD)
                                         ).then_inc(S["a_vpast"], 1)
                attention_tiles(a, pool, body, extra, steps)

            def norm(k, h):
                tiles = slice(HALF * h, HALF * h + HALF)
                power(mv8[:, tiles, 1], rstd8[:, tiles], ve8[:, tiles], HALF, "n_", k + 1)

            def split_weights(e, n, loads):
                pool.wait_ge(S[f"in_w1_{e}"], loads)
                pool.nop(nofuse=True)
                pool.tensor_copy(w1r[e][0][:], w1s[e][:]).then_inc(S["e_whi"], 1)
                pool.wait_ge(S["e_whi"], n + 1)
                pool.tensor_tensor(w1r[e][1][:], w1s[e][:], w1r[e][0][:], ALU.subtract).then_inc(S["e_w"], 1)

            def at(steps, m=None):
                def extra(t):
                    if t in steps:
                        norm(*steps[t])
                    if m is not None and t in (7, 8):
                        split_weights(t - 7, LAYERS0 * E0 + E8 * m + t - 7, 16 * (LAYERS0 + E8 // 2 * m + 1))
                return extra

            attention(0, at({6: (NORM_A, 0), 8: (NORM_U0, 0)}))
            pool.wait_ge(S["in_wt"], 16 * WEIGHT_LOADS)
            for n in range(3):
                mult(nat[:, 4 + n, :].rearrange("p (h d) -> p h d", d=HD), rows8[:, n:n + 1, :].broadcast_to([P, HEADS, HD]),
                     m16[:, :, None].broadcast_to([P, HEADS, HD])).then_inc(S["c_bd"], 1)

            def unit(l, h, last=False):
                v = 2 * l + h
                if h == 0:
                    if not isinstance(l, int) or l > 0:
                        pool.wait_ge(S["e_xe"], 2 * E0 * l)
                        pool.nop(nofuse=True)
                    gb = bt[:, LNG_L0:LNB_L0 + 16].rearrange("p (w l e) -> p w l e", w=2, e=E0)
                    pool.tensor_copy(lay_gb[:], gb[:, :, bass.ds(l, 1), :].rearrange("p w o e -> p w (o e)")
                                     ).then_inc(S["lay_pool"], 1)
                    pool.wait_ge(S["lay_pool"], l + 1)
                pool.wait_ge(S["n_T_sb"], 2 * v + 2)
                for e in range(E0):
                    if e == 3 and not last:
                        norm(v + 3, 1 - h)
                    step = E0 * v + e
                    slot, parts = xe[e % 2], xr[e % 2]
                    wait(pool, "e_h", CH * (step - 1))
                    pool.nop(nofuse=True)
                    for dst in (slot, parts[0]):
                        pool.tensor_scalar(dst[:], xhT[:, 512 * h:512 * h + 512], lay_gb[:, 0, e:e + 1], lay_gb[:, 1, e:e + 1],
                                           ALU.mult, ALU.add).then_inc(S["e_xf"], 1)
                    pool.wait_ge(S["e_xf"], 2 * step + 2)
                    pool.tensor_tensor(parts[1][:], slot[:], parts[0][:], ALU.subtract).then_inc(S["e_xe"], 1)
            norm(NORM_B, 1)

            def cache():
                pool.wait_ge(S["c_past"], 4)
                pool.wait_ge(S["k_sb"], 8)
                for s in range(2):
                    mult(keys_all[:, s], keys_all[:, s], past_k[:].rearrange("p t k -> p (t k)")).then_inc(S["c_cache"], 1)
                pool.wait_ge(S["in_cv"], 16)
                mult(cacheV[:], cacheV[:], past_v[0:SEQ, :, None].broadcast_to([SEQ, BATCH, P])).then_inc(S["c_cache"], 1)
                pool.wait_ge(S["c_cache"], 3)

            def layer_weights(m, base):
                n = LAYERS0 * E0 + E8 * m
                if m == 1:
                    cache()
                with pool.Fori(1, E8 // 2) as pair:
                    for i in range(2):
                        pool.wait_ge(S["e_h"], CH * (base + 4 * pair + 2 * i - 2))
                        split_weights(i, n + 2 * pair + i, 16 * (LAYERS0 + E8 // 2 * m + 1) + 16 * pair)
            pool.wait_ge(S["c_b_sb"], 2)
            for h in range(2):
                unit(0, h)
            with pool.Fori(1, LAYERS0 - 1) as l:
                for h in range(2):
                    unit(l, h)
            for h in range(2):
                unit(LAYERS0 - 1, h, last=(h == 1))
            attention(1, at({6: (NORM_L1, 0)}, 0))
            norm(NORM_L1 + 1, 1)
            layer_weights(0, STEP_L1)
            attention(2, at({6: (NORM_L2, 0)}, 1))
            norm(NORM_L2 + 1, 1)
            layer_weights(1, STEP_L2)
            def cache_drain(t):
                at({6: (NORM_MID, 0)})(t)
                if t == 7:
                    attention(SELF, None, "head")
            attention(CACHE, cache_drain)
            attention(SELF, at({-1: (NORM_MID + 1, 1), 6: (NORM_L3, 0)}), "rest")
            norm(NORM_L3 + 1, 1)
            pool.tensor_copy(sel_r, esel[:].rearrange("e g f -> e (g f)")).then_inc(S["l3_sel"], 1)
            pool.wait_ge(S["a_res"], TILES * 5)
            pool.tensor_tensor(x[:], x[:], cur[:], ALU.add).then_inc(S["l3_res"], 1)

        @block.scalar
        def _(act):
            def copy(o, i):
                return act.activation(o, i, ACT.Copy)

            def ld(dst, src, s):
                act.dma_start(dst, src).then_inc(S[s], 16)

            act.wait_ge(S["c_rows"], 1)
            for n, v in enumerate(("bq", "bk")):
                for a, w in enumerate((A[f"L0_xattn_{v}"], A[f"L1_xattn_{v}"], A[f"L2_xattn_{v}"].rearrange("h e -> (h e)"))):
                    row0 = BQ - 128 + 6 * n + 2 * a
                    ld(bt_rows[row0:row0 + 2, 1, :].rearrange("p (half d) -> p half d", half=2),
                       w.rearrange("(s d) -> s d", s=2)[:, None, :].broadcast_to([2, 2, SEQ]), "in_tab")
            for a, w in enumerate((A["L0_xattn_bv"], A["L1_xattn_bv"], A["L2_xattn_bv"].rearrange("h e -> (h e)"))):
                ld(bt_rows[BV - 128 + a:BV - 127 + a, 1, :], w.rearrange("(a n) -> a n", a=1), "in_tab")

            def weights(g):
                act.wait_ge(S["c_wT"], g + 1)
                slot = [0, 8, 12][g]
                copy(wat[:, slot:slot + 4, :], ps[:, min(g, 1), :].rearrange("p (m n) -> p m n", n=P)
                     ).then_inc(S["c_w_sb"], 1)

            def context_keys(a):
                if a == 0:
                    act.wait_ge(S["c_bT"], 1)
                    copy(bt[:, P:2 * P], bankB[:, 0:P]).then_inc(S["c_b_sb"], 1)
                    act.wait_ge(S["c_b_sb"], 1)
                act.wait_ge(S["k_ps"], a + 1)
                for s in range(2):
                    if a == CACHE:
                        copy(keys_all[:, s], ps[:, s, :]).then_inc(S["k_sb"], 1)
                    else:
                        act.activation(keys_all[:, s], ps[:, s, :], ACT.Identity,
                                       bias=bt[:, BK + 2 * a + s:BK + 2 * a + s + 1]).then_inc(S["k_sb"], 1)

            def context_values(a, groups):
                for g in groups if a < CACHE else ():
                    act.wait_ge(S["v_ps"], 4 * a + g + 1)
                    for half in range(2):
                        r = slice(64 * half, 64 * half + 64)
                        v = ps[r, 2 + g, :].rearrange("p (b c g d) -> p b c g d", b=4, g=2, d=HD)[:, :, :, half, :]
                        last = copy(values_all[r, 4 * g:4 * g + 4, :, (HD + 1) * half:(HD + 1) * half + HD], v)
                    last.then_inc(S["v_sb"], 1)

            def context_bias(a):
                act.wait_ge(S["ob_ps"], a + 1)
                copy(out_bias[:, a, :], ps[:, 0, 0:P]).then_inc(S["ob_sb"], 1)
                if a == 0:
                    copy(bt[:, 0:P], ps[:, 0, P:2 * P]).then_inc(S["c_b_sb"], 1)

            act.wait_ge(S["c_pool"], 14)
            context_keys(0)
            context_values(0, range(4))
            context_bias(0)

            def attention(a, extra=None, steps="all"):
                def body(f, s, c, p, nn, par):
                    if f is not None:
                        wait(act, "a_s", W(a, f) - (4 if a == CACHE else 2))
                        act.wait_ge(S["a_xT"], V(a, f))
                        turned = bankA[:, 0:P].rearrange("p (b k) -> p b k", b=2)
                        if a == SELF:
                            copy(xnT[par][:], turned[:, :, None, :].broadcast_to([P, 2, 2, SEQ])).then_inc(S["a_xT_sb"], 1)
                        else:
                            copy(xnT[par][:, :, 0, :], turned).then_inc(S["a_xT_sb"], 1)
                    if c is not None:
                        for half, banks in halves(a):
                            act.wait_ge(S["a_sub"], W(a, c, half))
                            pv = pview(a, par)[:, banks]
                            act.activation(pv, pv, ACT.Exp, scale=SCALE).then_inc(S["a_exp"], 1)
                    if f is not None:
                        if a >= CACHE:
                            wait(act, "a_kbd", V(a, f) - 2)
                        act.wait_ge(S["a_qk"], V(a, f))
                        q = bankA[:, 0:P].rearrange("p (s k) -> p s k", s=2)
                        for b in range(2):
                            r = slice(64 * b, 64 * b + 64)
                            if a < CACHE:
                                for s in range(2):
                                    last = act.activation(qT[par][r, s, r], q[r, s, :], ACT.Identity,
                                                          bias=bt[r, BQ + 2 * a + s:BQ + 2 * a + s + 1])
                            else:
                                copy(qT[par][r, :, r], q[r, :, :])
                        if a >= CACHE:
                            last = copy(kT[par][:], bankA[:, P:2 * P].rearrange("p (s k) -> p s k", s=2))
                        last.then_inc(S["a_qk_sb"], 1)

                    def own_values():
                        if s is None or a < CACHE:
                            return
                        act.wait_ge(S["a_vm"], TILES * (a - CACHE) + s + 1)
                        wait(act, "a_o", V(a, s) - 2)
                        o = 1 - par
                        if a == CACHE:
                            last = copy(vca[o][SEQ:P, :, :, 0:HD],
                                        tile_values[SEQ:P, :].rearrange("p (b h d) -> p b h d", b=2, d=HD))
                        else:
                            for half in range(2):
                                r = slice(64 * half, 64 * half + 64)
                                last = copy(vbd[o][r, :, :, (HD + 1) * half:(HD + 1) * half + HD],
                                            tile_values[r, :].rearrange("p (b c g d) -> p b c g d", b=2, g=2, d=HD)
                                            [:, :, :, half, :])
                        last.then_inc(S["a_v"], 1)

                    def turned_probs(q):
                        act.wait_ge(S["a_pT"], GROUP_BASE[a] + GROUPS[a] * c + q + 1)
                        copy(probT[:, 4 * q:4 * q + 4, :], ps[:, 4 + q % 2, :].rearrange("p (c n) -> p c n", n=P)
                             ).then_inc(S["a_pT_sb"], 1)

                    def turned_out():
                        if p is not None:
                            act.wait_ge(S["a_oT"], V(a, p))
                            copy(oT[:], bankB[:, 256:384]).then_inc(S["a_oT_sb"], 1)
                    before = GROUPS[a] // 2
                    if c is not None:
                        wait(act, "a_o", V(a, c) - 1)
                        turned_probs(0)
                    own_values()
                    if c is not None and before == 2:
                        turned_probs(1)
                    turned_out()
                    if c is not None:
                        for q in range(before, GROUPS[a]):
                            turned_probs(q)
                attention_tiles(a, act, body, extra, steps)

            def transposed(count, bank, dst):
                act.wait_ge(S["n_T"], count)
                copy(dst, ps[:, bank, :]).then_inc(S["n_T_sb"], 1)

            def tokens_T(m, g):
                transposed(2 * m + g + 1, 6 + g, xhT[:, 512 * g:512 * g + 512])
                if m < GATE_L3:
                    copy(xr[g][0][:], ps[:, 6 + g, :]).then_inc(S["x_hi"], 1)

            def next_context(a, m):
                def extra(t):
                    if t == 6:
                        context_keys(a + 1)
                    if t == 8:
                        if m is not None:
                            tokens_T(m, 0)
                        context_values(a + 1, range(2))
                return extra

            def gates(m, e, tiles=slice(0, TILES)):
                act.wait_ge(S["g_sub"], m + 1)
                act.activation(g_exp[:, tiles, 0:e], g_exp[:, tiles, 0:e], ACT.Exp).then_inc(S["g_ex"], 1)

            def turned_gates(count, bank, e, half):
                act.wait_ge(S["g_cT"], count)
                copy(combT[0:e, 512 * half:512 * half + 512], ps[0:e, bank, :]).then_inc(S["g_cT_sb"], 1)

            def gates_T(m, e):
                for g in range(2):
                    turned_gates(2 * m - UNITS + g + 1, 6 + g, e, g)

            def hidden(step, parity, col, func, first=False, chunks=range(CH)):
                if not first:
                    wait(act, "e_y", step - 1)
                for c in chunks:
                    act.wait_ge(S["e_h"], 4 * step + c + 1)
                    act.activation(hs[parity][:, c, :], hid[c], func, bias=lay_b1[:, col + c:col + c + 1]).then_inc(S["e_h_sb"], 1)

            def biases(col, n, count, used=None):
                if used is not None:
                    act.wait_ge(S["e_h_sb"], used)
                    act.nop(nofuse=True)
                act.activation(lay_b1[:, 0:n], bt[:, bass.ds(col, n)], ACT.Copy).then_inc(S["lay_act"], 1)
                act.wait_ge(S["lay_act"], count)

            attention(0, next_context(0, None))

            def lead(u, h, part):
                cols = slice(512 * h, 512 * h + 512)
                if part == 0:
                    transposed(2 * u + 1, 6, curT[:, cols])
                    transposed(2 * u + 2, 7, xhT[:, cols])
                elif part == 1:
                    gates(u, E0, slice(HALF * h, HALF * h + HALF))
                else:
                    turned_gates(u + 1, 7, E0, h)

            def unit(l, h, last=False):
                v = 2 * l + h
                if h == 0:
                    biases(B1_L0 + 16 * l, 16, l + 1, None if isinstance(l, int) and l == 0 else CH * E0 * v)
                for e in range(E0):
                    hidden(E0 * v + e, e % 2, e * CH, ACT.Gelu)
                    if isinstance(v, int) and v == 0 and e == 0:
                        lead(0, 0, 2)
                    if split_ahead(l, h, e, last):
                        weights_hi(*split_ahead(l, h, e, last))
                    if e > 0 and not last:
                        lead(v + 1, 1 - h, e - 1)
            def weights_hi(l, e):
                act.wait_ge(S[f"in_w1_{e}"], 16 * (l + 1))
                act.nop(nofuse=True)
                copy(w1r[e][0][:], w1s[e][:]).then_inc(S["e_whi"], 1)

            lead(0, 0, 0)
            context_bias(1)
            weights(1)
            weights_hi(0, 0)
            lead(0, 0, 1)
            weights_hi(0, 1)
            context_values(1, range(2, 4))
            for h in range(2):
                unit(0, h)
            with act.Fori(1, LAYERS0 - 1) as l:
                for h in range(2):
                    unit(l, h)
            for h in range(2):
                unit(LAYERS0 - 1, h, last=(h == 1))
            for a, m, base, table in ((1, GATE_L1, STEP_L1, B1_L1), (2, GATE_L2, STEP_L2, B1_L2)):
                attention(a, next_context(a, m))
                context_values(a + 1, range(2, 4))
                context_bias(a + 1)
                if a == 1:
                    weights(2)
                laid = LAYERS0 + E8 * (m - GATE_L1) + 1
                biases(table, CH, laid, CH * base)
                hidden(base, 0, 0, ACT.Relu, chunks=range(CH - 1))
                tokens_T(m, 1)
                hidden(base, 0, 0, ACT.Relu, chunks=range(CH - 1, CH))
                gates(m, E8)
                hidden(base + 1, 1, 0, ACT.Relu)
                gates_T(m, E8)
                with act.Fori(1, E8) as e:
                    biases(table + CH * e, CH, laid + e, CH * (base + 2 * e))
                    for h in range(2):
                        hidden(base + 2 * e + h, h, 0, ACT.Relu)
            def relu(s, chunks=range(CH)):
                for c in chunks:
                    act.wait_ge(S["l3_h"], 4 * s + c + 1)
                    act.activation(hs[s][:, c, :], hid[c], ACT.Relu).then_inc(S["l3_h_sb"], 1)
            attention(CACHE, lambda t: attention(SELF, None, "head") if t == 7 else None)
            attention(SELF, lambda t: tokens_T(GATE_L3, 0) if t == 8 else None, "rest")
            relu(0, range(3))
            tokens_T(GATE_L3, 1)
            relu(0, range(3, CH))
            gates(GATE_L3, E8)
            relu(1)
            for g in range(2):
                turned_gates(2 * GATE_L3 - UNITS + g + 1, 6 + g, E8, g)
                copy(gate_r[g][0], ps[0:E8, 6 + g, :]).then_inc(S["l3_ghi"], 1)

        @block.tensor
        def _(pe):
            pe.wait_ge(S["c_id"], 3)
            pe.wait_ge(S["in_ctx"], 16)
            for t in range(TILES):
                last = pe.transpose(ps[:, 5 + t // 4, (t % 4) * P:(t % 4 + 1) * P], ctx_tok[:, t, :], ident[:])
                if t % 4 == 3:
                    last.then_inc(S["c_cT"], 1)
            pe.wait_ge(S["in_w0"], 16 * 4)

            def weights(g):
                if g == 1:
                    pe.wait_ge(S["c_bd"], 3)
                for m in range(4):
                    last = pe.transpose(ps[:, min(g, 1), m * P:(m + 1) * P], nat[:, 4 * g + m, :], ident[:])
                last.then_inc(S["c_wT"], 1)

            def context_keys(a):
                wk = ident if a == CACHE else wat[:, 4 * a + 1, :]
                seqs = ctxT[:].rearrange("p (t b k) -> p b t k", b=2, k=SEQ)
                for s in range(2):
                    for b in range(2):
                        last = pe.matmul(ps[64 * b:64 * b + 64, s, :].rearrange("p (t k) -> p t k", k=SEQ),
                                         lhsT=wk[:, 64 * s:64 * s + 64], rhs=seqs[:, b], start=True, stop=True)
                last.then_inc(S["k_ps"], 1)
                if a == 0:
                    pe.wait_ge(S["in_tab"], 16 * 10)
                    pe.transpose(bankB[:, 0:P], bt_rows[:, 1, :], ident[:]).then_inc(S["c_bT"], 1)

            def context_values(a, groups):
                for g in groups if a < CACHE else ():
                    for b in range(4 * g, 4 * g + 4):
                        for half in range(2):
                            last = pe.matmul(ps[64 * half:64 * half + 64, 2 + g, (b % 4) * P:(b % 4 + 1) * P],
                                             lhsT=ctxT[:, SEQ * b:SEQ * b + SEQ], rhs=wat[:, 4 * a + 2, :], start=True, stop=True)
                    last.then_inc(S["v_ps"], 1)

            def context_bias(a):
                pe.wait_ge(S["k_sb"], 2 * a + 2)
                if a == 0:
                    pe.wait_ge(S["in_bias"], 16 * SMALL_LOADS)
                    pe.transpose(ps[:, 0, P:2 * P], bt_rows[:, 0, :], ident[:])
                    pe.wait_ge(S["c_bvw"], 1)
                    pe.wait_ge(S["in_bo"], 16 * 4)
                if a < CACHE:
                    pe.matmul(ps[:, 0, 0:P], lhsT=bv_wide[:, a, :], rhs=wat[:, 4 * a + 3, :], start=True, stop=False)
                pe.matmul(ps[:, 0, 0:P], lhsT=ones[0:1, :], rhs=bo[:, a, :], start=(a == CACHE), stop=True
                          ).then_inc(S["ob_ps"], 1)

            def context_read(a, groups):
                pe.wait_ge(S["k_sb"], 2 * a + 2)
                if a < CACHE:
                    pe.wait_ge(S["v_sb"], 4 * a + groups)
                pe.wait_ge(S["ob_sb"], a + 1)

            weights(0)
            pe.wait_ge(S["c_w_sb"], 1)
            pe.wait_ge(S["c_c_sb"], 2)
            context_keys(0)
            context_values(0, range(4))
            context_bias(0)
            context_read(0, 4)

            def attention(a, extra, steps="all", drained=None):
                wq, wk, wv, wo = (wat[:, 4 * a + n, :] for n in range(4))

                def front_x(f, par):
                    pe.wait_ge(S["a_xn"], V(a, f))
                    wait(pe, "a_qk_sb", V(a, f) - 1)
                    if a >= CACHE:
                        first = a == SELF and isinstance(f, int) and f == 0
                        wait(pe, "a_v", TILES * (a - CACHE) + (0 if first else f - 1))
                    pe.transpose(bankA[:, 0:P], xn[par][:], ident[:]).then_inc(S["a_xT"], 1)

                def front_qk(f, par):
                    for n, w in enumerate((wq, wk) if a >= CACHE else (wq,)):
                        for s in range(2):
                            for b in range(2):
                                last = pe.matmul(bankA[64 * b:64 * b + 64, n * P + 64 * s:n * P + 64 * s + 64],
                                                 lhsT=w[:, 64 * s:64 * s + 64], rhs=xnT[par][:, b, 0, :], start=True, stop=True)
                    last.then_inc(S["a_qk"], 1)

                def new_values(s, o):
                    for b in range(2):
                        dst = tile_values[:, b * P:(b + 1) * P]
                        if a == CACHE:
                            last = pe.matmul(dst[SEQ:P, :], lhsT=xnT[o][:, b, 0, :], rhs=wv, start=True, stop=True)
                        else:
                            last = pe.matmul(dst, lhsT=xnT[o][:, b, :, :].rearrange("p d k -> p (d k)"), rhs=wv,
                                             start=True, stop=True)
                    last.then_inc(S["a_vm"], 1)

                def score(s, o, between=None):
                    pe.wait_ge(S["a_kbd"], V(a, s))
                    pe.wait_ge(S["a_qk_sb"], V(a, s))
                    if a != CACHE:
                        wait(pe, "a_sub", W(a, s) - 2)
                    kv, (n, j, k) = kview(a, o), shape(a)
                    for i in range(n):
                        half, h0 = i * j // 8, i * j % 8
                        if a == CACHE and h0 == 0:
                            pe.wait_ge(S["a_sub"], W(a, s, half) - 2)
                        last = pe.matmul(sview(a, o)[:, i, :, :], lhsT=qT[o][:, half, :], rhs=kv[:, half, h0:h0 + j, :],
                                         start=True, stop=True)
                        if a == CACHE and i == 1:
                            last.then_inc(S["a_s"], 1)
                        if i == 0 and between is not None:
                            out_y(between)
                    last.then_inc(S["a_s"], 1)

                def turn(c, par, groups):
                    for q in groups:
                        done = GROUP_BASE[a] + GROUPS[a] * c + q
                        if q % 2 == 0:
                            pe.wait_ge(S["a_exp"], W(a, c, q // 2 if a == CACHE else 1))
                        wait(pe, "a_pT_sb", done - 1)
                        for k in range(4):
                            ch = 4 * q + k
                            last = pe.transpose(ps[:, 4 + q % 2, k * P:(k + 1) * P], prob[par][:, ch * P:(ch + 1) * P], ident[:])
                        last.then_inc(S["a_pT"], 1)

                def values(p, o, part=slice(None)):
                    pe.wait_ge(S["a_pT_sb"], GROUP_BASE[a] + GROUPS[a] * (p + 1))
                    if a >= CACHE:
                        pe.wait_ge(S["a_v"], TILES * (a - CACHE) + p + 1)
                    else:
                        pe.wait_ge(S["a_vb"], V(a, p))
                    if a == CACHE:
                        pe.wait_ge(S["a_vpast"], p + 1)
                    wait(pe, "a_res", V(a, p) - 1)
                    chunks = 4 * GROUPS[a]
                    w = HEADS * (HD + 1) // chunks
                    v = vca[o] if a == CACHE else vbd[o]
                    for c in range(chunks)[part]:
                        for b in range(2):
                            last = pe.matmul(bankB[64 * b:64 * b + 64, w * c:w * c + w], lhsT=probT[:, c, 64 * b:64 * b + 64],
                                             rhs=v[:, b, c, :], start=True, stop=True)
                    if c == chunks - 1:
                        last.then_inc(S["a_o"], 1)

                def out_T(p):
                    pe.wait_ge(S["a_on"], V(a, p))
                    pe.transpose(bankB[:, 256:384], on[:].rearrange("p h d -> p (h d)"), ident[:]).then_inc(S["a_oT"], 1)

                def out_y(p):
                    pe.wait_ge(S["a_oT_sb"], V(a, p))
                    pe.matmul(bankB[:, 384:512], lhsT=oT[:], rhs=wo, start=True, stop=True).then_inc(S["a_y"], 1)

                def body(f, s, c, p, nn, par):
                    filling = c is None and f is not None
                    if s is not None and a >= SCORES_FIRST and not filling:
                        score(s, 1 - par)
                    if f is not None:
                        front_x(f, par)
                    halfway = HEADS // 4 if a == SELF else None
                    if p is not None:
                        values(p, 1 - par, slice(0, halfway))
                    if f is not None:
                        pe.wait_ge(S["a_xT_sb"], V(a, f))
                    if s is not None and a >= CACHE:
                        new_values(s, 1 - par)
                    if f is not None:
                        front_qk(f, par)
                    if p is not None and a == SELF:
                        values(p, 1 - par, slice(halfway, None))
                    if drained is not None and c is None and p is not None:
                        drained()
                    if s is not None and a >= SCORES_FIRST and filling:
                        score(s, 1 - par)
                    if c is not None:
                        turn(c, par, range(GROUPS[a] // 2))
                        if a == CACHE and p is not None:
                            out_T(p)
                            turn(c, par, (2,))
                            out_y(p)
                            turn(c, par, (3,))
                    if p is not None and (a != CACHE or c is None):
                        out_T(p)
                    if c is not None and (a != CACHE or p is None):
                        turn(c, par, range(GROUPS[a] // 2, GROUPS[a]))
                    if f is not None and a < SCORES_FIRST:
                        score(f, par, p)
                    elif p is not None and (a != CACHE or c is None):
                        out_y(p)
                if steps != "rest" and 0 < a < SELF:
                    step = (0, STEP_L1, STEP_L2, STEP_L2 + 2 * E8)[a]
                    pe.wait_ge(S["e_h_sb"], CH * step)
                    pe.wait_ge(S["g_init"], UNITS + a - 1)

                def more(t):
                    if t == -1 and 0 < a < SELF:
                        pe.wait_ge(S["e_acc"], (0, STEP_L1, STEP_L2, STEP_L2 + 2 * E8)[a])
                    if extra is not None:
                        extra(t)
                attention_tiles(a, pe, body, more, steps)
                if steps != "head":
                    pe.wait_ge(S["a_res"], TILES * (a + 1))

            def turn_half(src, half, bank):
                for k in range(HALF):
                    last = pe.transpose(ps[:, bank, k * P:(k + 1) * P], src[:, HALF * half + k, :], ident[:])
                last.then_inc(S["n_T"], 1)

            def turn_tokens(k, g):
                pe.wait_ge(S["n_done"], k + 1)
                turn_half(xh, g, 6 + g)

            def next_context(a):
                def extra(t):
                    if t == 6:
                        if a == 0:
                            pe.wait_ge(S["in_wt"], 16 * WEIGHT_LOADS)
                        pe.wait_ge(S["a_sub"], W(a, 6))
                        context_keys(a + 1)
                    if t == 8:
                        pe.wait_ge(S["a_sub"], W(a, 7))
                        context_values(a + 1, range(2))
                return extra

            def router(srcT, cols, e, tiles=range(TILES)):
                for k, t in enumerate(tiles):
                    last = pe.matmul(ps[:, 6, k * e:(k + 1) * e], lhsT=srcT[:, t * P:(t + 1) * P], rhs=rw[:, cols],
                                     start=True, stop=True)
                last.then_inc(S["g_logits"], 1)

            def rank():
                pe.wait_ge(S["g_rank"], 1)
                pe.matmul(bankA[:, 64:128], lhsT=tri[:], rhs=g_sel[:].rearrange("p t e -> p (t e)"), start=True, stop=False)
                pe.matmul(bankA[:, 64:128], lhsT=ones[:], rhs=seen[:].rearrange("p t e -> p (t e)"), start=False, stop=True
                          ).then_inc(S["g_rank"], 1)

            def turn_gates(half, bank, e):
                for k in range(HALF):
                    last = pe.transpose(ps[0:e, bank, k * P:(k + 1) * P], comb[:, HALF * half + k, 0:e], ident[:])
                last.then_inc(S["g_cT"], 1)

            def gates_T(m, e):
                pe.wait_ge(S["g_comb"], m + 1)
                for g in range(2):
                    turn_gates(g, 6 + g, e)
                pe.wait_ge(S["g_cT_sb"], 2 * m - UNITS + 2)

            def gated_bias(b2, e, tiles=range(TILES)):
                for k, t in enumerate(tiles):
                    last = pe.matmul(ps[:, 6 + k // 4, (k % 4) * P:(k % 4 + 1) * P], lhsT=combT[0:e, t * P:(t + 1) * P],
                                     rhs=b2, start=True, stop=True)
                last.then_inc(S["g_b2"], 1)

            def hidden(step, slot, split, src, first=False, chunks=range(CH)):
                if split is not None:
                    pe.wait_ge(S["e_w"], split)
                w, (hi, lo) = w1r[slot], xr[src]
                for c in chunks:
                    if not first:
                        wait(pe, "e_h_sb", 4 * step + c - 3)
                    cols = slice(c * P, (c + 1) * P)
                    pe.matmul(hid[c], lhsT=w[0][:, cols], rhs=hi[:], start=True, stop=False)
                    pe.matmul(hid[c], lhsT=w[0][:, cols], rhs=lo[:], start=False, stop=False)
                    pe.matmul(hid[c], lhsT=w[1][:, cols], rhs=hi[:], start=False, stop=True).then_inc(S["e_h"], 1)

            def outputs(step, parity, slot, loads, first=False):
                pe.wait_ge(S["e_h_sb"], 4 * step + 4)
                if loads is not None:
                    pe.wait_ge(S[f"in_w2_{slot}"], loads)
                if not first:
                    wait(pe, "e_acc", step - 1)
                for k in range(4):
                    for c in range(CH):
                        last = pe.matmul(ps[:, 4 + parity, k * P:(k + 1) * P], lhsT=hs[parity][:, c, k * P:(k + 1) * P],
                                         rhs=w2s[slot][:, c, :], start=(c == 0), stop=(c == CH - 1))
                last.then_inc(S["e_y"], 1)

            attention(0, next_context(0))

            def lead(u, l, h, part):
                if part == 0:
                    pe.wait_ge(S["n_done"], NORM_U0 + 1 if isinstance(u, int) and u == 0 else u + 3)
                    wait(pe, "g_init", u)
                    turn_half(cur, h, 6)
                    turn_half(xh, h, 7)
                elif part == 1:
                    pe.wait_ge(S["n_T_sb"], 2 * u + 2)
                    router(curT, bass.ds(l * E0, E0), E0, range(HALF * h, HALF * h + HALF))
                else:
                    pe.wait_ge(S["g_comb"], u + 1)
                    turn_gates(h, 7, E0)

            def unit(l, h, last=False):
                v = 2 * l + h
                for e in range(E0):
                    pe.wait_ge(S["e_xe"], E0 * v + e + 1)
                    hidden(E0 * v + e, e, E0 * l + e + 1 if h == 0 else None, e % 2)
                    if e == 0:
                        if isinstance(v, int) and v == 0:
                            lead(0, 0, 0, 2)
                        pe.wait_ge(S["g_cT_sb"], v + 1)
                        pe.nop(nofuse=True)
                        gated_bias(b2_l0[:, bass.ds(l, 1), :].rearrange("e o h -> e (o h)"), E0, range(HALF * h, HALF * h + HALF))
                    if e == 2 and not last:
                        lead(v + 1, l + h, 1 - h, 1)
                    if not (isinstance(v, int) and v == 0 and e == 0):
                        outputs(E0 * v + e - 1, (e - 1) % 2, (e - 1) % E0, 16 * (l + 1) if h == 0 and e > 0
                                else 16 * l if h == 0 else 16 * (l + 1))
                    if e in (1, 3) and not last:
                        lead(v + 1, l + h, 1 - h, e - 1)
            lead(0, 0, 0, 0)
            context_bias(1)
            weights(1)
            lead(0, 0, 0, 1)
            context_values(1, range(2, 4))
            context_read(1, 4)
            pe.wait_ge(S["c_b_sb"], 2)
            pe.wait_ge(S["c_w_sb"], 2)
            for h in range(2):
                unit(0, h)
            with pe.Fori(1, LAYERS0 - 1) as l:
                for h in range(2):
                    unit(l, h)
            for h in range(2):
                unit(LAYERS0 - 1, h, last=(h == 1))
            attention(1, None, "head")
            outputs(STEP_L1 - 1, 1, E0 - 1, None)
            for a, m, base in ((1, GATE_L1, STEP_L1), (2, GATE_L2, STEP_L2)):
                k = NORM_L1 + 2 * (m - GATE_L1)
                attention(a, next_context(a), "rest", lambda k=k: turn_tokens(k, 0))
                context_values(a + 1, range(2, 4))
                context_bias(a + 1)
                if a == 1:
                    weights(2)
                context_read(a + 1, 4)
                pe.wait_ge(S["c_w_sb"], 3)
                loaded = 16 * (LAYERS0 + E8 // 2 * (m - GATE_L1) + 1)
                split = LAYERS0 * E0 + E8 * (m - GATE_L1) + 1

                def first(h, chunks=range(CH)):
                    pe.wait_ge(S["x_lo"], 2 * (m - GATE_L1) + h + 1)
                    pe.wait_ge(S["x_hi"], 2 * (m - GATE_L1) + h + 1)
                    hidden(base + h, 0, None if h else split, h, chunks=chunks)
                first(0, range(CH - 1))
                turn_tokens(k + 1, 1)
                first(0, range(CH - 1, CH))
                pe.wait_ge(S["n_T_sb"], 2 * m + 2)
                router(xhT, slice(16 + 8 * (m - GATE_L1), 24 + 8 * (m - GATE_L1)), E8)
                first(1)
                outputs(base, 0, 0, loaded)
                if m == GATE_L1:
                    rank()
                gates_T(m, E8)
                gated_bias(b2_l12[:, m - GATE_L1, :], E8)

                def pair(e, final, base=base, loaded=loaded, split=split):
                    for k in range(4):
                        st = base + 2 * e
                        h = k % 2
                        if not (final and k >= 2):
                            hidden(st + k + 2, (k // 2 + 1) % 2, None if h else split + e + k // 2 + 1, h)
                        if not (final and k == 3):
                            outputs(st + k + 1, 1 - h, (k + 1) // 2 % 2, loaded + 8 * (e + (k + 1) // 2 // 2 * 2) if h else None)
                with pe.Fori(0, E8 // 2 - 1) as e:
                    pair(2 * e, False)
                pair(E8 - 2, True)
                attention(a + 1, None, "head")
            attention(CACHE, None, "rest", lambda: attention(SELF, None, "head"))
            attention(SELF, lambda t: turn_tokens(NORM_L3, 0) if t == 8 else None, "rest")
            def hidden3(s, chunks=range(CH)):
                for c in chunks:
                    wait(pe, "l3_h_sb", 4 * s + c - 3)
                    pe.matmul(hid[c], lhsT=w1c[:].rearrange("p e f -> p (e f)")[:, c * P:(c + 1) * P],
                              rhs=xhT[:, 512 * s:512 * s + 512], start=True, stop=True).then_inc(S["l3_h"], 1)
            pe.wait_ge(S["in_w2nd"], 32)
            pe.wait_ge(S["n_T_sb"], 2 * GATE_L3 + 1)
            hidden3(0, range(3))
            turn_tokens(NORM_L3 + 1, 1)
            hidden3(0, range(3, CH))
            pe.wait_ge(S["n_T_sb"], 2 * GATE_L3 + 2)
            router(xhT, slice(32, 40), E8)
            hidden3(1)
            gates_T(GATE_L3, E8)
            pe.wait_ge(S["l3_sel"], 1)
            pe.wait_ge(S["l3_h_sb"], 2 * CH)
            for k in range(2 * CH):
                s, c = k // CH, k % CH
                wait(pe, "l3_gated", k - len(l3_banks) + 1)
                for part, ready in enumerate(("l3_ghi", "l3_glo")):
                    pe.wait_ge(S[ready], s + 1)
                    last = pe.matmul(ps[:, l3_banks[k % len(l3_banks)], :], lhsT=sel_r[:, c * P:(c + 1) * P],
                                     rhs=gate_r[s][part], start=(part == 0), stop=(part == 1))
                last.then_inc(S["l3_gate"], 1)
            for s in range(2):
                pe.wait_ge(S["l3_gated"], CH * (s + 1))
                for k in range(4):
                    for c in range(CH):
                        last = pe.matmul(ps[:, 6 + s, k * P:(k + 1) * P], lhsT=hs[s][:, c, k * P:(k + 1) * P],
                                         rhs=w2c[:, c, :], start=(c == 0), stop=(c == CH - 1))
                last.then_inc(S["l3_y"], 1)

        @block.vector
        def _(dve):
            def link(ins, name, value):
                ins.then_inc(S[name], 1)
                dve.wait_ge(S[name], value)

            dve.wait_ge(S["c_id"], 3)
            dve.tensor_reduce(m8[:], m16[:].rearrange("p (i j) -> p j i", j=HEADS // 2), AX, ALU.add).then_inc(S["c_dve"], 1)
            for g in range(2):
                dve.wait_ge(S["c_cT"], g + 1)
                dve.tensor_copy(ctxT[:, 512 * g:512 * g + 512], ps[:, 5 + g, :]).then_inc(S["c_c_sb"], 1)
            dve.wait_ge(S["c_wT"], 1)
            dve.tensor_copy(wat[:, 0:4, :], ps[:, 0, :].rearrange("p (m n) -> p m n", n=P)).then_inc(S["c_w_sb"], 1)
            dve.wait_ge(S["in_len"], 16)
            dve.wait_ge(S["c_pool"], 14)
            link(dve.tensor_copy(len_f[:], len_i[:]), "c_dve", 2)
            link(dve.tensor_reduce(len_max[:], len_f[:], AX, ALU.max), "c_dve", 3)
            for b in range(2):
                r = slice(64 * b, 64 * b + 64)
                dve.tensor_copy(len_half[r, :], len_f[r, :].rearrange("p (t b) -> p b t", b=2)[:, b]).then_inc(S["c_past"], 1)
            dve.wait_ge(S["c_past"], 2)
            dve.tensor_tensor(past_k[:], iota_k[:, None, :].broadcast_to([P, TILES, SEQ]),
                              len_half[:, :, None].broadcast_to([P, TILES, SEQ]), ALU.is_lt).then_inc(S["c_past"], 1)
            dve.tensor_tensor(past_v[:], iota_p[:, 0:1].broadcast_to([P, BATCH]), len_f[:], ALU.is_lt).then_inc(S["c_past"], 1)
            dve.tensor_scalar(kill_cache[:], iota_k[:], len_max[:, 0:1], None, ALU.is_ge).then_inc(S["c_past"], 1)
            dve.wait_ge(S["in_x"], 16)

            def attention(a, extra, steps="all"):
                src = cur if a == SELF else x
                def stats(t, par):
                    link(dve.bn_stats(stat[par][:], src[:, bass.ds(t, 1), :].rearrange("p o d -> p (o d)")), "a_stat", V(a, t))
                    dve.nop(nofuse=True)
                    dve.bn_aggr(mv[par][:], stat[par][:]).then_inc(S["a_mv"], 1)

                def normal(t, par):
                    dve.wait_ge(S["a_mv"], V(a, t))
                    dve.wait_ge(S["a_rstd"], V(a, t))
                    wait(dve, "a_xT", V(a, t) - 2)
                    o = dve.tensor_scalar(xn[par][:], src[:, bass.ds(t, 1), :].rearrange("p o d -> p (o d)"),
                                          mv[par][:, 0:1], rstd[par][:, 0:1], ALU.subtract, ALU.mult)
                    if a == SELF:
                        link(o, "a_aff", 2 * t + 1)
                        link(dve.tensor_tensor(xn[par][:], xn[par][:], bcast[:, 0, :], ALU.mult), "a_aff", 2 * t + 2)
                        o = dve.tensor_tensor(xn[par][:], xn[par][:], bcast[:, 1, :], ALU.add)
                    o.then_inc(S["a_xn"], 1)

                def shift_half(c, par, half, banks):
                    n, j, k = shape(a)
                    dve.wait_ge(S["a_max"], W(a, c, half))
                    dve.tensor_tensor(pview(a, par)[:, banks], sview(a, par)[:, banks],
                                      smax[:].rearrange("p (i j) -> p i j", j=j)[:, banks, :, None]
                                      .broadcast_to([P, 2, j, k]), ALU.subtract).then_inc(S["a_sub"], 1)

                def maxima(s, par, p=None):
                    if a == CACHE:
                        dve.wait_ge(S["a_pT"], GROUP_BASE[a] + (GROUPS[a] * (s - 1) if not isinstance(s, int) or s >= 1 else 0))
                    for half, banks in halves(a):
                        dve.wait_ge(S["a_s"], W(a, s, half))
                        sc, (n, j, k) = sview(a, par)[:, banks], shape(a)
                        full = [P, 2, j, SEQ]
                        if a == 1:
                            dve.wait_ge(S["a_kill"], s + 1)
                            dve.nop(nofuse=True)
                            link(dve.copy_predicated(sc, kill[par][:, None, None, :].broadcast_to(full),
                                                     neg[:, 0:1, None, None].broadcast_to(full)), "a_masked", s + 1)
                        if a == CACHE:
                            dve.nop(nofuse=True)
                            link(dve.copy_predicated(sc[:, :, :, 0:SEQ], kill_cache[:, None, None, :].broadcast_to(full),
                                                     neg[:, 1:2, None, None].broadcast_to(full)), "a_masked",
                                 TILES + 2 * s + half + 1)
                        dve.tensor_reduce(smax[:].rearrange("p (i j) -> p i j", j=j)[:, banks], sc, AX, ALU.max
                                          ).then_inc(S["a_max"], 1)
                        if a == CACHE:
                            if half == 1 and p is not None:
                                out_norm(p)
                            shift_half(s, par, half, banks)

                def shifted(c, par):
                    if a > 0 or not isinstance(c, int) or c >= 1:
                        dve.wait_ge(S["a_pT"], GROUP_BASE[a] + (GROUPS[a] * (c - 1) + 1 if not isinstance(c, int) or c >= 1 else 0))
                    for half, banks in halves(a):
                        shift_half(c, par, half, banks)

                def out_norm(p):
                    dve.wait_ge(S["a_o"], V(a, p))
                    o = bankB[:, 0:HEADS * (HD + 1)].rearrange("p (h w) -> p h w", w=HD + 1)
                    link(dve.reciprocal(rsum[:], o[:, :, HD]), "a_rs", V(a, p))
                    dve.tensor_tensor(on[:], o[:, :, 0:HD], rsum[:, :, None].broadcast_to([P, HEADS, HD]), ALU.mult
                                      ).then_inc(S["a_on"], 1)

                def residual(p):
                    dve.wait_ge(S["a_y"], V(a, p))
                    if a != SELF:
                        dve.wait_ge(S["a_bo"], V(a, p))
                    tile = src[:, bass.ds(p, 1), :].rearrange("p o d -> p (o d)")
                    dve.tensor_tensor(tile, bankB[:, 384:512], tile, ALU.add).then_inc(S["a_res"], 1)

                def body(f, s, c, p, nn, par):
                    if c is not None and a != CACHE:
                        shifted(c, par)
                    if nn is not None:
                        stats(nn, 1 - par)
                    if s is not None and a == CACHE:
                        maxima(s, 1 - par, p)
                    if p is not None and (a != CACHE or s is None):
                        out_norm(p)
                    if nn is not None:
                        normal(nn, 1 - par)
                    if a == SELF and isinstance(s, int) and s == 0:
                        norm_stats(NORM_MID + 1, x, 1)
                    if s is not None and a != CACHE:
                        maxima(s, 1 - par)
                    if p is not None:
                        residual(p)
                attention_tiles(a, dve, body, extra, steps)
                if steps != "head":
                    dve.wait_ge(S["a_res"], TILES * (a + 1))

            def norm_stats(k, src, h):
                tiles = range(HALF * h, HALF * h + HALF)
                for t in tiles:
                    last = dve.bn_stats(stat8[:, t, :], src[:, t, :])
                link(last, "n_stat", k + 1)
                dve.nop(nofuse=True)
                for t in tiles:
                    last = dve.bn_aggr(mv8[:, t, :], stat8[:, t, :])
                last.then_inc(S["n_mv"], 1)

            def norm_apply(k, src, dst, h):
                dve.wait_ge(S["n_rstd"], k + 1)
                for t in range(HALF * h, HALF * h + HALF):
                    last = dve.tensor_scalar(dst[:, t, :], src[:, t, :], mv8[:, t, 0:1], rstd8[:, t:t + 1], ALU.subtract, ALU.mult)
                return last

            def drain_norm(a, k, src, dst, more=None):
                def extra(t):
                    if t == 6:
                        dve.wait_ge(S["a_res"], V(a, HALF - 1))
                        norm_stats(k, src, 0)
                    if t == 7:
                        if k < NORM_L3:
                            norm_apply(k, src, dst, 0).then_inc(S["n_done"], 1)
                        else:
                            norm3(k, 0)
                    if more is not None:
                        more(t)
                return extra

            def norm3(k, h):
                tiles = slice(HALF * h, HALF * h + HALF)
                link(norm_apply(k, cur, xh, h), "n_aff", TILES + 2 + 2 * h)
                for v, op in ((2, ALU.mult), (3, ALU.add)):
                    last = dve.tensor_tensor(xh[:, tiles], xh[:, tiles], bcast[:, v:v + 1, :].broadcast_to([P, HALF, P]), op)
                    if v == 2:
                        link(last, "n_aff", TILES + 3 + 2 * h)
                last.then_inc(S["n_done"], 1)

            def gate(m, e, bias, ranked=False, tiles=slice(0, TILES)):
                count = tiles.stop - tiles.start
                full = [P, count, e]
                lg, two, key, sel, ex, cb = (v[:, tiles, 0:e] for v in (g_log, g_two, g_key, g_sel, g_exp, comb))
                most, tmp, total = (v[:, tiles] for v in (g_max, g_tmp, g_sum))
                n = [0]

                def chain(ins):
                    n[0] += 1
                    link(ins, "g_ln", GATE_LINKS * m + n[0])

                def wide(v):
                    return v[:, :, None].broadcast_to(full)

                def first_of(values, hot):
                    chain(dve.tensor_reduce(tmp, values, AX, ALU.max))
                    chain(dve.tensor_tensor(key, values, wide(tmp), ALU.is_equal))
                    chain(dve.tensor_tensor(key, key, order[:, None, 0:e].broadcast_to(full), ALU.mult))
                    chain(dve.tensor_reduce(total, key, AX, ALU.max))
                    chain(dve.tensor_tensor(hot, key, wide(total), ALU.is_equal))

                dve.wait_ge(S["g_logits"], m + 1)
                lp = ps[:, 6, 0:count * e].rearrange("p (t e) -> p t e", e=e)
                if bias is None:
                    chain(dve.tensor_copy(lg, lp))
                else:
                    chain(dve.tensor_tensor(lg, lp, bias.broadcast_to(full), ALU.add))
                chain(dve.tensor_reduce(most, lg, AX, ALU.max))
                dve.tensor_tensor(ex, lg, wide(most), ALU.subtract).then_inc(S["g_sub"], 1)
                first_of(lg, sel)
                chain(dve.scalar_tensor_tensor(out=two, in0=sel, scalar=-3e38, in1=lg, op0=ALU.mult, op1=ALU.add))
                first_of(two, two)
                chain(dve.tensor_tensor(sel, sel, two, ALU.add))
                dve.wait_ge(S["g_ex"], m + 1)
                chain(dve.tensor_tensor(ex, ex, sel, ALU.mult))
                chain(dve.tensor_reduce(total, ex, AX, ALU.add))
                chain(dve.reciprocal(total, total))
                if not ranked:
                    link(dve.tensor_tensor(cb, ex, wide(total), ALU.mult), "g_comb", m + 1)
                else:
                    link(dve.memset(seen[:, 0, :], 0.0), "n_aff", 1)
                    for t in range(1, TILES):
                        link(dve.tensor_tensor(seen[:, t, :], seen[:, t - 1, :], g_sel[:, t - 1, :], ALU.add), "n_aff", t + 1)
                    dve.tensor_tensor(cb, ex, wide(total), ALU.mult).then_inc(S["g_rank"], 1)
                    dve.wait_ge(S["g_rank"], 2)
                    link(dve.tensor_scalar(key, bankA[:, 64:128].rearrange("p (t e) -> p t e", e=e), float(CAPACITY), None,
                                           ALU.is_le), "n_aff", TILES + 1)
                    link(dve.tensor_tensor(cb, cb, key, ALU.mult), "g_comb", m + 1)
                assert n[0] == GATE_LINKS

            def gated_sum(step, half, e, dst, parity=None, same=False):
                dve.wait_ge(S["e_y"], step + 1)
                wait(dve, "e_acc", step if same else step - 1)
                for k in range(HALF):
                    t = HALF * half + k
                    last = dve.scalar_tensor_tensor(out=dst[:, t, :],
                                                    in0=ps[:, 4 + (half if parity is None else parity), k * P:(k + 1) * P],
                                                    scalar=comb[:, t, bass.ds(e, 1)], in1=dst[:, t, :],
                                                    op0=ALU.mult, op1=ALU.add)
                last.then_inc(S["e_acc"], 1)

            def first_unit(t):
                if t == 8:
                    dve.wait_ge(S["n_done"], NORM_A + 1)
                    norm_stats(NORM_U0, cur, 0)
            attention(0, drain_norm(0, NORM_A, x, cur, first_unit))
            norm_apply(NORM_U0, cur, xh, 0).then_inc(S["n_done"], 1)
            norm_stats(NORM_B, x, 1)
            norm_apply(NORM_B, x, cur, 1).then_inc(S["n_done"], 1)
            dve.wait_ge(S["n_done"], NORM_B + 1)
            dve.wait_ge(S["in_bias"], 16 * SMALL_LOADS)
            dve.wait_ge(S["in_mask"], 16)
            dve.tensor_scalar(mask[:], mask[:], 0, None, ALU.is_equal).then_inc(S["c_hide"], 1)

            def unit_norm(u, h):
                norm_stats(u + 2, cur, h)
                norm_apply(u + 2, cur, xh, h).then_inc(S["n_done"], 1)

            def unit_gate(u, l, h):
                tiles = slice(HALF * h, HALF * h + HALF)
                gate(u, E0, rbias[:, None, bass.ds(l * E0, E0)], tiles=tiles)
                link(dve.tensor_reduce(g_tmp[:, tiles], comb[:, tiles, 0:E0], AX, ALU.add), "g_csum", u + 1)

            def l0_residual(h):
                tiles = slice(HALF * h, HALF * h + HALF)
                link(dve.tensor_tensor(x[:, tiles], x[:, tiles], cur[:, tiles], ALU.add), "l0_x", h + 1)

            def unit(l, h, last=False):
                v = 2 * l + h
                wait(dve, "e_acc", E0 * v)
                dve.wait_ge(S["g_b2"], v + 1)
                for k in range(HALF):
                    t = HALF * h + k
                    ins = dve.scalar_tensor_tensor(out=cur[:, t, :], in0=cur[:, t, :], scalar=g_tmp[:, t:t + 1],
                                                   in1=ps[:, 6, k * P:(k + 1) * P], op0=ALU.mult, op1=ALU.add)
                link(ins, "g_init", v + 1)
                if not last:
                    unit_norm(v + 1, 1 - h)
                for e in range(E0):
                    for ahead in {0: (0, 1), 1: ()}.get(e, (e,)):
                        if split_ahead(l, h, ahead, last):
                            weights_lo(*split_ahead(l, h, ahead, last))
                    gated_sum(E0 * v + e, h, e, cur, parity=e % 2, same=True)
                    if e == 0 and not last:
                        unit_gate(v + 1, l + h, 1 - h)
                    if e == 0 and last:
                        l0_residual(0)
                        attention(1, None, "head")
            def weights_lo(l, e):
                dve.wait_ge(S["e_whi"], E0 * l + e + 1)
                dve.tensor_tensor(w1r[e][1][:], w1s[e][:], w1r[e][0][:], ALU.subtract).then_inc(S["e_w"], 1)

            weights_lo(0, 0)
            unit_gate(0, 0, 0)
            weights_lo(0, 1)
            for h in range(2):
                unit(0, h)
            with dve.Fori(1, LAYERS0 - 1) as l:
                for h in range(2):
                    unit(l, h)
            for h in range(2):
                unit(LAYERS0 - 1, h, last=(h == 1))
            dve.wait_ge(S["e_acc"], STEP_L1)
            l0_residual(1)
            for a, m, base in ((1, GATE_L1, STEP_L1), (2, GATE_L2, STEP_L2)):
                k = NORM_L1 + 2 * (m - GATE_L1)
                attention(a, drain_norm(a, k, x, xh), "rest")
                def rest(h, m=m):
                    dve.wait_ge(S["n_T_sb"], 2 * m + h + 1)
                    dve.wait_ge(S["x_hi"], 2 * (m - GATE_L1) + h + 1)
                    dve.tensor_tensor(xr[h][1][:], xhT[:, 512 * h:512 * h + 512], xr[h][0][:], ALU.subtract
                                      ).then_inc(S["x_lo"], 1)
                rest(0)
                norm_stats(k + 1, x, 1)
                norm_apply(k + 1, x, xh, 1).then_inc(S["n_done"], 1)
                rest(1)
                c0 = 16 + 8 * (m - GATE_L1)
                gate(m, E8, rbias[:, None, c0:c0 + 8], ranked=(m == GATE_L1))
                dve.wait_ge(S["g_b2"], m + 1)
                for g in range(2):
                    last = dve.tensor_tensor(x[:, 4 * g:4 * g + 4, :], ps[:, 6 + g, :].rearrange("p (t d) -> p t d", d=P),
                                             x[:, 4 * g:4 * g + 4, :], ALU.add)
                link(last, "g_init", m + 1)
                with dve.Fori(0, E8 - 1) as e:
                    for h in range(2):
                        gated_sum(base + 2 * e + h, h, e, x)
                gated_sum(base + 2 * E8 - 2, 0, E8 - 1, x)
                dve.wait_ge(S["e_acc"], base + 2 * E8 - 1)
                attention(a + 1, None, "head")
                gated_sum(base + 2 * E8 - 1, 1, E8 - 1, x)
                dve.wait_ge(S["e_acc"], base + 2 * E8)
            def self_head(t):
                if t == 7:
                    dve.wait_ge(S["n_done"], NORM_MID + 1)
                    attention(SELF, None, "head")
            attention(CACHE, drain_norm(CACHE, NORM_MID, x, cur, self_head), "rest")

            def second_half(t):
                if t == 0:
                    norm_apply(NORM_MID + 1, x, cur, 1).then_inc(S["n_done"], 1)
                    dve.wait_ge(S["n_done"], NORM_MID + 2)
            attention(SELF, drain_norm(SELF, NORM_L3, cur, xh, second_half), "rest")
            norm_stats(NORM_L3 + 1, cur, 1)
            norm3(NORM_L3 + 1, 1)
            gate(GATE_L3, E8, None)
            for g in range(2):
                dve.wait_ge(S["g_cT_sb"], 2 * GATE_L3 - UNITS + g + 1)
                dve.wait_ge(S["l3_ghi"], g + 1)
                dve.tensor_tensor(gate_r[g][1], combT[0:E8, 512 * g:512 * g + 512], gate_r[g][0], ALU.subtract
                                  ).then_inc(S["l3_glo"], 1)
            for k in range(2 * CH):
                hc = hs[k // CH][:, k % CH, :]
                dve.wait_ge(S["l3_h_sb"], k + 1)
                dve.wait_ge(S["l3_gate"], k + 1)
                dve.tensor_tensor(hc, ps[:, l3_banks[k % len(l3_banks)], :], hc, ALU.mult).then_inc(S["l3_gated"], 1)
            dve.wait_ge(S["l3_res"], 1)
            for s in range(2):
                dve.wait_ge(S["l3_y"], s + 1)
                dve.tensor_tensor(x[:, 4 * s:4 * s + 4, :], ps[:, 6 + s, :].rearrange("p (t d) -> p t d", d=P),
                                  x[:, 4 * s:4 * s + 4, :], ALU.add).then_inc(S["l3_x"], 1)


SMALL_LOADS = 18
WEIGHT_LOADS = 16
GATE_LINKS = 17


def kernel(**inputs):
    import numpy as _np
    import concourse.bacc as _bacc
    from concourse import mybir as _mybir
    from concourse.bass_utils import run_bass_kernel_spmd as _run

    nc = _bacc.Bacc("TRN2", target_bir_lowering=False, num_devices=1)
    arrays, aps = {}, {}
    for name, value in inputs.items():
        a = _np.ascontiguousarray(value)
        arrays[f"in_{name}_dram"] = a
        aps[name] = nc.dram_tensor(f"in_{name}_dram", a.shape, _mybir.dt.from_np(a.dtype), kind="ExternalInput").ap()
    shape = tuple(inputs["x"].shape)
    o = nc.dram_tensor("out_0_dram", shape, _mybir.dt.from_np(_np.dtype("float32")), kind="ExternalOutput").ap()
    build(nc, aps, o)
    r = _run(nc, [arrays], core_ids=[0])
    return r.results[0]["out_0_dram"]
```
